# Optimizing a Trainium2 kernel written in Bass

```python
import numpy as np
import jax
import jax.numpy as jnp

def _softmax(x, axis=-1):
    return jax.nn.softmax(x, axis=axis)

def _gelu(x):
    return jax.nn.gelu(x, approximate=True)

def _silu(x):
    return jax.nn.silu(x)

def _sigmoid(x):
    return jax.nn.sigmoid(x)

def _layernorm(x, axis=-1, eps=1e-05):
    m = jnp.mean(x, axis=axis, keepdims=True)
    v = jnp.var(x, axis=axis, keepdims=True)
    return (x - m) / jnp.sqrt(v + eps)

def _scatter_add(tgt, idx, src, axis=0):
    return tgt.at[idx].add(src)

def _segment_sum(src, seg, n):
    return jax.ops.segment_sum(src, seg, n)
kernel_name = 'mk_xattn_ffn_d2_seqx_r8_37a8e2'

def setup_inputs(seed: int=0):
    np.random.seed(seed)
    _w = jnp.asarray

    def _rec_inputs():
        import jax
        import jax.numpy as jnp
        _rk = jax.random.key(seed)
        x = 7.22e-05 + 1 * jax.random.normal(jax.random.fold_in(_rk, 1), (16, 56, 256), jnp.float32)
        _lenS = 56 - jax.random.randint(jax.random.fold_in(_rk, 7), (16,), 0, max(1, 56 // 4) + 1, jnp.int32)
        _lenS2 = 1500 - jax.random.randint(jax.random.fold_in(_rk, 8), (16,), 0, max(1, 1500 // 4) + 1, jnp.int32)
        _ctx_1024P = jax.random.normal(jax.random.fold_in(_rk, 11), (16, 16, 128), jnp.float32)
        _ctx_1024c = jax.random.dirichlet(jax.random.fold_in(_rk, 511), 0.3 * jnp.ones((16,), jnp.float32), (16, 1500))
        _ctx_1024t = jnp.einsum('bsk,bkd->bsd', _ctx_1024c, _ctx_1024P)
        _ctx_1024t = _ctx_1024t * jax.lax.rsqrt(jnp.mean(jnp.square(_ctx_1024t)) + 1e-12) * 0.953939
        ctx_1024 = -0.000673644 + 1.00013 * (_ctx_1024t + 0.3 * jax.random.normal(jax.random.fold_in(_rk, 611), (16, 1500, 128), jnp.float32))
        return (x, ctx_1024)
    x, ctx_1024 = _rec_inputs()

    def _L0_xattn_setup():
        import jax, jax.numpy as jnp
        import numpy as np
        B, S1, S2, DCA = (2, 256, 128, 16)
        QDIM, KDIM, H = (256, 128, 16)
        HD = QDIM // H
        SCALE = HD ** (-0.5)
        EPS = 1e-06
        DCA_WEIGHT = 1.0

        def _ln(t, w, b):
            m = jnp.mean(t, axis=-1, keepdims=True)
            v = jnp.var(t, axis=-1, keepdims=True)
            return (t - m) * jax.lax.rsqrt(v + EPS) * w + b

        def _attn(q, k, v):
            s = jnp.einsum('bhqd,bhkd->bhqk', q, k) * SCALE
            p = jax.nn.softmax(s, axis=-1)
            return jnp.einsum('bhqk,bhkd->bhqd', p, v)
        key = jax.random.key(seed)
        ks = jax.random.split(key, 8)
        w = lambda k, shape: jax.random.normal(k, shape, jnp.float32) * 0.02
        return {'x': jax.random.normal(ks[0], (B, S1, QDIM), jnp.float32), 'y': jax.random.normal(ks[1], (B, S2 + DCA, KDIM), jnp.float32), 'Wq': w(ks[2], (QDIM, QDIM)), 'bq': jnp.zeros((QDIM,), jnp.float32), 'Wk': w(ks[3], (KDIM, QDIM)), 'bk': jnp.zeros((QDIM,), jnp.float32), 'Wv': w(ks[4], (KDIM, QDIM)), 'bv': jnp.zeros((QDIM,), jnp.float32), 'Wkv_dca': w(ks[5], (KDIM, 2 * QDIM)), 'bkv_dca': jnp.zeros((2 * QDIM,), jnp.float32), 'qn_w': jnp.ones((HD,), jnp.float32), 'qn_b': jnp.zeros((HD,), jnp.float32), 'kn_w': jnp.ones((HD,), jnp.float32), 'kn_b': jnp.zeros((HD,), jnp.float32), 'kn_dca_w': jnp.ones((HD,), jnp.float32), 'kn_dca_b': jnp.zeros((HD,), jnp.float32), 'Wo': w(ks[6], (QDIM, QDIM)), 'bo': jnp.zeros((QDIM,), jnp.float32)}
    _L0_xattn_all = _L0_xattn_setup()
    _L0_xattn_in = {k: v for k, v in _L0_xattn_all.items() if k in ('Wq', 'bq', 'Wk', 'bk', 'Wv', 'bv', 'Wkv_dca', 'bkv_dca', 'qn_w', 'qn_b', 'kn_w', 'kn_b', 'kn_dca_w', 'kn_dca_b', 'Wo', 'bo')}
    del _L0_xattn_all

    def _L0_ffn_setup():
        import jax, jax.numpy as jnp
        import numpy as np
        E = 16
        K = 2
        D = 256
        I = 176
        CAP = 128
        VOCAB = 16160
        key = jax.random.key(seed)
        ks = jax.random.split(key, 11)
        B, S = (4, 128)
        sd = 1.0 / np.sqrt(D)
        si = 1.0 / np.sqrt(I)
        return {'x': jax.random.normal(ks[0], (B, S, D), jnp.float32), 'input_ids': jax.random.randint(ks[1], (B, S), 0, VOCAB, dtype=jnp.int64), 'gate_w': jax.random.normal(ks[2], (E, D), jnp.float32) * sd, 'gate_b': jax.random.normal(ks[3], (E,), jnp.float32) * 0.01, 'W1': jax.random.normal(ks[4], (E, I, D), jnp.float32) * sd, 'W3': jax.random.normal(ks[5], (E, I, D), jnp.float32) * sd, 'W2': jax.random.normal(ks[6], (E, D, I), jnp.float32) * si, 'Ws1': jax.random.normal(ks[7], (I, D), jnp.float32) * sd, 'Ws3': jax.random.normal(ks[8], (I, D), jnp.float32) * sd, 'Ws2': jax.random.normal(ks[9], (D, I), jnp.float32) * si}
    _L0_ffn_all = _L0_ffn_setup()
    _L0_ffn_in = {k: v for k, v in _L0_ffn_all.items() if k in ('input_ids', 'gate_w', 'gate_b', 'W1', 'W3', 'W2', 'Ws1', 'Ws3', 'Ws2')}
    del _L0_ffn_all

    def _L1_xattn_setup():
        import jax, jax.numpy as jnp
        import numpy as np
        EPS = 1e-05

        def rmsnorm(x, g, eps=EPS):
            var = jnp.mean(jnp.square(x), axis=-1, keepdims=True)
            return x * jax.lax.rsqrt(var + eps) * g
        key = jax.random.key(seed)
        ks = jax.random.split(key, 8)
        B, Sq, Skv = (2, 512, 64)
        dim, cdim, H, D = (256, 128, 16, 128)
        inner = H * D
        s = lambda f: 1.0 / np.sqrt(f)
        return {'hidden_states': jax.random.normal(ks[0], (B, Sq, dim), jnp.float32), 'encoder_hidden_states': jax.random.normal(ks[1], (B, Skv, cdim), jnp.float32), 'Wq': jax.random.normal(ks[2], (dim, inner), jnp.float32) * s(dim), 'Wk': jax.random.normal(ks[3], (cdim, inner), jnp.float32) * s(cdim), 'Wv': jax.random.normal(ks[4], (cdim, inner), jnp.float32) * s(cdim), 'Wo': jax.random.normal(ks[5], (inner, dim), jnp.float32) * s(inner), 'gq': jnp.ones((D,), jnp.float32), 'gk': jnp.ones((D,), jnp.float32)}
    _L1_xattn_all = _L1_xattn_setup()
    _L1_xattn_in = {k: v for k, v in _L1_xattn_all.items() if k in ('Wq', 'Wk', 'Wv', 'Wo', 'gq', 'gk')}
    del _L1_xattn_all

    def _L1_ffn_setup():
        import jax, jax.numpy as jnp
        import numpy as np
        EPS = 1e-05

        def weight_quant(w):
            scale = 1.0 / jnp.clip(jnp.mean(jnp.abs(w)), EPS, None)
            return jnp.clip(jnp.round(w * scale), -1.0, 1.0) / scale

        def act_quant(x):
            scale = 127.0 / jnp.clip(jnp.max(jnp.abs(x), axis=-1, keepdims=True), EPS, None)
            return jnp.clip(jnp.round(x * scale), -128.0, 127.0) / scale

        def bitlinear(x, w):
            return jnp.einsum('bsd,od->bso', act_quant(x), weight_quant(w))
        key = jax.random.key(seed)
        k1, k2, k3, k4 = jax.random.split(key, 4)
        B, S, D = (4, 256, 256)
        I = int(np.ceil(D * np.pi / 64) * 64)
        x = jax.random.normal(k1, (B, S, D), dtype=jnp.float32)
        w_gate = jax.random.normal(k2, (I, D), dtype=jnp.float32) * 0.02
        w_up = jax.random.normal(k3, (I, D), dtype=jnp.float32) * 0.02
        w_down = jax.random.normal(k4, (D, I), dtype=jnp.float32) * 0.02
        return {'x': x, 'w_gate': w_gate, 'w_up': w_up, 'w_down': w_down}
    _L1_ffn_all = _L1_ffn_setup()
    _L1_ffn_in = {k: v for k, v in _L1_ffn_all.items() if k in ('w_gate', 'w_up', 'w_down')}
    del _L1_ffn_all
    return {'x': x, 'ctx_1024': ctx_1024, 'L0_xattn_Wq': _L0_xattn_in['Wq'], 'L0_xattn_bq': _L0_xattn_in['bq'], 'L0_xattn_Wk': _L0_xattn_in['Wk'], 'L0_xattn_bk': _L0_xattn_in['bk'], 'L0_xattn_Wv': _L0_xattn_in['Wv'], 'L0_xattn_bv': _L0_xattn_in['bv'], 'L0_xattn_Wkv_dca': _L0_xattn_in['Wkv_dca'], 'L0_xattn_bkv_dca': _L0_xattn_in['bkv_dca'], 'L0_xattn_qn_w': _L0_xattn_in['qn_w'], 'L0_xattn_qn_b': _L0_xattn_in['qn_b'], 'L0_xattn_kn_w': _L0_xattn_in['kn_w'], 'L0_xattn_kn_b': _L0_xattn_in['kn_b'], 'L0_xattn_kn_dca_w': _L0_xattn_in['kn_dca_w'], 'L0_xattn_kn_dca_b': _L0_xattn_in['kn_dca_b'], 'L0_xattn_Wo': _L0_xattn_in['Wo'], 'L0_xattn_bo': _L0_xattn_in['bo'], 'L0_ffn_input_ids': _L0_ffn_in['input_ids'], 'L0_ffn_gate_w': _L0_ffn_in['gate_w'], 'L0_ffn_gate_b': _L0_ffn_in['gate_b'], 'L0_ffn_W1': _L0_ffn_in['W1'], 'L0_ffn_W3': _L0_ffn_in['W3'], 'L0_ffn_W2': _L0_ffn_in['W2'], 'L0_ffn_Ws1': _L0_ffn_in['Ws1'], 'L0_ffn_Ws3': _L0_ffn_in['Ws3'], 'L0_ffn_Ws2': _L0_ffn_in['Ws2'], 'L1_xattn_Wq': _L1_xattn_in['Wq'], 'L1_xattn_Wk': _L1_xattn_in['Wk'], 'L1_xattn_Wv': _L1_xattn_in['Wv'], 'L1_xattn_Wo': _L1_xattn_in['Wo'], 'L1_xattn_gq': _L1_xattn_in['gq'], 'L1_xattn_gk': _L1_xattn_in['gk'], 'L1_ffn_w_gate': _L1_ffn_in['w_gate'], 'L1_ffn_w_up': _L1_ffn_in['w_up'], 'L1_ffn_w_down': _L1_ffn_in['w_down']}

def reference(x, ctx_1024, L0_xattn_Wq, L0_xattn_bq, L0_xattn_Wk, L0_xattn_bk, L0_xattn_Wv, L0_xattn_bv, L0_xattn_Wkv_dca, L0_xattn_bkv_dca, L0_xattn_qn_w, L0_xattn_qn_b, L0_xattn_kn_w, L0_xattn_kn_b, L0_xattn_kn_dca_w, L0_xattn_kn_dca_b, L0_xattn_Wo, L0_xattn_bo, L0_ffn_input_ids, L0_ffn_gate_w, L0_ffn_gate_b, L0_ffn_W1, L0_ffn_W3, L0_ffn_W2, L0_ffn_Ws1, L0_ffn_Ws3, L0_ffn_Ws2, L1_xattn_Wq, L1_xattn_Wk, L1_xattn_Wv, L1_xattn_Wo, L1_xattn_gq, L1_xattn_gk, L1_ffn_w_gate, L1_ffn_w_up, L1_ffn_w_down):
    import jax
    import jax.numpy as jnp

    def _L0_xattn_ref(x, y, Wq, bq, Wk, bk, Wv, bv, Wkv_dca, bkv_dca, qn_w, qn_b, kn_w, kn_b, kn_dca_w, kn_dca_b, Wo, bo):
        import jax, jax.numpy as jnp
        import numpy as np
        B, S1, S2, DCA = (2, 256, 128, 16)
        QDIM, KDIM, H = (256, 128, 16)
        HD = QDIM // H
        SCALE = HD ** (-0.5)
        EPS = 1e-06
        DCA_WEIGHT = 1.0

        def _ln(t, w, b):
            m = jnp.mean(t, axis=-1, keepdims=True)
            v = jnp.var(t, axis=-1, keepdims=True)
            return (t - m) * jax.lax.rsqrt(v + EPS) * w + b

        def _attn(q, k, v):
            s = jnp.einsum('bhqd,bhkd->bhqk', q, k) * SCALE
            p = jax.nn.softmax(s, axis=-1)
            return jnp.einsum('bhqk,bhkd->bhqd', p, v)
        b, s1, _ = x.shape
        y_dca = y[:, -DCA:, :]
        y_main = y[:, :-DCA, :]
        kv_dca = (y_dca @ Wkv_dca + bkv_dca).reshape(b, DCA, 2, H, HD)
        k_dca = _ln(kv_dca[:, :, 0], kn_dca_w, kn_dca_b)
        v_dca = kv_dca[:, :, 1]
        s2 = y_main.shape[1]
        q = _ln((x @ Wq + bq).reshape(b, s1, H, HD), qn_w, qn_b)
        kv = jnp.concatenate([y_main @ Wk + bk, y_main @ Wv + bv], axis=-1)
        kv = kv.reshape(b, s2, H, 2 * HD)
        k = _ln(kv[..., :HD], kn_w, kn_b)
        v = kv[..., HD:]
        qT = q.transpose(0, 2, 1, 3)
        ctx = _attn(qT, k.transpose(0, 2, 1, 3), v.transpose(0, 2, 1, 3))
        ctx = ctx.transpose(0, 2, 1, 3).reshape(b, s1, QDIM)
        ctx_dca = _attn(qT, k_dca.transpose(0, 2, 1, 3), v_dca.transpose(0, 2, 1, 3))
        ctx_dca = ctx_dca.transpose(0, 2, 1, 3).reshape(b, s1, QDIM)
        ctx = ctx + DCA_WEIGHT * ctx_dca
        return ctx @ Wo + bo

    def _L0_ffn_ref(x, input_ids, gate_w, gate_b, W1, W3, W2, Ws1, Ws3, Ws2):
        import jax, jax.numpy as jnp
        import numpy as np
        E = 16
        K = 2
        D = 256
        I = 176
        CAP = 128
        VOCAB = 16160
        shape = x.shape
        xt = x.reshape(-1, D)
        T = xt.shape[0]
        logits = xt.astype(jnp.float32) @ gate_w.astype(jnp.float32).T
        scores = jnp.sqrt(jax.nn.softplus(logits))
        _, idx = jax.lax.top_k(scores + gate_b, K)
        w = jnp.take_along_axis(scores, idx, axis=1)
        w = w / jnp.sum(w, axis=1, keepdims=True)
        e = idx.reshape(-1)
        onehot = jax.nn.one_hot(e, E, dtype=jnp.int32)
        pos = jnp.sum(onehot * (jnp.cumsum(onehot, axis=0) - 1), axis=1)
        valid = pos < CAP
        posc = jnp.where(valid, pos, 0)
        x_pairs = jnp.repeat(xt, K, axis=0)
        x_pairs = jnp.where(valid[:, None], x_pairs, 0.0)
        buf = jnp.zeros((E, CAP, D), xt.dtype).at[e, posc].add(x_pairs)
        g = jnp.einsum('ecd,eid->eci', buf, W1).astype(jnp.float32)
        u = jnp.einsum('ecd,eid->eci', buf, W3).astype(jnp.float32)
        h = (jax.nn.silu(g) * u).astype(xt.dtype)
        out = jnp.einsum('eci,edi->ecd', h, W2)
        y_pairs = out[e, posc] * (w.reshape(-1) * valid)[:, None]
        y = y_pairs.reshape(T, K, D).sum(axis=1)
        gs = jax.nn.silu((xt @ Ws1.T).astype(jnp.float32))
        us = (xt @ Ws3.T).astype(jnp.float32)
        shared = (gs * us).astype(xt.dtype) @ Ws2.T
        return (y + shared).astype(x.dtype).reshape(shape)

    def _L1_xattn_ref(hidden_states, encoder_hidden_states, Wq, Wk, Wv, Wo, gq, gk):
        import jax, jax.numpy as jnp
        import numpy as np
        EPS = 1e-05

        def rmsnorm(x, g, eps=EPS):
            var = jnp.mean(jnp.square(x), axis=-1, keepdims=True)
            return x * jax.lax.rsqrt(var + eps) * g
        B, Sq, _ = hidden_states.shape
        Skv = encoder_hidden_states.shape[1]
        D = gq.shape[0]
        H = Wq.shape[1] // D
        scale = 1.0 / np.sqrt(D)
        q = (hidden_states @ Wq).reshape(B, Sq, H, D)
        k = (encoder_hidden_states @ Wk).reshape(B, Skv, H, D)
        v = (encoder_hidden_states @ Wv).reshape(B, Skv, H, D)
        q = rmsnorm(q, gq)
        k = rmsnorm(k, gk)
        scores = jnp.einsum('bqhd,bkhd->bhqk', q, k) * scale
        attn = jax.nn.softmax(scores, axis=-1)
        out = jnp.einsum('bhqk,bkhd->bqhd', attn, v)
        out = out.reshape(B, Sq, H * D)
        return out @ Wo

    def _L1_ffn_ref(x, w_gate, w_up, w_down):
        import jax, jax.numpy as jnp
        import numpy as np
        EPS = 1e-05

        def weight_quant(w):
            scale = 1.0 / jnp.clip(jnp.mean(jnp.abs(w)), EPS, None)
            return jnp.clip(jnp.round(w * scale), -1.0, 1.0) / scale

        def act_quant(x):
            scale = 127.0 / jnp.clip(jnp.max(jnp.abs(x), axis=-1, keepdims=True), EPS, None)
            return jnp.clip(jnp.round(x * scale), -128.0, 127.0) / scale

        def bitlinear(x, w):
            return jnp.einsum('bsd,od->bso', act_quant(x), weight_quant(w))
        gate = jax.nn.silu(bitlinear(x, w_gate))
        up = bitlinear(x, w_up)
        return bitlinear(gate * up, w_down)
    x = x + _L0_xattn_ref(_layernorm(x, axis=-1), ctx_1024, L0_xattn_Wq, L0_xattn_bq, L0_xattn_Wk, L0_xattn_bk, L0_xattn_Wv, L0_xattn_bv, L0_xattn_Wkv_dca, L0_xattn_bkv_dca, L0_xattn_qn_w, L0_xattn_qn_b, L0_xattn_kn_w, L0_xattn_kn_b, L0_xattn_kn_dca_w, L0_xattn_kn_dca_b, L0_xattn_Wo, L0_xattn_bo)
    x = x + _L0_ffn_ref(_layernorm(x, axis=-1), L0_ffn_input_ids, L0_ffn_gate_w, L0_ffn_gate_b, L0_ffn_W1, L0_ffn_W3, L0_ffn_W2, L0_ffn_Ws1, L0_ffn_Ws3, L0_ffn_Ws2)
    x = x + _L1_xattn_ref(_layernorm(x, axis=-1), ctx_1024, L1_xattn_Wq, L1_xattn_Wk, L1_xattn_Wv, L1_xattn_Wo, L1_xattn_gq, L1_xattn_gk)
    x = x + _L1_ffn_ref(_layernorm(x, axis=-1), L1_ffn_w_gate, L1_ffn_w_up, L1_ffn_w_down)
    return x

_drawn_inputs = setup_inputs


def setup_inputs(seed=0):
    import zlib

    import numpy as np

    out = dict(_drawn_inputs(seed))
    spreads = {'L0_xattn_bq': (0.0, 0.1),
     'L0_xattn_bk': (0.0, 0.1),
     'L0_xattn_bv': (0.0, 0.1),
     'L0_xattn_bkv_dca': (0.0, 0.1),
     'L0_xattn_qn_w': (1.0, 0.2),
     'L0_xattn_qn_b': (0.0, 0.269),
     'L0_xattn_kn_w': (1.0, 0.6),
     'L0_xattn_kn_b': (0.0, 0.8),
     'L0_xattn_kn_dca_w': (1.0, 0.2),
     'L0_xattn_kn_dca_b': (0.0, 0.8),
     'L0_xattn_bo': (0.0, 0.1),
     'L1_xattn_gq': (1.0, 0.564),
     'L1_xattn_gk': (1.0, 0.582)}
    factors = {'L1_ffn_w_gate': 8.0, 'L1_ffn_w_up': 7.392, 'L1_ffn_w_down': 7.417}
    for name, (base, spread) in spreads.items():
        noise = np.random.default_rng([zlib.crc32(name.encode()), seed]).standard_normal(out[name].shape)
        drawn = base * np.exp(spread * noise) if base else spread * noise
        out[name] = jnp.asarray(drawn.astype(out[name].dtype))
    for name, factor in factors.items():
        out[name] = (out[name] * factor).astype(out[name].dtype)
    return out
```

```python
from contextlib import ExitStack

import numpy as np

import concourse.bass as bass
from concourse import mybir

F32 = mybir.dt.float32
BF16 = mybir.dt.bfloat16
U32 = mybir.dt.uint32
I32 = mybir.dt.int32
ALU = mybir.AluOpType
ACT = mybir.ActivationFunctionType
X = mybir.AxisListType.X

P = 128
B, NQ, D = 16, 56, 256
C, H = 128, 16
HQ = H * NQ
HALF = HQ // 2
SEQ, DCA = 1500, 16
NK = 12
TT = 2 * NQ
NT = B // 2
T = B * NQ
HD0, HD1 = D // H, 128
E, CAP, FF = 16, 128, 176
FI = 832
FT = 7
LASTF = FI - 6 * P
KR1 = SEQ - (NK - 1) * P
KR0 = KR1 - DCA
RING = 4
MAGIC = 12582912.0


class Shared:
    pass


def phase_norms(nc, g):
    with ExitStack() as ctx:
        sb = lambda n, s, d=F32: ctx.enter_context(nc.sbuf_tensor(n, s, d))
        wall = sb("n_wall", [P, 2304])
        yT = [sb(f"n_yT{i}", [P, SEQ]) for i in range(2)]
        sq = sb("n_sq", [P, 3, 1024])
        km = sb("n_km", [P, H])
        bkm = sb("n_bkm", [1, H])
        slot = [ctx.enter_context(nc.psum_tensor(f"n_slot{i}", [P, 1024], F32)) for i in range(3)]
        W = [1024, 1024, 256]
        w_in, yT_in = g.sem("n_w_in"), [g.sem("n_yT_in0"), g.sem("n_yT_in1")]
        w_ready, cent = g.sem("n_w_ready"), g.sem("n_cent")
        prod, slot_free = g.sem("n_prod"), g.sem("n_slot_free")
        sq_free, sums = g.sem("n_sq_free"), g.sem("n_sums")
        wd, sqd = sb("n_wd", [P, D]), sb("n_sqd", [DCA, D])
        kmd, bkmd = sb("n_kmd", [P, H]), sb("n_bkmd", [1, H])
        dca_prod, dca_taken, dca_sums = g.sem("n_dca_prod"), g.sem("n_dca_taken"), g.sem("n_dca_sums")
        kd = wd[:, :].rearrange("p (h d) -> p h d", h=H)
        bkd = g.bkdrow[0:1, :].rearrange("p (h d) -> p h d", h=H)
        block = ctx.enter_context(nc.Block())
        k0 = wall[:, 2048:2304].rearrange("p (h d) -> p h d", h=H)
        bk0 = g.bk0row[0:1, :].rearrange("p (h d) -> p h d", h=H)
        TILES = B * NK

        @block.sync
        def _(sp):
            sp.dma_start(wall[:, 0:2048], g.a["L1_Wk"]).then_inc(w_in, 16)
            sp.dma_start(wall[:, 2048:2304], g.a["L0_Wk"]).then_inc(w_in, 16)
            sp.dma_start(wd[:, :], g.a["L0_Wkd"]).then_inc(w_in, 16)
            for i in range(2):
                sp.dma_start(yT[i][:, :], g.a["ctxT"][i]).then_inc(yT_in[i], 16)
            with sp.Fori(0, B // 2 - 1) as u:
                for i in range(2):
                    sp.wait_ge(dca_prod, 2 * u + i + 1)
                    sp.dma_start(yT[i][:, :], g.a["ctxT"][2 * u + 2 + i]).then_inc(yT_in[i], 16)

        @block.tensor
        def _(pe):
            pe.wait_ge(w_in, 48)
            pe.wait_ge(w_ready, 4)
            with pe.Fori(0, B // 2) as u:
                for i in range(2):
                    pe.wait_ge(yT_in[i], 16 * u + 16)
                    for j in range(NK):
                        n = P if j < NK - 1 else KR1
                        tile = (2 * u + i) * NK + j
                        lhs = yT[i][:, j * P:j * P + n]
                        for s in range(3):
                            pe.wait_ge(slot_free, tile * 3 + s + 1)
                            for c in range(0, W[s], 512):
                                w = min(512, W[s] - c)
                                mm = pe.matmul(slot[s][0:n, c:c + w], lhs,
                                               wall[:, 1024 * s + c:1024 * s + c + w],
                                               start=True, stop=(s < 2))
                            if s == 2:
                                mm = pe.matmul(slot[s][0:n, 0:256], g.ones[0:1, 0:n], g.bk0row[0:1, :],
                                               start=False, stop=True)
                            mm.then_inc(prod, 1)
                    pe.wait_ge(dca_taken, 2 * u + i)
                    pe.matmul(slot[2][0:DCA, 512:768], yT[i][:, SEQ - DCA:SEQ], wd[:, :], start=True, stop=False)
                    pe.matmul(slot[2][0:DCA, 512:768], g.ones[0:1, 0:DCA], g.bkdrow[0:1, :],
                              start=False, stop=True).then_inc(dca_prod, 1)

        @block.scalar
        def _(act):
            act.sem_inc(slot_free, 3)
            with act.Fori(0, B // 2) as u:
                for i in range(2):
                    for j in range(NK):
                        n = P if j < NK - 1 else KR1
                        tile = (2 * u + i) * NK + j
                        for s in range(3):
                            act.wait_ge(prod, tile * 3 + s + 1)
                            act.wait_ge(sq_free, tile * 3 + s + 1)
                            act.activation(sq[0:n, s, 0:W[s]], slot[s][0:n, 0:W[s]], ACT.Square)\
                               .then_inc(slot_free, 1)
                    act.wait_ge(dca_prod, 2 * u + i + 1)
                    act.wait_ge(dca_sums, 2 * u + i)
                    act.activation(sqd[:, :], slot[2][0:DCA, 512:768], ACT.Square).then_inc(dca_taken, 1)
            act.wait_ge(sums, 3)
            act.activation(g.rkd[:, :, :].rearrange("p b h -> p (b h)"),
                           g.rkd[:, :, :].rearrange("p b h -> p (b h)"), ACT.Sqrt).then_inc(sums, 1)
            act.activation(g.rk[:, :, :, :].rearrange("p b j h -> p (b j h)"),
                           g.rk[:, :, :, :].rearrange("p b j h -> p (b j h)"), ACT.Sqrt).then_inc(sums, 1)

        @block.vector
        def _(dve):
            dve.wait_ge(w_in, 48)
            heads_of = [(km, k0, P), (bkm, bk0, 1), (kmd, kd, P), (bkmd, bkd, 1)]
            for mean, w, _ in heads_of:
                dve.tensor_reduce(mean[:, :], w, X, ALU.add).then_inc(cent, 1)
            dve.memset(g.rk[:, :, :, :], 1.0).then_inc(cent, 1)
            dve.wait_ge(cent, 5)
            for mean, w, n in heads_of:
                dve.scalar_tensor_tensor(out=w, in0=mean[:, :, None].broadcast_to([n, H, HD0]),
                                         scalar=-1.0 / HD0, in1=w, op0=ALU.mult, op1=ALU.add).then_inc(w_ready, 1)
            dve.sem_inc(sq_free, 3)
            with dve.Fori(0, B // 2) as u:
                for i in range(2):
                    for j in range(NK):
                        n = P if j < NK - 1 else KR1
                        tile = (2 * u + i) * NK + j
                        for s in range(3):
                            dve.wait_ge(slot_free, tile * 3 + s + 1 + 3)
                            heads = 8 if s < 2 else H
                            dve.tensor_reduce(
                                g.rk[0:n, 2 * u + i, j, 8 * s:8 * s + heads],
                                sq[0:n, s, 0:W[s]].rearrange("p (h d) -> p h d", h=heads),
                                X, ALU.add).then_inc(sq_free, 1)
                    dve.wait_ge(dca_taken, 2 * u + i + 1)
                    dve.tensor_reduce(g.rkd[:, 2 * u + i, :], sqd[:, :].rearrange("p (h d) -> p h d", h=H),
                                      X, ALU.add).then_inc(dca_sums, 1)
            dve.wait_ge(sq_free, TILES * 3 + 3)
            dve.wait_ge(dca_sums, B)
            r1, r0 = g.rk[:, :, :, 0:H], g.rk[:, :, :, H:2 * H]
            dve.tensor_scalar(r1, r1, 1.0 / HD1, 1e-5, ALU.mult, ALU.add).then_inc(sums, 1)
            dve.tensor_scalar(r0, r0, 1.0 / HD0, 1e-6, ALU.mult, ALU.add).then_inc(sums, 1)
            dve.tensor_scalar(g.rkd[:, :, :], g.rkd[:, :, :], 1.0 / HD0, 1e-6, ALU.mult, ALU.add).then_inc(sums, 1)
            dve.wait_ge(sums, 5)
            flatd = g.rkd[:, :, :].rearrange("p b h -> p (b h)")
            dve.reciprocal(flatd, flatd).then_inc(sums, 1)
            flat = g.rk[:, :, :, :].rearrange("p b j h -> p (b j h)")
            dve.reciprocal(flat, flat).then_inc(sums, 1)


def phase_layernorm(nc, g, name):
    with ExitStack() as ctx:
        sb = lambda n, s, d=F32: ctx.enter_context(nc.sbuf_tensor(f"{name}_{n}", s, d))
        st, mv, rs = sb("st", [TT, NT, 6]), sb("mv", [TT, NT, 2]), sb("rs", [TT, NT])
        ps = [ctx.enter_context(nc.psum_tensor(f"{name}_ps{i}", [P, 512], F32)) for i in range(4)]
        stats, std, xn_ready = g.sem(f"{name}_stats"), g.sem(f"{name}_std"), g.sem(f"{name}_xn_ready")
        tr, copied = g.sem(f"{name}_tr"), g.sem(f"{name}_copied")
        block = ctx.enter_context(nc.Block())

        @block.vector
        def _(dve):
            for t in range(NT):
                dve.bn_stats(st[:, t, :], g.x[:, t, :]).then_inc(stats, 1)
            dve.wait_ge(stats, NT)
            for t in range(NT):
                dve.bn_aggr(mv[:, t, :], st[:, t, :]).then_inc(stats, 1)
            dve.wait_ge(stats, 2 * NT)
            dve.tensor_scalar(rs[:, :], mv[:, :, 1], 1e-5, None, ALU.add).then_inc(std, 1)
            dve.wait_ge(std, 2)
            dve.reciprocal(rs[:, :], rs[:, :]).then_inc(std, 1)
            dve.wait_ge(std, 3)
            for t in range(NT):
                dve.tensor_scalar(g.xn[:, t, :], g.x[:, t, :], mv[:, t, 0:1], rs[:, t:t + 1],
                                  ALU.subtract, ALU.mult).then_inc(xn_ready, 1)
            for n in range(0, 4, 2):
                dve.wait_ge(tr, n + 1)
                dve.tensor_copy(g.xnT[:, n // 2, 0:HALF], ps[n][:, 0:HALF]).then_inc(copied, 1)

        @block.scalar
        def _(act):
            act.wait_ge(std, 1)
            act.activation(rs[:, :], rs[:, :], ACT.Sqrt).then_inc(std, 1)
            for n in range(1, 4, 2):
                act.wait_ge(tr, n + 1)
                act.activation(g.xnT[:, n // 2, HALF:T], ps[n][:, 0:HALF], ACT.Copy).then_inc(copied, 1)

        @block.tensor
        def _(pe):
            for n in range(4):
                k, half = n // 2, n % 2
                pe.wait_ge(xn_ready, 4 * half + 4)
                for t in range(4):
                    mm = pe.transpose(ps[n][:, t * TT:(t + 1) * TT],
                                      g.xn[:, 4 * half + t, k * P:(k + 1) * P], g.ident[0:TT, 0:TT])
                mm.then_inc(tr, 1)


def phase_queries(nc, g, layer):
    with ExitStack() as ctx:
        sb = lambda n, s, d=F32: ctx.enter_context(nc.sbuf_tensor(f"q{layer}_{n}", s, d))
        groups = H if layer else 2
        wq = [sb(f"wq{i}", [P, 2, P]) for i in range(2)]
        qT, sq, rq = sb("qT", [P, T]), sb("sq", [P, T]), sb("rq", [P, T])
        qn = [sb(f"qn{i}", [P, T]) for i in range(2)]
        ps = [ctx.enter_context(nc.psum_tensor(f"q{layer}_ps{i}", [P, 2, 512], F32)) for i in range(4)]
        S = lambda n: g.sem(f"q{layer}_{n}")
        if layer:
            wk = [sb(f"wk{i}", [P, C]) for i in range(2)]
            wks = [sb(f"wks{i}", [P, C]) for i in range(2)]
            scale = sb("scale", [P, 3])
            qout = [sb(f"qout{i}", [P, T]) for i in range(2)]
            w_in = [S("w_in0"), S("w_in1")]
            sc_in, sc_ready = S("sc_in"), S("sc_ready")
            wk_ready, q_ready, qc_ready, sq_ready = S("wk_ready"), S("q_ready"), S("qc_ready"), S("sq_ready")
            sum_ready, rq_steps, qn_ready = S("sum_ready"), S("rq_steps"), S("qn_ready")
            out_ready, out_copied, out_free = S("out_ready"), S("out_copied"), [S("out_free0"), S("out_free1")]
            block = ctx.enter_context(nc.Block())
            pq, psum, pout = ps[0], ps[1], [ps[2], ps[3]]
            v2 = lambda t: t[:, :].rearrange("p (a n) -> p a n", a=2)

            @block.sync
            def _(sp):
                with nc.allow_non_contiguous_dma(reason="columns of 128 scales"):
                    sp.dma_start(scale[:, 0:1], g.a["gq"]).then_inc(sc_in, 16)
                    sp.dma_start(scale[:, 1:2], g.a["gk"]).then_inc(sc_in, 16)

                def load(h, i):
                    sp.dma_start(wq[i][:, :, :], g.a["L1_Wq"][h]).then_inc(w_in[i], 16)
                    sp.dma_start(wk[i][:, :], g.a["L1_WkT"][h]).then_inc(w_in[i], 16)
                for i in range(2):
                    load(i, i)
                def store(h, i):
                    sp.wait_ge(out_copied, h + 1)
                    sp.dma_start(g.qdram[1][:, :, bass.ds(h * NQ, NQ)].rearrange("b c q -> c b q"),
                                 qout[i][:, :].rearrange("c (b q) -> c b q", b=B)).then_inc(out_free[i], 16)
                with sp.Fori(0, H // 2 - 1) as u:
                    for i in range(2):
                        store(2 * u + i, i)
                        load(2 * u + i + 2, i)
                for i in range(2):
                    store(H - 2 + i, i)
                for i in range(2):
                    sp.wait_ge(out_free[i], 16 * (H // 2))

            @block.tensor
            def _(pe):
                with pe.Fori(0, H // 2) as u:
                    for i in range(2):
                        h = 2 * u + i
                        pe.wait_ge(w_in[i], 32 * u + 32)
                        pe.wait_ge(qc_ready, h)
                        for half in range(2):
                            for k in range(2):
                                mm = pe.matmul(pq[:, half, 0:HALF], wq[i][:, k, :],
                                               g.xnT[:, k, half * HALF:(half + 1) * HALF],
                                               start=(k == 0), stop=(k == 1))
                        mm.then_inc(q_ready, 1)
                        pe.wait_ge(sq_ready, h + 1)
                        for half in range(2):
                            mm = pe.matmul(psum[:, half, 0:HALF], g.ones[:, :],
                                           sq[:, half * HALF:(half + 1) * HALF], start=True, stop=True)
                        mm.then_inc(sum_ready, 1)
                        pe.wait_ge(qn_ready, h + 1)
                        pe.wait_ge(wk_ready, h + 1)
                        pe.wait_ge(out_copied, h)
                        for half in range(2):
                            mm = pe.matmul(pout[i][:, half, 0:HALF], wks[i][:, :],
                                           qn[i][:, half * HALF:(half + 1) * HALF], start=True, stop=True)
                        mm.then_inc(out_ready, 1)

            @block.scalar
            def _(act):
                with act.Fori(0, H // 2) as u:
                    for i in range(2):
                        h = 2 * u + i
                        act.wait_ge(qc_ready, h + 1)
                        act.wait_ge(sum_ready, h)
                        act.activation(sq[:, :], qT[:, :], ACT.Square).then_inc(sq_ready, 1)
                        act.wait_ge(rq_steps, 3 * h + 1)
                        act.activation(rq[:, :], rq[:, :], ACT.Sqrt).then_inc(rq_steps, 1)

            @block.vector
            def _(dve):
                dve.wait_ge(sc_in, 32)
                dve.tensor_scalar(scale[:, 2:3], scale[:, 0:1], scale[:, 1:2], HD1 ** -0.5,
                                  ALU.mult, ALU.mult).then_inc(sc_ready, 1)
                dve.wait_ge(sc_ready, 1)
                with dve.Fori(0, H // 2) as u:
                    for i in range(2):
                        h = 2 * u + i
                        dve.wait_ge(w_in[i], 32 * u + 32)
                        dve.tensor_scalar(wks[i][:, :], wk[i][:, :], scale[:, 2:3], None, ALU.mult)\
                           .then_inc(wk_ready, 1)
                        dve.wait_ge(q_ready, h + 1)
                        dve.tensor_copy(v2(qT), pq[:, :, 0:HALF]).then_inc(qc_ready, 1)
                        dve.wait_ge(sum_ready, h + 1)
                        dve.tensor_scalar(v2(rq), psum[:, :, 0:HALF], 1.0 / HD1, 1e-5, ALU.mult, ALU.add)\
                           .then_inc(rq_steps, 1)
                        dve.wait_ge(rq_steps, 3 * h + 2)
                        dve.reciprocal(rq[:, :], rq[:, :]).then_inc(rq_steps, 1)
                        dve.wait_ge(rq_steps, 3 * h + 3)
                        dve.wait_ge(qc_ready, h + 1)
                        dve.tensor_tensor(qn[i][:, :], qT[:, :], rq[:, :], ALU.mult).then_inc(qn_ready, 1)
                        dve.wait_ge(out_ready, h + 1)
                        dve.wait_ge(out_free[i], 16 * u)
                        dve.tensor_copy(v2(qout[i]), pout[i][:, :, 0:HALF]).then_inc(out_copied, 1)
            return

        wk_in = sb("wk_in", [P, 2, 2, C + 1])
        wkc = sb("wkc", [P, 2, 2, C + 1])
        wqa = sb("wqa", [P, 2, D])
        cols = sb("cols", [P, 2, 5])
        mkw = sb("mkw", [P, 2, 2, 8])
        lb = sb("lb", [P, 2, 2, H])
        lhk = [sb(f"lhk{i}", [P, C]) for i in range(2)]
        qa, qc = sb("qa", [P, T]), sb("qc", [P, T])
        qs = [sb(f"qs{i}", [P, T]) for i in range(2)]
        qout = [sb(f"qout{i}", [P, T]) for i in range(2)]
        bt = sb("bt", [H, 2, T])
        parts = sb("parts", [H, 3, T], BF16)
        in_done, pe_done, dve_done, act_done = S("in_done"), S("products"), S("vector_steps"), S("scalar_steps")
        lh_ready, hq_ready, copied, stored = S("lh_ready"), S("hq_ready"), S("copied"), [S("stored0"), S("stored1")]
        b_stored, b_ready = S("b_stored"), S("b_ready")
        block = ctx.enter_context(nc.Block())
        v2 = lambda t: t[:, :].rearrange("p (a n) -> p a n", a=2)
        NL = 32

        @block.sync
        def _(sp):
            sp.dma_start(wk_in[:, :, :, :], g.a["k0T"]).then_inc(in_done, 16)
            sp.dma_start(wqa[:, :, :], g.a["L0_Wq"]).then_inc(in_done, 16)
            sp.dma_start(cols[:, :, :], g.a["cols0"]).then_inc(in_done, 16)

            def store(v, h, m2, i, u):
                sp.wait_ge(copied, m2 + 1)
                sp.dma_start(g.qdram[2 * v][:, :, bass.ds(h * NQ, NQ)].rearrange("b c q -> c b q"),
                             qout[i][:, :].rearrange("c (b q) -> c b q", b=B)).then_inc(stored[i], 16)
            for r in range(4):
                v, half = r // 2, r % 2
                with sp.Fori(0, 4) as u:
                    for i in range(2):
                        store(v, half * 8 + 2 * u + i, r * 8 + 2 * u + i, i, u)
            for n in range(3):
                sp.dma_start(g.bdram[:, n, :].rearrange("b (h q) -> h b q", h=H),
                             parts[:, n, :].rearrange("h (b q) -> h b q", b=B)).then_inc(b_stored, 16)
            sp.dma_start(g.bdram_d.rearrange("b (h q) -> h b q", h=H),
                         bt[:, 1, :].rearrange("h (b q) -> h b q", b=B)).then_inc(b_stored, 16)
            sp.wait_ge(b_stored, 64)
            for i in range(2):
                sp.wait_ge(stored[i], 16 * NL // 2)

        @block.tensor
        def _(pe):
            pe.wait_ge(in_done, 48)
            for v in range(2):
                for half in range(2):
                    mm = pe.matmul(ps[3][:, v, half * 256:half * 256 + C + 1], g.cen[:, :], wk_in[:, v, half, :],
                                   start=True, stop=True)
            mm.then_inc(pe_done, 1)
            for half in range(2):
                for n in range(2):
                    for k in range(2):
                        mm = pe.matmul(ps[0][:, n, 0:HALF], wqa[:, k, half * P:(half + 1) * P],
                                       g.xnT[:, k, n * HALF:(n + 1) * HALF], start=(k == 0), stop=(k == 1))
                mm.then_inc(pe_done, 1)
                pe.wait_ge(dve_done, 2 + 6 * half)
                for n in range(2):
                    mm = pe.matmul(ps[1][:, n, 0:HALF], g.cen[:, :], qa[:, n * HALF:(n + 1) * HALF],
                                   start=True, stop=True)
                mm.then_inc(pe_done, 1)
                pe.wait_ge(act_done, 1 + 2 * half)
                for n in range(2):
                    mm = pe.matmul(ps[2][:, n, 0:HALF], g.blk[:, :], sq[:, n * HALF:(n + 1) * HALF],
                                   start=True, stop=True)
                mm.then_inc(pe_done, 1)
            pe.wait_ge(dve_done, 14)
            for v in range(2):
                for n in range(2):
                    for half in range(2):
                        mm = pe.matmul(ps[v][0:H, n, 0:HALF], lb[:, v, half, :],
                                       qs[half][:, n * HALF:(n + 1) * HALF], start=(half == 0), stop=(half == 1))
            mm.then_inc(pe_done, 1)
            for r in range(4):
                with pe.Fori(0, 4) as u:
                    for i in range(2):
                        m = r * 8 + 2 * u + i
                        pe.wait_ge(lh_ready, m + 1)
                        pe.wait_ge(copied, m)
                        for n in range(2):
                            mm = pe.matmul(ps[2 + i][:, n, 0:HALF], lhk[i][:, :],
                                           qs[r % 2][:, n * HALF:(n + 1) * HALF], start=True, stop=True)
                        mm.then_inc(hq_ready, 1)

        @block.scalar
        def _(act):
            for half in range(2):
                act.wait_ge(dve_done, 3 + 6 * half)
                act.activation(sq[:, :], qc[:, :], ACT.Square).then_inc(act_done, 1)
                act.wait_ge(dve_done, 4 + 6 * half)
                act.activation(rq[:, :], rq[:, :], ACT.Sqrt).then_inc(act_done, 1)

        @block.vector
        def _(dve):
            dve.wait_ge(in_done, 48)
            dve.wait_ge(pe_done, 1)
            for v in range(2):
                src = ps[3][:, v, :].rearrange("p (a n) -> p a n", a=2)[:, :, 0:C + 1]
                ins = dve.tensor_copy(wkc[:, v, :, :], src)
            ins.then_inc(dve_done, 1)
            for half in range(2):
                d0 = 6 * half
                dve.wait_ge(pe_done, 2 + 3 * half)
                dve.tensor_scalar(v2(qa), ps[0][:, :, 0:HALF], cols[:, half, 0:1], None, ALU.add)\
                   .then_inc(dve_done, 1)
                dve.wait_ge(pe_done, 3 + 3 * half)
                dve.tensor_copy(v2(qc), ps[1][:, :, 0:HALF]).then_inc(dve_done, 1)
                dve.wait_ge(pe_done, 4 + 3 * half)
                dve.tensor_scalar(v2(rq), ps[2][:, :, 0:HALF], 1.0 / HD0, 1e-6, ALU.mult, ALU.add)\
                   .then_inc(dve_done, 1)
                dve.wait_ge(act_done, 2 + 2 * half)
                dve.reciprocal(rq[:, :], rq[:, :]).then_inc(dve_done, 1)
                dve.wait_ge(dve_done, d0 + 5)
                dve.tensor_tensor(qc[:, :], qc[:, :], rq[:, :], ALU.mult).then_inc(dve_done, 1)
                dve.wait_ge(dve_done, d0 + 6)
                dve.tensor_scalar(qs[half][:, :], qc[:, :], cols[:, half, 1:2], cols[:, half, 2:3],
                                  ALU.mult, ALU.add).then_inc(dve_done, 1)
            for v in range(2):
                for half in range(2):
                    ins = dve.tensor_scalar(mkw[:, v, half, :], g.hmask[:, :], cols[:, half, 3 + v:4 + v],
                                            HD0 ** -0.5, ALU.mult, ALU.mult)
            ins.then_inc(b_ready, 1)
            dve.memset(lb[:, :, :, :], 0.0).then_inc(b_ready, 1)
            dve.wait_ge(b_ready, 2)
            for v in range(2):
                for half in range(2):
                    ins = dve.tensor_scalar(lb[:, v, half, 8 * half:8 * half + 8], mkw[:, v, half, :],
                                            wkc[:, v, half, C:C + 1], None, ALU.mult)
            ins.then_inc(dve_done, 1)
            dve.wait_ge(pe_done, 8)
            for v in range(2):
                ins = dve.tensor_copy(bt[:, v, :].rearrange("p (a n) -> p a n", a=2), ps[v][0:H, :, 0:HALF])
            ins.then_inc(b_ready, 1)
            dve.wait_ge(b_ready, 3)
            for n in range(3):
                dve.tensor_copy(parts[:, n, :], bt[:, 0, :]).then_inc(b_ready, 1)
                dve.wait_ge(b_ready, 4 + 2 * n)
                dve.tensor_tensor(bt[:, 0, :], bt[:, 0, :], parts[:, n, :], ALU.subtract).then_inc(b_ready, 1)
                dve.wait_ge(b_ready, 5 + 2 * n)
            for r in range(4):
                v, half = r // 2, r % 2

                with dve.Fori(0, 4) as u:
                    for i in range(2):
                        m = r * 8 + 2 * u + i
                        dve.tensor_scalar(lhk[i][:, :], wkc[:, v, half, 0:C], mkw[:, v, half, bass.ds(2 * u + i, 1)],
                                          None, ALU.mult).then_inc(lh_ready, 1)
                        dve.wait_ge(hq_ready, m + 1)
                        dve.wait_ge(stored[i], 16 * (4 * r + u))
                        dve.tensor_copy(v2(qout[i]), ps[2 + i][:, :, 0:HALF]).then_inc(copied, 1)


def phase_attention(nc, g, kind):
    nk = 1 if kind == 2 else NK
    rows = lambda j: DCA if kind == 2 else P if j < NK - 1 else (KR1 if kind == 1 else KR0)
    first = SEQ - DCA if kind == 2 else 0
    ncol = DCA if kind == 2 else SEQ
    rp = DCA if kind == 2 else P
    qd, od = g.qdram[kind], g.odram[kind]
    with ExitStack() as ctx:
        sb = lambda n, s, d=F32: ctx.enter_context(nc.sbuf_tensor(f"a{kind}_{n}", s, d))
        two = lambda n, s, d=F32: [sb(f"{n}{i}", s, d) for i in range(2)]
        yT, y1, Q = two("yT", [P, ncol]), two("y1", [rp, nk, C + 1]), two("Q", [P, HQ])
        bias = two("bias", [3, HQ], BF16) if kind == 0 else two("biasd", [1, HQ])
        ones3 = sb("ones3", [3, P], BF16)
        S = two("S", [rp, nk, HQ])
        mx, mb = sb("mx", [P, HQ]), sb("mb", [rp, HQ])
        mcol, diag = sb("mcol", [P, FT]), sb("diag", [P, FT, P])
        rden, on, oT = sb("rden", [P, FT]), sb("on", [P, FT, C]), sb("oT", [P, HQ])
        ring = [ctx.enter_context(nc.psum_tensor(f"a{kind}_ring{i}", [P, 512], F32)) for i in range(RING)]
        tb = ctx.enter_context(nc.psum_tensor(f"a{kind}_tb", [P, 512], F32))
        ob = [ctx.enter_context(nc.psum_tensor(f"a{kind}_ob{i}", [P, 512], F32)) for i in range(3)]
        N = lambda n: g.sem(f"a{kind}_{n}")
        yT_in, y_in, one_set = [N("yT_in0"), N("yT_in1")], [N("y_in0"), N("y_in1")], N("one_set")
        s_ready, s_scaled, mx_ready = N("s_ready"), N("s_scaled"), N("mx_ready")
        mT_ready, mT_taken, diag_ready = N("mT_ready"), N("mT_taken"), N("diag_ready")
        mb_psum, mb_ready, shifted, p_ready = N("mb_psum"), N("mb_ready"), N("shifted"), N("p_ready")
        o_ready, rden_ready, on_ready = N("o_ready"), N("rden_ready"), N("on_ready")
        oT_ready, oT_copied, stored = N("oT_ready"), N("oT_copied"), N("stored")
        block = ctx.enter_context(nc.Block())
        SC = 2 * nk
        USES = SC + 2
        OI = [(0, 3), (3, 6), (6, 7)]
        TI = [(0, 4), (4, 7)]
        is_int = lambda b: isinstance(b, int)

        def steps(eng, step):
            step(0, 0, 0, True, False, False)
            step(1, 0, 1, True, True, False)
            with eng.Fori(0, (B - 2) // 2) as u:
                for i in range(2):
                    step(2 * u + 2 + i, u + 1, i, True, True, True)
            step(B, B // 2, 0, False, True, True)
            step(B + 1, B // 2, 1, False, False, True)

        @block.sync
        def _(sp):
            def load(b, i):
                sp.dma_start(yT[i][:, :], g.a["ctxT"][b, :, first:SEQ]).then_inc(yT_in[i], 16)
                sp.dma_start(Q[i][:, :], qd[b]).then_inc(yT_in[i], 16)
                if kind == 0:
                    sp.dma_start(bias[i][:, :], g.bdram[b]).then_inc(yT_in[i], 16)
                if kind == 2:
                    sp.dma_start(bias[i][:, :], g.bdram_d[bass.ds(b, 1), :]).then_inc(yT_in[i], 16)

            def load_y(b, i):
                n = rows(nk - 1)
                if kind != 2:
                    sp.dma_start(y1[i][:, 0:NK - 1, 0:C],
                                 g.a["ctx"][b, 0:(NK - 1) * P, :].rearrange("(j p) c -> p j c", p=P)).then_inc(y_in[i], 16)
                r0 = first + (nk - 1) * P
                sp.dma_start(y1[i][0:n, nk - 1, 0:C], g.a["ctx"][b, r0:r0 + n, :]).then_inc(y_in[i], 16)
            sp.wait_ge(one_set, 3)
            for i in range(2):
                load(i, i)
                load_y(i, i)
            with sp.Fori(0, (B - 2) // 2) as u:
                for i in range(2):
                    b = 2 * u + 2 + i
                    sp.wait_ge(s_ready, SC * (b - 1))
                    load(b, i)
                    sp.wait_ge(o_ready, b - 1)
                    load_y(b, i)
            sp.wait_ge(stored, 16 * B)

        LW = 16 * (2 if kind == 1 else 3)
        YW = 16 * (1 if kind == 2 else 2)

        @block.tensor
        def _(pe):
            def step(b, pair, i, front, back, out):
                def scores(j):
                    n = rows(j)
                    for half in range(2):
                        use = 2 * j + half
                        r = (USES * i + use) % RING
                        if use >= RING:
                            pe.wait_ge(s_scaled, SC * b + use - RING + 1)
                        elif not is_int(b) or b > 0:
                            if use >= RING - 2:
                                pe.wait_ge(mb_ready, 2 * b + use - RING + 1)
                            else:
                                pe.wait_ge(s_scaled, SC * b)
                        cols = slice(half * HALF, (half + 1) * HALF)
                        mm = pe.matmul(ring[r][0:n, 0:HALF], yT[i][:, j * P:j * P + n], Q[i][:, cols],
                                       start=True, stop=(kind == 1))
                        if kind != 1:
                            one = ones3[:, 0:n] if kind == 0 else g.ones[0:1, 0:n]
                            mm = pe.matmul(ring[r][0:n, 0:HALF], one, bias[i][:, cols], start=False, stop=True)
                        mm.then_inc(s_ready, 1)

                def output(j):
                    n = rows(j)
                    pe.wait_ge(p_ready, nk * (b - 1) + j + 1)
                    for k, (lo, hi) in enumerate(OI):
                        for q in range(lo, hi):
                            mm = pe.matmul(ob[k][:, (q - lo) * (C + 1):(q - lo + 1) * (C + 1)],
                                           S[1 - i][0:n, j, q * P:(q + 1) * P], y1[1 - i][0:n, j, :],
                                           start=(j == 0 and q == lo), stop=(j == nk - 1),
                                           skip_group_check=True)
                    if j == nk - 1:
                        mm.then_inc(o_ready, 1)

                def transposes_out():
                    pe.wait_ge(on_ready, 3 * (b - 1))
                    for k, (lo, hi) in enumerate(TI):
                        if k == 0:
                            pe.wait_ge(mT_taken, 2 * min(b, B) if is_int(b) else 2 * b)
                            pe.wait_ge(oT_copied, 2 * (b - 2))
                        else:
                            pe.wait_ge(oT_copied, 2 * (b - 2) + k)
                        for q in range(lo, hi):
                            mm = pe.transpose(tb[:, (q - lo) * P:(q - lo + 1) * P], on[:, q, :], g.ident[:, :])
                        mm.then_inc(oT_ready, 1)

                if front:
                    pe.wait_ge(yT_in[i], (pair + 1) * LW)
                if back:
                    pe.wait_ge(y_in[1 - i], (pair if i == 0 else pair + 1) * YW)
                    if not (is_int(b) and b == 1):
                        pe.wait_ge(on_ready, 3 * (b - 1))
                lag = min(2, nk)
                for j in range(nk + lag):
                    if front and j < nk:
                        scores(j)
                    if out and j == min(4, nk - 1):
                        transposes_out()
                    if back and j >= lag:
                        output(j - lag)
                if front:
                    pe.wait_ge(mx_ready, nk * (b + 1))
                    if out:
                        pe.wait_ge(oT_copied, 2 * (b - 1))
                    for k, (lo, hi) in enumerate(TI):
                        if k:
                            pe.wait_ge(mT_taken, 2 * b + k)
                        for q in range(lo, hi):
                            mm = pe.transpose(tb[:, (q - lo) * P:(q - lo + 1) * P], mx[:, q * P:(q + 1) * P],
                                              g.ident[:, :])
                        mm.then_inc(mT_ready, 1)
                    pe.wait_ge(diag_ready, b + 1)
                    if not (is_int(b) and b == 0):
                        pe.wait_ge(mb_ready, 2 * b)
                    for half in range(2):
                        r = (USES * i + SC + half) % RING
                        mm = pe.matmul(ring[r][0:rp, 0:HALF], g.ones[:, 0:rp],
                                       diag[:, :, :].rearrange("p a n -> p (a n)")[:, half * HALF:(half + 1) * HALF],
                                       start=True, stop=True)
                        mm.then_inc(mb_psum, 1)
            steps(pe, step)

        @block.vector
        def _(dve):
            dve.memset(ones3[:, :], 1.0).then_inc(one_set, 1)
            for i in range(2):
                dve.memset(y1[i][:, :, C:C + 1], 1.0).then_inc(one_set, 1)
            hoff = 0 if kind else H
            if rp < P:
                dve.memset(mx[:, :], -3.0e38).then_inc(one_set, 1)
                dve.wait_ge(one_set, 4)

            def step(b, pair, i, front, back, out):
                for j in range(nk):
                    n = rows(j)
                    if front:
                        for half in range(2):
                            r = (USES * i + 2 * j + half) % RING
                            dve.wait_ge(s_ready, SC * b + 2 * j + half + 1)
                            if j == 0 and half == 0 and not (is_int(b) and b < 2):
                                dve.wait_ge(o_ready, b - 1)
                            if kind == 2:
                                rk = g.rkd[0:n, b, 8 * half:8 * half + 8]
                            else:
                                rk = g.rk[0:n, b, j, hoff + 8 * half:hoff + 8 * half + 8]
                            dve.tensor_tensor(
                                S[i][0:n, j, half * HALF:(half + 1) * HALF].rearrange("p (h q) -> p h q", h=8),
                                ring[r][0:n, 0:HALF].rearrange("p (h q) -> p h q", h=8),
                                rk.unsqueeze(2).broadcast_to([n, 8, NQ]), ALU.mult).then_inc(s_scaled, 1)
                        dve.wait_ge(s_scaled, SC * b + 2 * j + 2)
                        if j == 0:
                            if not (is_int(b) and b == 0):
                                dve.wait_ge(mT_ready, 2 * b)
                            dve.tensor_copy(mx[0:rp, :], S[i][:, 0, :]).then_inc(mx_ready, 1)
                        else:
                            dve.wait_ge(mx_ready, nk * b + j)
                            dve.tensor_tensor(mx[0:n, :], mx[0:n, :], S[i][0:n, j, :], ALU.max).then_inc(mx_ready, 1)
                if front:
                    for k, (lo, hi) in enumerate(TI):
                        dve.wait_ge(mT_ready, 2 * b + k + 1)
                        dve.tensor_reduce(mcol[:, lo:hi],
                                          tb[:, 0:(hi - lo) * P].rearrange("p (a n) -> p a n", n=P),
                                          X, ALU.max).then_inc(mT_taken, 1)
                    dve.wait_ge(mT_taken, 2 * b + 2)
                    dve.tensor_tensor(diag[:, :, :], g.ident[:, None, :].broadcast_to([P, FT, P]),
                                      mcol[:, :, None].broadcast_to([P, FT, P]), ALU.mult).then_inc(diag_ready, 1)
                if back:
                    dve.wait_ge(o_ready, b)
                    if not (is_int(b) and b == 1):
                        dve.wait_ge(oT_ready, 2 * (b - 1))
                    for k, (lo, hi) in enumerate(OI):
                        den = ob[k][:, 0:(hi - lo) * (C + 1)].rearrange("p (a n) -> p a n", n=C + 1)
                        ins = dve.reciprocal(rden[:, lo:hi], den[:, :, C])
                    ins.then_inc(rden_ready, 1)
                    dve.wait_ge(rden_ready, b)
                    for k, (lo, hi) in enumerate(OI):
                        den = ob[k][:, 0:(hi - lo) * (C + 1)].rearrange("p (a n) -> p a n", n=C + 1)
                        dve.tensor_tensor(on[:, lo:hi, :], den[:, :, 0:C],
                                          rden[:, lo:hi].unsqueeze(2).broadcast_to([P, hi - lo, C]), ALU.mult)\
                           .then_inc(on_ready, 1)
            steps(dve, step)

        @block.gpsimd
        def _(pool):
            def step(b, pair, i, front, back, out):
                if not back:
                    return
                for j in range(nk):
                    n = rows(j)
                    if j == 0:
                        pool.wait_ge(mb_ready, 2 * b)
                    pool.tensor_tensor(S[1 - i][0:n, j, :], S[1 - i][0:n, j, :], mb[0:n, :], ALU.subtract)\
                        .then_inc(shifted, 1)
            steps(pool, step)

        @block.scalar
        def _(act):
            def step(b, pair, i, front, back, out):
                for j in range(nk):
                    n = rows(j)
                    if back:
                        act.wait_ge(shifted, nk * (b - 1) + j + 1)
                        act.activation(S[1 - i][0:n, j, :], S[1 - i][0:n, j, :], ACT.Exp).then_inc(p_ready, 1)
                    if out and j == min(5, nk - 1):
                        if not (is_int(b) and b == 2):
                            act.wait_ge(stored, 16 * (b - 2))
                        for k, (lo, hi) in enumerate(TI):
                            act.wait_ge(oT_ready, 2 * (b - 2) + k + 1)
                            act.activation(oT[:, lo * P:hi * P], tb[:, 0:(hi - lo) * P], ACT.Copy).then_inc(oT_copied, 1)
                        act.wait_ge(oT_copied, 2 * (b - 1))
                        act.dma_start(od[b - 2], oT[:, :]).then_inc(stored, 16)
                if front:
                    if back:
                        act.wait_ge(shifted, nk * b)
                    for half in range(2):
                        r = (USES * i + SC + half) % RING
                        act.wait_ge(mb_psum, 2 * b + half + 1)
                        act.activation(mb[:, half * HALF:(half + 1) * HALF], ring[r][0:rp, 0:HALF], ACT.Copy)\
                           .then_inc(mb_ready, 1)
            steps(act, step)


def phase_project(nc, g, layer):
    with ExitStack() as ctx:
        sb = lambda n, s, d=F32: ctx.enter_context(nc.sbuf_tensor(f"p{layer}_{n}", s, d))
        V = 1 if layer else 2
        src = [g.odram[1]] if layer else [g.odram[0], g.odram[2]]
        M = sb("M", [P, V * H, D])
        wv = sb("wv", [P, V * H, C])
        wo = sb("wo", [P, H if layer else 2, D])
        NB = B // 2
        ot = [sb(f"ot{i}", [P, NB, HQ]) for i in range(2)]
        sumT = sb("sumT", [P, 2, T])
        NCH = 2 * V
        ps = [ctx.enter_context(nc.psum_tensor(f"p{layer}_ps{i}", [P, 512], F32)) for i in range(8)]
        N = lambda n: g.sem(f"p{layer}_{n}")
        w_in, ot_in, masked = N("w_in"), [N("ot_in0"), N("ot_in1")], N("masked")
        m_ready, m_copied, acc_ready, added = N("m_ready"), N("m_copied"), N("acc_ready"), N("added")
        sum_ready, back = N("sum_ready"), N("back")
        if not layer:
            v0 = sb("v0", [P, 2, 2, C])
            bv, bvs, bo, bias = sb("bv", [P, 2, 2]), sb("bvs", [P, 2]), sb("bo", [1, D]), sb("bias", [P, 2])
            bias_steps = N("bias_steps")
        block = ctx.enter_context(nc.Block())
        NM = V * H // 2

        @block.sync
        def _(sp):
            if layer:
                sp.dma_start(wv[:, :, :], g.a["L1_WvT"].rearrange("h d c -> d h c")).then_inc(w_in, 16)
                sp.dma_start(wo[:, :, :], g.a["L1_Wo"].rearrange("h d n -> d h n")).then_inc(w_in, 16)
            else:
                sp.dma_start(v0[:, :, :, :], g.a["v0T"]).then_inc(w_in, 16)
                sp.dma_start(wo[:, :, :], g.a["L0_Wo"]).then_inc(w_in, 16)
                sp.dma_start(bv[:, :, :], g.a["bv0"]).then_inc(w_in, 16)
                sp.dma_start(bo[:, :], g.a["bo0"]).then_inc(w_in, 16)

            for n in range(NCH):
                if n >= 2:
                    sp.wait_ge(acc_ready, n - 1)
                half = n % 2
                sp.dma_start(ot[half][:, :, :], src[n // 2][half * NB:(half + 1) * NB].rearrange("b c n -> c b n"))\
                    .then_inc(ot_in[half], 16)

        @block.tensor
        def _(pe):
            pe.wait_ge(w_in, 32 if layer else 64)
            if not layer:
                pe.wait_ge(masked, 1)
                pe.wait_ge(bias_steps, 1)
                for dk in range(2):
                    cols = slice(dk * P, (dk + 1) * P)
                    for half in range(2):
                        pe.matmul(ps[7][:, dk:dk + 1], wo[:, half, cols], bvs[:, half:half + 1],
                                  start=(half == 0), stop=False)
                    mm = pe.matmul(ps[7][:, dk:dk + 1], bo[0:1, cols], g.ones[0:1, 0:1], start=False, stop=True)
                mm.then_inc(bias_steps, 1)
            for m in range(NM):
                if m >= 4:
                    pe.wait_ge(m_copied, m - 3)
                for k in range(2):
                    h = 2 * m + k
                    rhs = wo[:, h, :] if layer else wo[:, (h % H) // 8, :]
                    mm = pe.matmul(ps[m % 4][:, k * D:(k + 1) * D], wv[:, h, :], rhs, start=True, stop=True)
                mm.then_inc(m_ready, 1)
            pe.wait_ge(m_copied, NM)
            for n in range(NCH):
                v, half = n // 2, n % 2
                pe.wait_ge(ot_in[half], 16 * v + 16)
                if n == 0:
                    if not layer:
                        pe.wait_ge(bias_steps, 3)
                for h in range(H):
                    rhs = ot[half][:, :, h * NQ:(h + 1) * NQ]
                    for dk in range(2):
                        mm = pe.matmul(ps[4 + 2 * half + dk][:, 0:HALF].rearrange("p (b q) -> p b q", b=NB),
                                       M[:, v * H + h, dk * P:(dk + 1) * P], rhs,
                                       start=(v == 0 and h == 0), stop=(v == V - 1 and h == H - 1),
                                       skip_group_check=True)
                mm.then_inc(acc_ready, 1)
            for m in range(NT // 2):
                pe.wait_ge(sum_ready, 2 if m < 2 else 4)
                for k in range(2):
                    t = 2 * m + k
                    for dk in range(2):
                        mm = pe.transpose(ps[m][0:TT, (2 * k + dk) * P:(2 * k + dk + 1) * P],
                                          sumT[:, dk, t * TT:(t + 1) * TT], g.ident[:, :])
                mm.then_inc(back, 1)

        @block.scalar
        def _(act):
            for m in range(1, NM, 2):
                act.wait_ge(m_ready, m + 1)
                act.wait_ge(m_copied, m)
                act.activation(M[:, 2 * m:2 * m + 2, :].rearrange("p a n -> p (a n)"), ps[m % 4][:, :], ACT.Copy)\
                    .then_inc(m_copied, 1)

        @block.vector
        def _(dve):
            if not layer:
                dve.wait_ge(w_in, 64)
                for n in range(2 * H):
                    v, h = n // H, n % H
                    ins = dve.tensor_scalar(wv[:, n, :], v0[:, v, h // 8, :], g.hmask[:, h % 8:h % 8 + 1], None,
                                            ALU.mult)
                ins.then_inc(masked, 1)
                dve.tensor_tensor(bvs[:, :], bv[:, 0, :], bv[:, 1, :], ALU.add).then_inc(bias_steps, 1)
            for m in range(0, NM, 2):
                dve.wait_ge(m_ready, m + 1)
                if m:
                    dve.wait_ge(m_copied, m)
                dve.tensor_copy(M[:, 2 * m:2 * m + 2, :].rearrange("p a n -> p (a n)"), ps[m % 4][:, :])\
                    .then_inc(m_copied, 1)
            if not layer:
                dve.wait_ge(bias_steps, 2)
                dve.tensor_copy(bias[:, :], ps[7][:, 0:2]).then_inc(bias_steps, 1)
                dve.wait_ge(bias_steps, 3)
            for half in range(2):
                dve.wait_ge(acc_ready, NCH - 1 + half)
                for dk in range(2):
                    dst = sumT[:, dk, half * HALF:(half + 1) * HALF]
                    if layer:
                        dve.tensor_copy(dst, ps[4 + 2 * half + dk][:, 0:HALF]).then_inc(sum_ready, 1)
                    else:
                        dve.tensor_scalar(dst, ps[4 + 2 * half + dk][:, 0:HALF], bias[:, dk:dk + 1], None, ALU.add)\
                           .then_inc(sum_ready, 1)
            for m in range(NT // 2):
                dve.wait_ge(back, m + 1)
                xs = g.x[:, 2 * m:2 * m + 2, :]
                dve.tensor_tensor(xs, xs, ps[m][0:TT, :].rearrange("p (a n) -> p a n", a=2), ALU.add).then_inc(added, 1)


def phase_moe(nc, g):
    SLOTS = E * CAP
    NOE = 99.0
    with ExitStack() as ctx:
        sb = lambda n, s, d=F32: ctx.enter_context(nc.sbuf_tensor(f"m_{n}", s, d))
        N = lambda n: g.sem(f"m_{n}")
        r3 = lambda n: sb(n, [TT, NT, E])
        gw, gb, eid, trash, low = sb("gw", [P, 2, E]), sb("gb", [TT, E]), sb("eid", [TT, E]), \
            sb("trash", [TT, 2, NT]), sb("low", [TT, TT])
        lg, ab, ex, up, ln, dd, sc, sk = [r3(n) for n in ("lg", "ab", "ex", "up", "ln", "dd", "sc", "sk")]
        oh, tmp, A, pos = [r3("oh0"), r3("oh1")], r3("tmp"), r3("A"), r3("pos")
        mcol, ei, w, den = sb("mcol", [TT, NT]), sb("ei", [TT, 2, NT]), sb("w", [TT, 2, NT]), sb("den", [TT, NT])
        ps_, valid, base, sidx, gidx = [sb(n, [TT, 2, NT]) for n in ("pcol", "valid", "base", "sidx", "gidx")]
        su, gu = sb("su", [TT, 2 * NT], U32), sb("gu", [TT, 2 * NT], U32)
        zero = sb("zero", [P, 2048])
        w13 = [sb(f"w13{i}", [P, 2, 2, 256]) for i in range(2)]
        w2 = [sb(f"w2{i}", [P, 2, D]) for i in range(2)]
        xe, xeT, he, ye = [[sb(f"{n}{i}", [P, 2 * P]) for i in range(2)] for n in ("xe", "xeT", "he", "ye")]
        ee = [sb(f"ee{i}", [P, 2 * P]) for i in range(2)]
        hs, es = sb("hs", [P, 2, T]), sb("es", [P, T])
        yg = sb("yg", [TT, 2 * NT, D])
        ps = [ctx.enter_context(nc.psum_tensor(f"m_ps{i}", [P, 512], F32)) for i in range(8)]
        c_in, w_in, x_in = N("c_in"), [N("w_in0"), N("w_in1")], [N("x_in0"), N("x_in1")]
        zeroed, zero_out, scattered, gathered = N("zeroed"), N("zero_out"), N("scattered"), N("gathered")
        lg_psum, act_steps, steps, count_psum = N("lg_psum"), N("act_steps"), N("router_steps"), N("count_psum")
        shared_in, sh_psum, sh_exp, sh_steps, sh_out, sh_added = N("shared_in"), N("sh_psum"), N("sh_exp"), \
            N("sh_steps"), N("sh_out"), N("sh_added")
        w_zero, side = N("w_zero"), N("side_steps")
        xT_psum, xT_ready, gu_psum, e_exp, e_steps, h_ready, y_psum, y_ready = [
            N(n) for n in ("xT_psum", "xT_ready", "gu_psum", "e_exp", "e_steps", "h_ready", "y_psum", "y_ready")]
        y_stored, summed = [N("y_stored0"), N("y_stored1")], N("summed")
        block = ctx.enter_context(nc.Block())
        xbuf, ybuf = g.xbuf, g.ybuf

        @block.sync
        def _(sp):
            consts = [(gw, g.a["gw"]), (gb, g.a["gb"]), (eid, g.a["eid"]), (trash, g.a["trash"]), (low, g.a["low"])]
            for dst, src in consts:
                sp.dma_start(dst[tuple(slice(None) for _ in dst.shape)], src).then_inc(c_in, 16)

            def load_w(e, i):
                sp.dma_start(w13[i][:, :, 0, 0:FF], g.a["W1T"][e]).then_inc(w_in[i], 16)
                sp.dma_start(w13[i][:, :, 1, 0:FF], g.a["W3T"][e]).then_inc(w_in[i], 16)
                sp.dma_start(w2[i][:, 0, :], g.a["W2T"][e, 0:P, :]).then_inc(w_in[i], 16)
                sp.dma_start(w2[i][0:FF - P, 1, :], g.a["W2T"][e, P:FF, :]).then_inc(w_in[i], 16)
            sp.wait_ge(zeroed, 1)
            for n in range(0, SLOTS, 1024):
                sp.dma_start(xbuf[n:n + 1024, :].rearrange("(p a) d -> p (a d)", p=P), zero[:, :]).then_inc(zero_out, 16)
            sp.wait_ge(w_zero, 2)
            load_w(E, 0)
            load_w(0, 1)
            sp.wait_ge(sh_out, NT)
            sp.wait_ge(scattered, 16 * 2 * NT)
            sp.dma_start(xe[1][:, :], xbuf[0:CAP, :]).then_inc(x_in[1], 16)
            load_w(1, 0)
            sp.dma_start(xe[0][:, :], xbuf[CAP:2 * CAP, :]).then_inc(x_in[0], 16)

            def store(e, i):
                sp.wait_ge(y_ready, e + 1)
                sp.dma_start(ybuf[bass.ds(e * CAP, CAP), :], ye[i][:, :]).then_inc(y_stored[i], 16)
            with sp.Fori(0, E // 2 - 1) as u:
                for k in range(2):
                    e, i = 2 * u + k, 1 - k
                    store(e, i)
                    load_w(e + 2, i)
                    sp.dma_start(xe[i][:, :], xbuf[bass.ds((e + 2) * CAP, CAP), :]).then_inc(x_in[i], 16)
            for k in range(2):
                store(E - 2 + k, 1 - k)

        @block.gpsimd
        def _(pool):
            pool.memset(zero[:, :], 0.0).then_inc(zeroed, 1)
            for i in range(2):
                pool.memset(w13[i][:, :, :, :], 0.0).then_inc(w_zero, 1)
            pool.wait_ge(zero_out, 16 * (SLOTS // 1024))
            pool.wait_ge(steps, 29)
            for t in range(NT):
                for k in range(2):
                    pool.indirect_dma_start(
                        out=xbuf, out_offset=bass.IndirectOffsetOnAxis(ap=su[:, k * NT + t:k * NT + t + 1], axis=0),
                        in_=g.xn[:, t, :], in_offset=None).then_inc(scattered, 16)
            for i in range(2):
                pool.wait_ge(y_stored[i], 16 * (E // 2))
            for t in range(NT):
                for k in range(2):
                    n = k * NT + t
                    pool.indirect_dma_start(
                        out=yg[:, n, :], out_offset=None, in_=ybuf,
                        in_offset=bass.IndirectOffsetOnAxis(ap=gu[:, n:n + 1], axis=0)).then_inc(gathered, 16)
            pool.wait_ge(gathered, 16 * 2 * NT)

        @block.tensor
        def _(pe):
            pe.wait_ge(c_in, 16 * 5)
            for t in range(NT):
                for k in range(2):
                    mm = pe.matmul(ps[0][0:TT, t * E:(t + 1) * E], g.xnT[:, k, t * TT:(t + 1) * TT], gw[:, k, :],
                                   start=(k == 0), stop=(k == 1), skip_group_check=True)
            mm.then_inc(lg_psum, 1)
            pe.wait_ge(w_in[0], 64)
            def shared_part(part):
                for gu_ in range(2):
                    for half in range(2):
                        for k in range(2):
                            mm = pe.matmul(ps[1 + 2 * gu_ + half][:, 0:HALF],
                                           w13[0][:, k, gu_, part * P:(part + 1) * P],
                                           g.xnT[:, k, half * HALF:(half + 1) * HALF], start=(k == 0), stop=(k == 1))
                mm.then_inc(sh_psum, 1)
            shared_part(0)
            pe.wait_ge(steps, 19)
            flat = A[:, :, :].rearrange("p t e -> p (t e)")
            pe.matmul(ps[0][0:TT, 0:E], low[:, :], flat[:, 0:E], start=True, stop=True, skip_group_check=True)
            pe.matmul(ps[0][0:TT, E:NT * E], low[:, :], flat[:, E:NT * E], start=True, stop=False,
                      skip_group_check=True)
            for t in reversed(range(NT - 1)):
                mm = pe.matmul(ps[0][0:TT, (t + 1) * E:NT * E].rearrange("p (t e) -> p t e", e=E), g.ones[0:TT, 0:TT],
                               A[:, t:t + 1, :].broadcast_to([TT, NT - 1 - t, E]), start=False, stop=(t == 0),
                               skip_group_check=True)
            mm.then_inc(count_psum, 1)
            pe.wait_ge(sh_steps, 4)
            shared_part(1)
            pe.wait_ge(sh_steps, 8)
            for t in range(NT):
                if t >= 2:
                    pe.wait_ge(sh_added, t - 1)
                pe.matmul(ps[5 + t % 2][0:TT, 0:D], hs[:, 0, t * TT:(t + 1) * TT], w2[0][:, 0, :], start=True, stop=False)
                pe.matmul(ps[5 + t % 2][0:TT, 0:D], hs[0:FF - P, 1, t * TT:(t + 1) * TT], w2[0][0:FF - P, 1, :],
                          start=False, stop=True).then_inc(sh_out, 1)
            pe.wait_ge(sh_added, NT)

            with pe.Fori(0, E // 2) as u:
                for k in range(2):
                    e, i = 2 * u + k, 1 - k
                    pe.wait_ge(x_in[i], 16 * u + 16)
                    pe.wait_ge(w_in[i], 64 * u + (128 if k else 64))
                    pe.wait_ge(xT_ready, e)
                    for d in range(2):
                        mm = pe.transpose(ps[4 * k][:, d * P:(d + 1) * P], xe[i][:, d * P:(d + 1) * P], g.ident[:, :])
                    mm.then_inc(xT_psum, 1)
                for k in range(2):
                    e, i = 2 * u + k, 1 - k
                    pe.wait_ge(xT_ready, e + 1)
                    pe.wait_ge(h_ready, e)
                    for m in range(4):
                        bank = ps[4 * k + 1 + m // 2]
                        for d in range(2):
                            mm = pe.matmul(bank[:, (m % 2) * P:(m % 2 + 1) * P],
                                           w13[i][:, d, m // 2, (m % 2) * P:(m % 2 + 1) * P],
                                           xeT[i][:, d * P:(d + 1) * P], start=(d == 0), stop=(d == 1),
                                           skip_group_check=True)
                    mm.then_inc(gu_psum, 1)
                for k in range(2):
                    e, i = 2 * u + k, 1 - k
                    pe.wait_ge(h_ready, e + 1)
                    pe.wait_ge(y_ready, e)
                    pe.matmul(ps[4 * k + 3][:, 0:D], he[i][:, 0:P], w2[i][:, 0, :], start=True, stop=False)
                    pe.matmul(ps[4 * k + 3][:, 0:D], he[i][0:FF - P, P:2 * P], w2[i][0:FF - P, 1, :],
                              start=False, stop=True).then_inc(y_psum, 1)

        @block.scalar
        def _(act):
            act.wait_ge(steps, 2)
            act.activation(ex[:, :, :], ab[:, :, :], ACT.Exp, scale=-1.0).then_inc(act_steps, 1)
            for part in range(2):
                for half in range(2):
                    act.wait_ge(sh_psum, part + 1)
                    if part:
                        act.wait_ge(sh_steps, 2 * half + 2)
                    act.activation(es[:, half * HALF:(half + 1) * HALF], ps[1 + half][:, 0:HALF], ACT.Exp, scale=-1.0)\
                       .then_inc(sh_exp, 1)
                if part == 0:
                    act.wait_ge(steps, 3)
                    act.activation(ln[:, :, :], up[:, :, :], ACT.Ln).then_inc(act_steps, 1)
                    act.wait_ge(steps, 8)
                    act.activation(sc[:, :, :], sc[:, :, :], ACT.Sqrt).then_inc(act_steps, 1)
            with act.Fori(0, E // 2) as u:
                for k in range(2):
                    e, i = 2 * u + k, 1 - k
                    act.wait_ge(gu_psum, e + 1)
                    act.wait_ge(h_ready, e)
                    act.activation(ee[i][:, :], ps[4 * k + 1][:, 0:2 * P], ACT.Exp, scale=-1.0).then_inc(e_exp, 1)
                for k in range(2):
                    e, i = 2 * u + k, 1 - k
                    act.wait_ge(y_psum, e + 1)
                    act.wait_ge(y_stored[i], 16 * u)
                    act.activation(ye[i][:, :], ps[4 * k + 3][:, 0:D], ACT.Copy).then_inc(y_ready, 1)

        @block.vector
        def _(dve):
            at = [0]

            def step(ins):
                at[0] += 1
                ins.then_inc(steps, 1)
                dve.wait_ge(steps, at[0])

            def bt(col):
                return col.unsqueeze(2).broadcast_to([TT, NT, E])

            def be(row):
                return row.unsqueeze(1).broadcast_to([TT, NT, E])
            a3 = lambda t: t[:, :, :]
            dve.wait_ge(lg_psum, 1)
            dve.wait_ge(c_in, 16 * 5)
            step(dve.tensor_copy(lg[:, :, :], ps[0][0:TT, 0:NT * E].rearrange("p (t e) -> p t e", e=E)))
            step(dve.scalar_tensor_tensor(out=a3(ab), in0=a3(lg), scalar=-1.0, in1=a3(lg), op0=ALU.mult,
                                          op1=ALU.max))
            dve.wait_ge(act_steps, 1)
            step(dve.tensor_scalar(a3(up), a3(ex), 1.0, None, ALU.add))
            step(dve.tensor_scalar(a3(dd), a3(up), 1.0, 1e-30, ALU.subtract, ALU.max))
            dve.reciprocal(a3(sk), a3(dd)).then_inc(side, 1)
            dve.tensor_scalar(a3(tmp), a3(up), 1.0, None, ALU.is_equal).then_inc(side, 1)
            dve.wait_ge(act_steps, 2)
            dve.wait_ge(side, 2)
            step(dve.tensor_tensor(a3(sk), a3(sk), a3(ln), ALU.mult))
            step(dve.tensor_tensor(a3(sk), a3(sk), a3(tmp), ALU.add))
            step(dve.tensor_tensor(a3(sk), a3(sk), a3(ex), ALU.mult))
            step(dve.scalar_tensor_tensor(out=a3(sc), in0=a3(lg), scalar=0.0, in1=a3(sk), op0=ALU.max,
                                          op1=ALU.add))
            dve.wait_ge(act_steps, 3)
            step(dve.tensor_tensor(a3(sk), a3(sc), be(gb[:, :]), ALU.add))
            for k in range(2):
                step(dve.tensor_reduce(mcol[:, :], a3(sk), X, ALU.max))
                step(dve.tensor_tensor(a3(tmp), a3(sk), bt(mcol[:, :]), ALU.is_equal))
                step(dve.tensor_tensor(a3(tmp), a3(tmp), be(eid[:, :]), ALU.mult))
                step(dve.tensor_reduce(ei[:, k, :], a3(tmp), X, ALU.min))
                if k == 0:
                    step(dve.tensor_tensor(a3(oh[0]), be(eid[:, :]), bt(ei[:, 0, :]), ALU.is_equal))
                    dve.scalar_tensor_tensor(out=a3(sk), in0=a3(oh[0]), scalar=-3e38, in1=a3(sk), op0=ALU.mult,
                                             op1=ALU.add).then_inc(side, 1)
                    dve.wait_ge(side, 3)
                else:
                    dve.tensor_tensor(a3(oh[1]), be(eid[:, :]), bt(ei[:, 1, :]), ALU.is_equal).then_inc(side, 1)
                    dve.wait_ge(side, 4)
                    step(dve.tensor_tensor(a3(A), a3(oh[0]), a3(oh[1]), ALU.add))
            for k in range(2):
                dve.tensor_tensor(a3(tmp if k else up), a3(oh[k]), a3(sc), ALU.mult).then_inc(side, 1)
                dve.wait_ge(side, 5 + 2 * k)
                dve.tensor_reduce(w[:, k, :], a3(tmp if k else up), X, ALU.add).then_inc(side, 1)
            dve.wait_ge(side, 8)
            step(dve.tensor_tensor(den[:, :], w[:, 0, :], w[:, 1, :], ALU.add))
            step(dve.reciprocal(den[:, :], den[:, :]))
            dve.wait_ge(count_psum, 1)
            step(dve.tensor_copy(a3(pos), ps[0][0:TT, 0:NT * E].rearrange("p (t e) -> p t e", e=E)))
            for k in range(2):
                dve.tensor_tensor(a3(tmp if k else up), a3(oh[k]), a3(pos), ALU.mult).then_inc(side, 1)
                dve.wait_ge(side, 9 + 2 * k)
                dve.tensor_reduce(ps_[:, k, :], a3(tmp if k else up), X, ALU.add).then_inc(side, 1)
            dve.wait_ge(side, 12)
            step(dve.tensor_scalar(a3(valid), a3(ps_), float(CAP), None, ALU.is_lt))
            step(dve.tensor_scalar(a3(base), a3(ei), NOE, float(CAP), ALU.add, ALU.mult))
            step(dve.tensor_tensor(a3(gidx), a3(ps_), a3(valid), ALU.mult))
            step(dve.tensor_tensor(a3(sidx), a3(base), a3(ps_), ALU.add))
            dve.tensor_tensor(a3(gidx), a3(gidx), a3(base), ALU.add).then_inc(side, 1)
            dve.tensor_tensor(a3(sidx), a3(sidx), a3(trash), ALU.subtract).then_inc(side, 1)
            dve.wait_ge(side, 14)
            step(dve.tensor_tensor(a3(sidx), a3(sidx), a3(valid), ALU.mult))
            step(dve.tensor_tensor(a3(sidx), a3(sidx), a3(trash), ALU.add))
            dve.tensor_copy(gu[:, :], gidx[:, :, :].rearrange("p k t -> p (k t)")).then_inc(side, 1)
            step(dve.tensor_copy(su[:, :], sidx[:, :, :].rearrange("p k t -> p (k t)")))
            dve.tensor_tensor(a3(w), a3(w), a3(valid), ALU.mult).then_inc(side, 1)
            dve.wait_ge(side, 16)
            dve.tensor_tensor(a3(w), a3(w), den[:, :].unsqueeze(1).broadcast_to([TT, 2, NT]), ALU.mult).then_inc(side, 1)

            n = 0
            for part in range(2):
                for half in range(2):
                    e_ = es[:, half * HALF:(half + 1) * HALF]
                    h_ = hs[:, part, half * HALF:(half + 1) * HALF]
                    dve.wait_ge(sh_exp, 2 * part + half + 1)
                    dve.tensor_scalar(e_, e_, 1.0, None, ALU.add).then_inc(side, 1)
                    dve.wait_ge(side, 18 + 2 * n)
                    dve.reciprocal(e_, e_).then_inc(side, 1)
                    dve.wait_ge(side, 19 + 2 * n)
                    dve.tensor_tensor(h_, ps[1 + half][:, 0:HALF], e_, ALU.mult).then_inc(sh_steps, 1)
                    dve.wait_ge(sh_steps, 2 * n + 1)
                    dve.tensor_tensor(h_, h_, ps[3 + half][:, 0:HALF], ALU.mult).then_inc(sh_steps, 1)
                    n += 1
            for t in range(NT):
                dve.wait_ge(sh_out, t + 1)
                dve.tensor_tensor(g.x[:, t, :], g.x[:, t, :], ps[5 + t % 2][0:TT, 0:D], ALU.add).then_inc(sh_added, 1)

            with dve.Fori(0, E // 2) as u:
                for k in range(2):
                    e, i = 2 * u + k, 1 - k
                    dve.wait_ge(xT_psum, e + 1)
                    dve.tensor_copy(xeT[i][:, :], ps[4 * k][:, 0:2 * P]).then_inc(xT_ready, 1)
                for k in range(2):
                    e, i = 2 * u + k, 1 - k
                    dve.wait_ge(e_exp, e + 1)
                    dve.tensor_scalar(ee[i][:, :], ee[i][:, :], 1.0, None, ALU.add).then_inc(e_steps, 1)
                    dve.wait_ge(e_steps, 3 * e + 1)
                    dve.reciprocal(ee[i][:, :], ee[i][:, :]).then_inc(e_steps, 1)
                    dve.wait_ge(e_steps, 3 * e + 2)
                    dve.wait_ge(y_psum, e)
                    dve.tensor_tensor(he[i][:, :], ps[4 * k + 1][:, 0:2 * P], ee[i][:, :], ALU.mult).then_inc(e_steps, 1)
                    dve.wait_ge(e_steps, 3 * e + 3)
                    dve.tensor_tensor(he[i][:, :], he[i][:, :], ps[4 * k + 2][:, 0:2 * P], ALU.mult).then_inc(h_ready, 1)
            for t in range(NT):
                for k in range(2):
                    n = k * NT + t
                    dve.wait_ge(gathered, 16 * 2 * NT)
                    if t or k:
                        dve.wait_ge(summed, 2 * t + k)
                    dve.scalar_tensor_tensor(out=g.x[:, t, :], in0=yg[:, n, :], scalar=w[:, k, t:t + 1],
                                             in1=g.x[:, t, :], op0=ALU.mult, op1=ALU.add).then_inc(summed, 1)


def phase_bitlinear(nc, g):
    with ExitStack() as ctx:
        sb = lambda n, s, d=F32: ctx.enter_context(nc.sbuf_tensor(f"b_{n}", s, d))
        N = lambda n: g.sem(f"b_{n}")
        wf = [sb("wg", [P, 2, FI]), sb("wu", [P, 2, FI]), sb("wd", [P, FT, D])]
        wq = [sb("wgq", [P, 2, FI], BF16), sb("wuq", [P, 2, FI], BF16), sb("wdq", [P, FT, D], BF16)]
        wabs, wm, wsc = sb("wabs", [P, 3]), sb("wm", [P, 3]), sb("wsc", [P, 3])
        ma, sx, sg, cc = sb("ma", [TT, NT]), sb("sx", [TT, NT]), sb("sg", [TT, NT]), sb("cc", [TT, NT])
        xq = sb("xq", [TT, NT, D])
        xqT = sb("xqT", [P, 2, T], BF16)
        th, hh, hm = sb("th", [TT, FI]), sb("hh", [TT, FI]), sb("hm", [TT, 4])
        hT = sb("hT", [P, FT, TT], BF16)
        pgu = [ctx.enter_context(nc.psum_tensor(f"b_pgu{i}", [P, 1024], F32)) for i in range(2)]
        pt = ctx.enter_context(nc.psum_tensor("b_pt", [P, 1024], F32))
        pd = ctx.enter_context(nc.psum_tensor("b_pd", [P, 512], F32))
        pw = ctx.enter_context(nc.psum_tensor("b_pw", [P, 512], F32))
        w_in, wd_zero, sums, w_steps, wsum_psum = N("w_in"), N("wd_zero"), N("sums"), N("w_steps"), N("wsum_psum")
        x_steps, xT_psum, xT_ready = N("x_steps"), N("xT_psum"), N("xT_ready")
        gu_psum, tanh_ready, h_steps, hT_psum, hT_ready, d_psum, added, stored = [
            N(n) for n in ("gu_psum", "tanh_ready", "h_steps", "hT_psum", "hT_ready", "d_psum", "added", "stored")]
        block = ctx.enter_context(nc.Block())
        h_sc = N("h_scaled")
        HS = 7
        FC = [(0, 512), (512, FI)]

        @block.sync
        def _(sp):
            sp.dma_start(wf[0][:, :, :], g.a["WgT"]).then_inc(w_in, 16)
            sp.dma_start(wf[1][:, :, :], g.a["WuT"]).then_inc(w_in, 16)
            sp.wait_ge(wd_zero, 1)
            sp.dma_start(wf[2][:, 0:FT - 1, :], g.a["WdT"][0:(FT - 1) * P, :].rearrange("(f p) d -> p f d", p=P))\
              .then_inc(w_in, 16)
            sp.dma_start(wf[2][0:LASTF, FT - 1, :], g.a["WdT"][(FT - 1) * P:FI, :]).then_inc(w_in, 16)
            o = g.out.rearrange("b q d -> (b q) d").rearrange("(t p) d -> p t d", p=TT)
            for half in range(2):
                sp.wait_ge(added, 4 * half + 4)
                sp.dma_start(o[:, 4 * half:4 * half + 4, :], g.x[:, 4 * half:4 * half + 4, :]).then_inc(stored, 16)
            sp.wait_ge(stored, 32)

        @block.gpsimd
        def _(pool):
            pool.memset(wf[2][:, FT - 1, :], 0.0).then_inc(wd_zero, 1)

        @block.tensor
        def _(pe):
            pe.wait_ge(sums, 3)
            pe.matmul(pw[:, 0:3], g.ones[:, :], wabs[:, :], start=True, stop=True).then_inc(wsum_psum, 1)
            pe.wait_ge(x_steps, 13)
            for n in range(4):
                k, half = n // 2, n % 2
                bank = [pt[:, 0:512], pt[:, 512:1024], pd[:, :], pw[:, :]][n]
                if n == 3:
                    pe.wait_ge(w_steps, 1)
                for t in range(4):
                    mm = pe.transpose(bank[:, t * TT:(t + 1) * TT], xq[:, 4 * half + t, k * P:(k + 1) * P],
                                      g.ident[0:TT, 0:TT])
                mm.then_inc(xT_psum, 1)

            def gate_up(t):
                for m in range(2):
                    for lo, hi in FC:
                        for k in range(2):
                            mm = pe.matmul(pgu[m][0:TT, lo:hi], xqT[:, k, bass.ds(t * TT, TT)], wq[m][:, k, lo:hi],
                                           start=(k == 0), stop=(k == 1))
                mm.then_inc(gu_psum, 1)

            def tile(t, last):
                if not last:
                    pe.wait_ge(h_steps, HS * t + 2)
                    gate_up(t + 1)
                pe.wait_ge(h_steps, HS * t + HS)
                for f in range(FT):
                    n = P if f < FT - 1 else LASTF
                    lo = f * TT if f < 4 else 512 + (f - 4) * TT
                    mm = pe.transpose(pt[0:n, lo:lo + TT], hh[:, f * P:f * P + n], g.ident[0:TT, 0:TT])
                mm.then_inc(hT_psum, 1)
                pe.wait_ge(hT_ready, 3 * t + 3)
                for f in range(FT):
                    n = P if f < FT - 1 else LASTF
                    mm = pe.matmul(pd[0:TT, 0:D], hT[0:n, f, :], wq[2][0:n, f, :], start=(f == 0), stop=(f == FT - 1))
                mm.then_inc(d_psum, 1)
            pe.wait_ge(w_steps, 12)
            pe.wait_ge(xT_ready, 4)
            gate_up(0)
            with pe.Fori(0, 3) as u:
                for i in range(2):
                    tile(2 * u + i, False)
            tile(NT - 2, False)
            tile(NT - 1, True)

        @block.scalar
        def _(act):
            with act.Fori(0, NT) as t:
                act.wait_ge(gu_psum, t + 1)
                act.wait_ge(x_steps, 15)
                act.activation(th[:, :], pgu[0][0:TT, 0:FI], ACT.Tanh, scale=sg[:, bass.ds(t, 1)]).then_inc(tanh_ready, 1)

        @block.vector
        def _(dve):
            count = float(FI * D)
            for m in range(3):
                dve.wait_ge(w_in, 64)
                dve.tensor_reduce(wabs[:, m:m + 1], wf[m][:, :, :], mybir.AxisListType.XY, ALU.add,
                                  apply_absolute_value=True).then_inc(sums, 1)
            dve.tensor_reduce(ma[:, :], g.xn[:, :, :], X, ALU.max, apply_absolute_value=True).then_inc(x_steps, 1)
            dve.wait_ge(x_steps, 1)
            dve.tensor_scalar(ma[:, :], ma[:, :], 1e-5, None, ALU.max).then_inc(x_steps, 1)
            dve.wait_ge(x_steps, 2)
            dve.reciprocal(sx[:, :], ma[:, :]).then_inc(x_steps, 1)
            dve.wait_ge(x_steps, 3)
            dve.tensor_scalar(sx[:, :], sx[:, :], 127.0, None, ALU.mult).then_inc(x_steps, 1)
            dve.wait_ge(x_steps, 4)
            for t in range(NT):
                ins = dve.tensor_scalar(xq[:, t, :], g.xn[:, t, :], sx[:, t:t + 1], 127.0, ALU.mult, ALU.min)
                ins.then_inc(x_steps, 1)
            dve.wait_ge(x_steps, 12)
            dve.tensor_scalar(xq[:, :, :], xq[:, :, :], -128.0, MAGIC, ALU.max, ALU.add).then_inc(sums, 1)
            dve.wait_ge(sums, 4)
            dve.tensor_scalar(xq[:, :, :], xq[:, :, :], MAGIC, None, ALU.subtract).then_inc(x_steps, 1)

            dve.wait_ge(wsum_psum, 1)
            dve.tensor_scalar(wm[:, :], pw[:, 0:3], 1.0 / count, 1e-5, ALU.mult, ALU.max).then_inc(w_steps, 1)
            dve.wait_ge(w_steps, 1)
            dve.reciprocal(wsc[:, :], wm[:, :]).then_inc(w_steps, 1)
            dve.wait_ge(w_steps, 2)
            for m in range(3):
                w = wf[m][:, :, :]
                dve.tensor_scalar(w, w, wsc[:, m:m + 1], 1.0, ALU.mult, ALU.min).then_inc(w_steps, 1)
                dve.wait_ge(w_steps, 3 * m + 3)
                dve.tensor_scalar(w, w, -1.0, MAGIC, ALU.max, ALU.add).then_inc(w_steps, 1)
                dve.wait_ge(w_steps, 3 * m + 4)
                dve.tensor_scalar(wq[m][:, :, :], w, MAGIC, None, ALU.subtract).then_inc(w_steps, 1)
            for n in range(4):
                k, half = n // 2, n % 2
                bank = [pt[:, 0:512], pt[:, 512:1024], pd[:, :], pw[:, :]][n]
                dve.wait_ge(xT_psum, n + 1)
                dve.tensor_copy(xqT[:, k, half * HALF:(half + 1) * HALF], bank[:, 0:HALF]).then_inc(xT_ready, 1)
            dve.wait_ge(x_steps, 13)
            dve.tensor_scalar(sg[:, :], ma[:, :], wm[0:TT, 0:1], 0.5 / 127.0, ALU.mult, ALU.mult).then_inc(x_steps, 1)
            dve.wait_ge(w_steps, 11)
            dve.wait_ge(x_steps, 14)
            dve.tensor_tensor(cc[:, :], sg[:, :], ma[:, :], ALU.mult).then_inc(x_steps, 1)
            dve.wait_ge(x_steps, 15)
            dve.tensor_scalar(cc[:, :], cc[:, :], wm[0:TT, 1:2], 1.0 / 127.0, ALU.mult, ALU.mult).then_inc(w_steps, 1)
            dve.wait_ge(w_steps, 12)

            with dve.Fori(0, NT) as t:
                c = cc[:, bass.ds(t, 1)]
                dve.wait_ge(tanh_ready, t + 1)
                dve.wait_ge(hT_psum, t)
                dve.scalar_tensor_tensor(out=hh[:, :], in0=th[:, :], scalar=1.0, in1=pgu[0][0:TT, 0:FI],
                                         op0=ALU.add, op1=ALU.mult).then_inc(h_steps, 1)
                dve.wait_ge(h_steps, HS * t + 1)
                dve.tensor_tensor(hh[:, :], hh[:, :], pgu[1][0:TT, 0:FI], ALU.mult).then_inc(h_steps, 1)
                dve.wait_ge(h_steps, HS * t + 2)
                dve.tensor_reduce(hm[:, 0:1], hh[:, :], X, ALU.max, apply_absolute_value=True).then_inc(h_steps, 1)
                dve.wait_ge(h_steps, HS * t + 3)
                dve.tensor_scalar(hm[:, 1:2], hm[:, 0:1], c, 1e-5, ALU.mult, ALU.max).then_inc(h_steps, 1)
                dve.wait_ge(h_steps, HS * t + 4)
                dve.reciprocal(hm[:, 2:3], hm[:, 1:2]).then_inc(h_steps, 1)
                dve.wait_ge(h_steps, HS * t + 5)
                dve.tensor_scalar(hm[:, 3:4], hm[:, 2:3], c, 127.0, ALU.mult, ALU.mult).then_inc(h_sc, 1)
                dve.wait_ge(h_sc, 3 * t + 1)
                dve.tensor_scalar(hh[:, :], hh[:, :], hm[:, 3:4], 127.0, ALU.mult, ALU.min).then_inc(h_sc, 1)
                dve.wait_ge(h_sc, 3 * t + 2)
                dve.tensor_scalar(hh[:, :], hh[:, :], -128.0, MAGIC, ALU.max, ALU.add).then_inc(h_sc, 1)
                dve.wait_ge(h_sc, 3 * t + 3)
                dve.tensor_scalar(hh[:, :], hh[:, :], MAGIC, None, ALU.subtract).then_inc(h_steps, 1)
                dve.tensor_scalar(hm[:, 2:3], hm[:, 1:2], wm[0:TT, 2:3], 1.0 / 127.0, ALU.mult, ALU.mult)\
                   .then_inc(h_steps, 1)
                dve.wait_ge(hT_psum, t + 1)
                dve.tensor_copy(hT[:, 0:4, :].rearrange("p f n -> p (f n)"), pt[:, 0:4 * TT]).then_inc(hT_ready, 1)
                dve.tensor_copy(hT[:, 4:6, :].rearrange("p f n -> p (f n)"), pt[:, 512:512 + 2 * TT]).then_inc(hT_ready, 1)
                dve.tensor_copy(hT[0:LASTF, 6, :], pt[0:LASTF, 512 + 2 * TT:512 + 3 * TT]).then_inc(hT_ready, 1)
                dve.wait_ge(d_psum, t + 1)
                dve.wait_ge(h_steps, HS * t + 7)
                dve.scalar_tensor_tensor(out=g.x[:, t, :], in0=pd[0:TT, 0:D], scalar=hm[:, 2:3], in1=g.x[:, t, :],
                                         op0=ALU.mult, op1=ALU.add).then_inc(added, 1)


def phase_setup(nc, g):
    loaded = g.sem("loaded")
    n = 0
    with nc.Block() as block:
        @block.sync
        def _(sp):
            items = [(g.x, g.a["x"]), (g.ident, g.a["ident"]), (g.ones, g.a["ones"]), (g.cen, g.a["cen"]), (g.blk, g.a["blk"]),
                     (g.hmask, g.a["hmask"]), (g.bk0row, g.a["bk0"]), (g.bkdrow, g.a["bkd"])]
            for dst, src in items:
                sp.dma_start(dst[tuple(slice(None) for _ in dst.shape)], src).then_inc(loaded, 16)
            sp.wait_ge(loaded, 16 * len(items))


def build(nc, a, out):
    with ExitStack() as ctx:
        sb = lambda n, s, d=F32: ctx.enter_context(nc.sbuf_tensor(n, s, d))
        g = Shared()
        g.a, g.out = a, out
        g.sem = nc.alloc_semaphore
        g.x, g.xn = sb("x", [TT, NT, D]), sb("xn", [TT, NT, D])
        g.xnT = sb("xnT", [P, 2, T])
        g.rk = sb("rk", [P, B, NK, 2 * H])
        g.rkd = sb("rkd", [DCA, B, H])
        g.ident, g.ones = sb("ident", [P, P]), sb("ones", [P, P])
        g.cen, g.blk, g.hmask = sb("cen", [P, P]), sb("blk", [P, P]), sb("hmask", [P, 8])
        g.bk0row, g.bkdrow = sb("bk0row", [1, D]), sb("bkdrow", [1, D])
        g.qdram = [nc.dram_tensor(f"qdram{l}", [B, P, HQ], F32).ap() for l in range(3)]
        g.odram = [nc.dram_tensor(f"odram{l}", [B, P, HQ], F32).ap() for l in range(3)]
        g.bdram = nc.dram_tensor("bdram", [B, 3, HQ], BF16).ap()
        g.xbuf = nc.dram_tensor("xbuf", [E * CAP + 2 * T, D], F32).ap()
        g.ybuf = nc.dram_tensor("ybuf", [E * CAP, D], F32).ap()
        g.bdram_d = nc.dram_tensor("bdram_d", [B, HQ], F32).ap()
        todo = [lambda: phase_setup(nc, g), lambda: phase_norms(nc, g),
                lambda: phase_layernorm(nc, g, "l0"),
                lambda: phase_queries(nc, g, 0), lambda: phase_attention(nc, g, 0),
                lambda: phase_attention(nc, g, 2), lambda: phase_project(nc, g, 0),
                lambda: phase_layernorm(nc, g, "l1"), lambda: phase_moe(nc, g),
                lambda: phase_layernorm(nc, g, "l2"), lambda: phase_queries(nc, g, 1),
                lambda: phase_attention(nc, g, 1), lambda: phase_project(nc, g, 1),
                lambda: phase_layernorm(nc, g, "l3"), lambda: phase_bitlinear(nc, g)]
        for layer in (todo[:9], todo[9:]):
            with nc.cleanup_on_exit():
                for f in layer:
                    f()


def laid_out(i):
    rows = lambda w: w.reshape(2, P, -1).transpose(1, 0, 2)
    wkv = np.concatenate([i["L0_xattn_Wk"], i["L0_xattn_Wv"]], 1).reshape(C, H, 2, HD0)
    bkv = np.concatenate([i["L0_xattn_bk"], i["L0_xattn_bv"]]).reshape(H, 2, HD0)
    wk0, wv0 = wkv[:, :, 0].reshape(C, D), wkv[:, :, 1].reshape(C, D)
    bk0, bv0 = bkv[:, 0].reshape(D), bkv[:, 1].reshape(D)
    wkd, wvd = i["L0_xattn_Wkv_dca"][:, :D], i["L0_xattn_Wkv_dca"][:, D:]
    bkd, bvd = i["L0_xattn_bkv_dca"][:D], i["L0_xattn_bkv_dca"][D:]
    k0T = np.stack([np.concatenate([w, b[None]], 0).T.reshape(2, P, C + 1)
                    for w, b in ((wk0, bk0), (wkd, bkd))])
    rep = lambda w: np.tile(w, 8)
    bq = i["L0_xattn_bq"].reshape(2, P)
    cols = np.stack([np.stack([bq[s], rep(i["L0_xattn_qn_w"]), rep(i["L0_xattn_qn_b"]),
                               rep(i["L0_xattn_kn_w"]), rep(i["L0_xattn_kn_dca_w"])], 1) for s in range(2)])
    head = np.arange(P) // HD0
    same = (head[:, None] == head[None, :]).astype(np.float32)
    a = {
        "x": i["x"].reshape(NT, TT, D).transpose(1, 0, 2),
        "ctx": i["ctx_1024"], "ctxT": i["ctx_1024"].transpose(0, 2, 1),
        "ident": np.eye(P, dtype=np.float32), "ones": np.ones((P, P), np.float32),
        "cen": np.eye(P, dtype=np.float32) - same / np.float32(HD0), "blk": same,
        "hmask": (head[:, None] == np.arange(8)[None, :]).astype(np.float32),
        "low": np.triu(np.ones((TT, TT), np.float32), 1),
        "L0_Wk": wk0, "L0_Wkd": wkd, "bk0": bk0[None], "bkd": bkd[None],
        "k0T": k0T.transpose(2, 0, 1, 3), "cols0": cols.transpose(1, 0, 2),
        "L0_Wq": rows(i["L0_xattn_Wq"]),
        "v0T": np.stack([w.T.reshape(2, P, C) for w in (wv0, wvd)]).transpose(2, 0, 1, 3),
        "bv0": np.stack([bv0.reshape(2, P).T, bvd.reshape(2, P).T], 1), "L0_Wo": rows(i["L0_xattn_Wo"]),
        "bo0": i["L0_xattn_bo"][None],
        "L1_Wk": i["L1_xattn_Wk"],
        "L1_Wq": i["L1_xattn_Wq"].reshape(2, P, H, P).transpose(2, 1, 0, 3),
        "L1_WkT": i["L1_xattn_Wk"].T.reshape(H, P, C),
        "gq": i["L1_xattn_gq"][:, None], "gk": i["L1_xattn_gk"][:, None],
        "L1_WvT": i["L1_xattn_Wv"].T.reshape(H, P, C), "L1_Wo": i["L1_xattn_Wo"].reshape(H, P, D),
    }
    kxn = lambda w: w.transpose(0, 2, 1).reshape(E + 1, 2, P, FF).transpose(0, 2, 1, 3)
    a["W1T"] = kxn(np.concatenate([i["L0_ffn_W1"], i["L0_ffn_Ws1"][None]]))
    a["W3T"] = kxn(np.concatenate([i["L0_ffn_W3"], i["L0_ffn_Ws3"][None]]))
    a["W2T"] = np.concatenate([i["L0_ffn_W2"], i["L0_ffn_Ws2"][None]]).transpose(0, 2, 1)
    a["gw"] = rows(i["L0_ffn_gate_w"].T)
    a["gb"] = np.broadcast_to(i["L0_ffn_gate_b"], (TT, E))
    a["eid"] = np.broadcast_to(np.arange(E, dtype=np.float32) - 99, (TT, E))
    token = np.arange(NT)[None, None, :] * TT + np.arange(TT)[:, None, None]
    a["WgT"], a["WuT"] = rows(i["L1_ffn_w_gate"].T), rows(i["L1_ffn_w_up"].T)
    a["WdT"] = i["L1_ffn_w_down"].T
    a["trash"] = (E * CAP + 2 * token + np.arange(2)[None, :, None]).astype(np.float32)
    return a


_OUTS = [((B, NQ, D), "float32")]


def kernel(**inputs):
    import numpy as _np
    import concourse.bacc as _bacc
    from concourse import mybir as _mybir
    from concourse.bass_utils import run_bass_kernel_spmd as _run

    nc = _bacc.Bacc("TRN2", target_bir_lowering=False, num_devices=1)
    arrays, aps = {}, {}
    for name, arr in laid_out({k: _np.asarray(v) for k, v in inputs.items()}).items():
        arr = _np.ascontiguousarray(arr)
        arrays[f"in_{name}"] = arr
        aps[name] = nc.dram_tensor(f"in_{name}", arr.shape, _mybir.dt.from_np(arr.dtype), kind="ExternalInput").ap()
    out = nc.dram_tensor("out_0", _OUTS[0][0], F32, kind="ExternalOutput").ap()
    build(nc, aps, out)
    return _run(nc, [arrays], core_ids=[0]).results[0]["out_0"]
```

```python
from contextlib import ExitStack

import numpy as np

import concourse.bass as bass
from concourse import mybir

F32 = mybir.dt.float32
BF16 = mybir.dt.bfloat16
F32R = mybir.dt.float32r
U32 = mybir.dt.uint32
I32 = mybir.dt.int32
ALU = mybir.AluOpType
ACT = mybir.ActivationFunctionType
X = mybir.AxisListType.X

P = 128
B, NQ, D = 16, 56, 256
C, H = 128, 16
HQ = H * NQ
HALF = HQ // 2
SEQ, DCA = 1500, 16
NK = 12
TT = 2 * NQ
NT = B // 2
T = B * NQ
HD0, HD1 = D // H, 128
E, CAP, FF = 16, 128, 176
FI = 832
FT = 7
LASTF = FI - 6 * P
KR1 = SEQ - (NK - 1) * P
KR0 = KR1 - DCA
RING = 4
MAGIC = 12582912.0


class Shared:
    pass


def phase_norms(nc, g):
    with ExitStack() as ctx:
        sb = lambda n, s, d=F32: ctx.enter_context(nc.sbuf_tensor(n, s, d))
        WN = (H * HD1 + D)
        wall = sb("n_wall", [P, WN])
        wh, wl = sb("n_wh", [P, WN], F32R), sb("n_wl", [P, WN], F32R)
        yT = [sb(f"n_yT{i}", [P, SEQ]) for i in range(2)]
        yh, yl = [[sb(f"n_{n}{i}", [P, SEQ], F32R) for i in range(2)] for n in ("yh", "yl")]
        sq = sb("n_sq", [P, 3, 1024])
        km = sb("n_km", [P, H])
        bkm = sb("n_bkm", [1, H])
        bpart, bparts, ones3 = sb("n_bpart", [1, 3, D], BF16), sb("n_bparts", [3, D], BF16), sb("n_ones3", [3, P], BF16)
        slot = [ctx.enter_context(nc.psum_tensor(f"n_slot{i}", [P, 1024], F32)) for i in range(3)]
        W = [1024, 1024, 256]
        w_in, yT_in = g.sem("n_w_in"), [g.sem("n_yT_in0"), g.sem("n_yT_in1")]
        w_ready, cent, w_split = g.sem("n_w_ready"), g.sem("n_cent"), g.sem("n_w_split")
        b_steps, b_in, y_high, y_split = g.sem("n_b_steps"), g.sem("n_b_in"), g.sem("n_y_high"), g.sem("n_y_split")
        parts_used = g.sem("n_parts_used")
        prod, slot_free = g.sem("n_prod"), g.sem("n_slot_free")
        sq_free, scaled, rooted, inverted = g.sem("n_sq_free"), g.sem("n_scaled"), g.sem("n_rooted"), g.sem("n_inverted")
        block = ctx.enter_context(nc.Block())
        k0 = wall[:, 2048:2304].rearrange("p (h d) -> p h d", h=H)
        bk0 = g.bk0row[0:1, :].rearrange("p (h d) -> p h d", h=H)

        @block.sync
        def _(sp):
            sp.dma_start(wall[:, 0:2048], g.a["L1_Wk"]).then_inc(w_in, 16)
            sp.dma_start(wall[:, 2048:2304], g.a["L0_Wk"]).then_inc(w_in, 16)
            for i in range(2):
                sp.dma_start(yT[i][:, :], g.a["ctxT"][i]).then_inc(yT_in[i], 16)
            sp.wait_ge(b_steps, 6)
            for n in range(3):
                sp.dma_start(bparts[n:n + 1, :], bpart[0:1, n, :]).then_inc(b_in, 16)
            with sp.Fori(0, B // 2 - 1) as u:
                for i in range(2):
                    sp.wait_ge(y_split, 2 * u + i + 1)
                    sp.dma_start(yT[i][:, :], g.a["ctxT"][2 * u + 2 + i]).then_inc(yT_in[i], 16)
            sp.wait_ge(b_in, 48)

        @block.gpsimd
        def _(pool):
            pool.wait_ge(w_in, 32)
            pool.tensor_copy(wh[:, 0:2048], wall[:, 0:2048]).then_inc(w_split, 1)
            pool.sem_inc(parts_used, 2)
            with pool.Fori(0, B // 2) as u:
                for i in range(2):
                    pool.wait_ge(yT_in[i], 16 * u + 16)
                    pool.wait_ge(parts_used, 2 * u + i + 1)
                    pool.tensor_tensor(yh[i][:, :], yT[i][:, :], g.ones[:, 0:1].broadcast_to([P, SEQ]), ALU.mult)\
                        .then_inc(y_high, 1)
                    pool.wait_ge(y_high, 2 * u + i + 1)
                    pool.tensor_tensor(yl[i][:, :], yT[i][:, :], yh[i][:, :], ALU.subtract).then_inc(y_split, 1)

        @block.tensor
        def _(pe):
            pe.wait_ge(w_split, 4)
            pe.wait_ge(b_in, 48)
            with pe.Fori(0, B // 2) as u:
                for i in range(2):
                    pe.wait_ge(y_split, 2 * u + i + 1)
                    for j in range(NK):
                        n = P if j < NK - 1 else KR1
                        tile = (2 * u + i) * NK + j
                        high, low = yh[i][:, j * P:j * P + n], yl[i][:, j * P:j * P + n]
                        for s in range(3):
                            pe.wait_ge(slot_free, tile * 3 + s + 1)
                            for c in range(0, W[s], 512):
                                w = min(512, W[s] - c)
                                cols = slice(1024 * s + c, 1024 * s + c + w)
                                dst = slot[s][0:n, c:c + w]
                                pe.matmul(dst, high, wh[:, cols], start=True, stop=False)
                                pe.matmul(dst, high, wl[:, cols], start=False, stop=False)
                                mm = pe.matmul(dst, low, wh[:, cols], start=False, stop=(s < 2))
                                if s == 2 and j == NK - 1:
                                    mm.then_inc(parts_used, 1)
                            if s == 2:
                                mm = pe.matmul(slot[s][0:n, 0:256], ones3[:, 0:n], bparts[:, :], start=False, stop=True)
                            mm.then_inc(prod, 1)

        @block.scalar
        def _(act):
            def roots(b):
                act.wait_ge(scaled, 2 * (b + 2))
                act.activation(g.rk_all[:, b + 1, :, :], g.rk_all[:, b + 1, :, :], ACT.Sqrt).then_inc(rooted, 1)
            act.sem_inc(slot_free, 3)
            with act.Fori(0, B // 2) as u:
                for i in range(2):
                    b = 2 * u + i
                    for j in range(NK):
                        if j == 4:
                            roots(b - 1)
                        n = P if j < NK - 1 else KR1
                        tile = b * NK + j
                        for s in range(3):
                            act.wait_ge(prod, tile * 3 + s + 1)
                            act.wait_ge(sq_free, tile * 3 + s + 1)
                            act.activation(sq[0:n, s, 0:W[s]], slot[s][0:n, 0:W[s]], ACT.Square)\
                               .then_inc(slot_free, 1)
            roots(B - 1)

        @block.vector
        def _(dve):
            dve.wait_ge(w_in, 32)
            heads_of = [(km, k0, P), (bkm, bk0, 1)]
            for mean, w, _ in heads_of:
                dve.tensor_reduce(mean[:, :], w, X, ALU.add).then_inc(cent, 1)
            dve.memset(g.rk_all[:, :, :, :], 1.0).then_inc(cent, 1)
            dve.wait_ge(cent, 3)
            for mean, w, n in heads_of:
                dve.scalar_tensor_tensor(out=w, in0=mean[:, :, None].broadcast_to([n, H, HD0]),
                                         scalar=-1.0 / HD0, in1=w, op0=ALU.mult, op1=ALU.add).then_inc(w_ready, 1)
            dve.wait_ge(w_ready, 2)
            dve.wait_ge(w_split, 1)
            dve.tensor_tensor(wl[:, 0:2048], wall[:, 0:2048], wh[:, 0:2048], ALU.subtract).then_inc(w_split, 1)
            dve.tensor_copy(wh[:, 2048:2304], wall[:, 2048:2304]).then_inc(w_split, 1)
            dve.memset(ones3[:, :], 1.0).then_inc(b_steps, 1)
            for n in range(3):
                dve.tensor_copy(bpart[:, n, :], g.bk0row[:, :]).then_inc(b_steps, 1)
                dve.wait_ge(b_steps, 2 + 2 * n)
                if n < 2:
                    dve.tensor_tensor(g.bk0row[:, :], g.bk0row[:, :], bpart[:, n, :], ALU.subtract).then_inc(b_steps, 1)
                    dve.wait_ge(b_steps, 3 + 2 * n)
            dve.wait_ge(w_split, 3)
            dve.tensor_tensor(wl[:, 2048:2304], wall[:, 2048:2304], wh[:, 2048:2304], ALU.subtract).then_inc(w_split, 1)
            def scale(b):
                dve.wait_ge(sq_free, (b + 1) * NK * 3 + 3)
                r1, r0 = g.rk_all[:, b + 1, :, 0:H], g.rk_all[:, b + 1, :, H:2 * H]
                dve.tensor_scalar(r1, r1, 1.0 / HD1, 1e-5, ALU.mult, ALU.add).then_inc(scaled, 1)
                dve.tensor_scalar(r0, r0, 1.0 / HD0, 1e-6, ALU.mult, ALU.add).then_inc(scaled, 1)

            def invert(b):
                dve.reciprocal(g.rk_all[:, b + 1, :, :], g.rk_all[:, b + 1, :, :]).then_inc(inverted, 1)
            dve.sem_inc(sq_free, 3)
            with dve.Fori(0, B // 2) as u:
                for i in range(2):
                    b = 2 * u + i
                    for j in range(NK):
                        if j == 1:
                            scale(b - 1)
                        if j == 7:
                            dve.wait_ge(rooted, b + 1)
                        n = P if j < NK - 1 else KR1
                        tile = b * NK + j
                        for s in range(3):
                            dve.wait_ge(slot_free, tile * 3 + s + 1 + 3)
                            heads = 8 if s < 2 else H
                            dve.tensor_reduce(
                                g.rk[0:n, b, j, 8 * s:8 * s + heads],
                                sq[0:n, s, 0:W[s]].rearrange("p (h d) -> p h d", h=heads),
                                X, ALU.add).then_inc(sq_free, 1)
                        if j == 7:
                            invert(b - 1)
            scale(B - 1)
            dve.wait_ge(rooted, B + 1)
            invert(B - 1)


def phase_layernorm(nc, g, name):
    with ExitStack() as ctx:
        sb = lambda n, s, d=F32: ctx.enter_context(nc.sbuf_tensor(f"{name}_{n}", s, d))
        st, mv, rs = sb("st", [TT, NT, 6]), sb("mv", [TT, NT, 2]), sb("rs", [TT, NT])
        ps = [ctx.enter_context(nc.psum_tensor(f"{name}_ps{i}", [P, 512], F32)) for i in range(4)]
        stats, std, xn_ready = g.sem(f"{name}_stats"), g.sem(f"{name}_std"), g.sem(f"{name}_xn_ready")
        tr, copied = g.sem(f"{name}_tr"), g.sem(f"{name}_copied")
        block = ctx.enter_context(nc.Block())

        @block.vector
        def _(dve):
            for t in range(NT):
                dve.bn_stats(st[:, t, :], g.x[:, t, :]).then_inc(stats, 1)
            dve.wait_ge(stats, NT)
            for t in range(NT):
                dve.bn_aggr(mv[:, t, :], st[:, t, :]).then_inc(stats, 1)
            dve.wait_ge(stats, 2 * NT)
            dve.tensor_scalar(rs[:, :], mv[:, :, 1], 1e-5, None, ALU.add).then_inc(std, 1)
            dve.wait_ge(std, 2)
            dve.reciprocal(rs[:, :], rs[:, :]).then_inc(std, 1)
            dve.wait_ge(std, 3)
            for t in range(NT):
                dve.tensor_scalar(g.xn[:, t, :], g.x[:, t, :], mv[:, t, 0:1], rs[:, t:t + 1],
                                  ALU.subtract, ALU.mult).then_inc(xn_ready, 1)
            for n in range(0, 4, 2):
                dve.wait_ge(tr, n + 1)
                dve.tensor_copy(g.xnT[:, n // 2, 0:HALF], ps[n][:, 0:HALF]).then_inc(copied, 1)

        @block.scalar
        def _(act):
            act.wait_ge(std, 1)
            act.activation(rs[:, :], rs[:, :], ACT.Sqrt).then_inc(std, 1)
            for n in range(1, 4, 2):
                act.wait_ge(tr, n + 1)
                act.activation(g.xnT[:, n // 2, HALF:T], ps[n][:, 0:HALF], ACT.Copy).then_inc(copied, 1)

        @block.tensor
        def _(pe):
            for n in range(4):
                k, half = n // 2, n % 2
                pe.wait_ge(xn_ready, 4 * half + 4)
                for t in range(4):
                    mm = pe.transpose(ps[n][:, t * TT:(t + 1) * TT],
                                      g.xn[:, 4 * half + t, k * P:(k + 1) * P], g.ident[0:TT, 0:TT])
                mm.then_inc(tr, 1)


def phase_queries0(nc, g):
    with ExitStack() as ctx:
        sb = lambda n, s, d=F32: ctx.enter_context(nc.sbuf_tensor(f"q0_{n}", s, d))
        S = lambda n: g.sem(f"q0_{n}")
        wk_in, wkc = sb("wk_in", [P, 2, C + 1]), sb("wkc", [P, 2, C + 1])
        wqa = sb("wqa", [P, 2, D])
        mkw = sb("mkw", [P, 2, 8])
        lb = sb("lb", [P, 2, H])
        lhk = [sb(f"lhk{i}", [P, C]) for i in range(2)]
        eps = sb("eps", [P, 1])
        qa, qc, sq, rq = [[sb(f"{n}{i}", [P, T]) for i in range(2)] for n in ("qa", "qc", "sq", "rq")]
        qall = sb("qall", [P, B, HQ])
        bt = sb("bt", [H, T])
        parts = sb("parts", [H, 3, T], BF16)
        ps = [ctx.enter_context(nc.psum_tensor(f"q0_ps{i}", [P, 2, 512], F32)) for i in range(4)]
        in_done, wk_psum, wk_ready = S("in_done"), S("wk_psum"), S("wk_ready")
        q_psum, q_ready, c_psum, c_ready, sq_ready = S("q_psum"), S("q_ready"), S("c_psum"), S("c_ready"), S("sq_ready")
        sum_psum, rooted, inverted, qn_ready, qs_ready = S("sum_psum"), S("rooted"), S("inverted"), S("qn_ready"), S("qs_ready")
        mask_ready, lb_ready, b_psum, b_steps = S("mask_ready"), S("lb_ready"), S("b_psum"), S("b_steps")
        lh_ready, hq_psum, copied, stored = S("lh_ready"), S("hq_psum"), S("copied"), S("stored")
        block = ctx.enter_context(nc.Block())
        v2 = lambda t: t[:, :].rearrange("p (a n) -> p a n", a=2)

        @block.sync
        def _(sp):
            sp.dma_start(wqa[:, :, :], g.a["L0_Wq"]).then_inc(in_done, 16)
            sp.dma_start(g.cols[:, :, :], g.a["cols0"]).then_inc(in_done, 16)
            sp.dma_start(wk_in[:, :, :], g.a["k0T"]).then_inc(in_done, 16)
            sp.wait_ge(b_steps, 7)
            for n in range(3):
                sp.dma_start(g.bdram[:, n, :].rearrange("b (h q) -> h b q", h=H),
                             parts[:, n, :].rearrange("h (b q) -> h b q", b=B)).then_inc(stored, 16)
            for half in range(2):
                sp.wait_ge(copied, 8 * half + 8 + 1)
                sp.dma_start(g.qdram[0][:, :, half * HALF:(half + 1) * HALF].rearrange("b c n -> c b n"),
                             qall[:, :, half * HALF:(half + 1) * HALF]).then_inc(stored, 16)
            sp.wait_ge(stored, 16 * 5)

        @block.tensor
        def _(pe):
            def both(dst, lhs, rhs):
                for n in range(2):
                    mm = pe.matmul(dst[:, n, 0:HALF], lhs, rhs[:, n * HALF:(n + 1) * HALF], start=True, stop=True)
                return mm
            pe.wait_ge(in_done, 48)
            for half in range(2):
                for n in range(2):
                    for k in range(2):
                        mm = pe.matmul(ps[half][:, n, 0:HALF], wqa[:, k, half * P:(half + 1) * P],
                                       g.xnT[:, k, n * HALF:(n + 1) * HALF], start=(k == 0), stop=(k == 1))
                mm.then_inc(q_psum, 1)
            for half in range(2):
                mm = pe.matmul(ps[2][:, 0, half * 256:half * 256 + C + 1], g.cen[:, :], wk_in[:, half, :],
                               start=True, stop=True)
            mm.then_inc(wk_psum, 1)
            pe.wait_ge(wk_ready, 1)
            for half in range(2):
                pe.wait_ge(q_ready, half + 1)
                both(ps[2 + half], g.cen[:, :], qa[half]).then_inc(c_psum, 1)
            for half in range(2):
                pe.wait_ge(sq_ready, half + 1)
                both(ps[half], g.blk[:, :], sq[half]).then_inc(sum_psum, 1)
            pe.wait_ge(qs_ready, 2)
            pe.wait_ge(lb_ready, 1)
            pe.wait_ge(rooted, 2)
            for n in range(2):
                for half in range(2):
                    mm = pe.matmul(ps[0][0:H, n, 0:HALF], lb[:, half, :], g.qs[half][:, n * HALF:(n + 1) * HALF],
                                   start=(half == 0), stop=(half == 1))
            mm.then_inc(b_psum, 1)
            for half in range(2):
                with pe.Fori(0, 4) as u:
                    for i in range(2):
                        h = 8 * half + 2 * u + i
                        pe.wait_ge(lh_ready, h + 1)
                        pe.wait_ge(copied, h)
                        both(ps[2 + i], lhk[i][:, :], g.qs[half]).then_inc(hq_psum, 1)

        @block.scalar
        def _(act):
            for half in range(2):
                act.wait_ge(c_psum, half + 1)
                act.activation(v2(sq[half]), ps[2 + half][:, :, 0:HALF], ACT.Square).then_inc(sq_ready, 1)
            act.wait_ge(mask_ready, 2)
            for half in range(2):
                act.wait_ge(sum_psum, half + 1)
                act.activation(v2(rq[half]), ps[half][:, :, 0:HALF], ACT.Sqrt, scale=1.0 / HD0, bias=eps[:, 0:1])\
                   .then_inc(rooted, 1)
            act.wait_ge(c_ready, 2)
            act.sem_inc(copied, 1)
            with act.Fori(0, 8) as u:
                for i in range(2):
                    h = 2 * u + i
                    act.wait_ge(hq_psum, h + 1)
                    for n in range(2):
                        ins = act.activation(qall[:, 8 * n:8 * n + 8, bass.ds(h * NQ, NQ)],
                                             ps[2 + i][:, n, 0:HALF].rearrange("p (b q) -> p b q", q=NQ), ACT.Copy)
                    ins.then_inc(copied, 1)

        @block.vector
        def _(dve):
            dve.memset(eps[:, :], 1e-6).then_inc(mask_ready, 1)
            dve.wait_ge(in_done, 48)
            for half in range(2):
                ins = dve.tensor_scalar(mkw[:, half, :], g.hmask[:, :], g.cols[:, half, 3:4], HD0 ** -0.5,
                                        ALU.mult, ALU.mult)
            ins.then_inc(mask_ready, 1)
            dve.memset(lb[:, :, :], 0.0).then_inc(b_steps, 1)
            for half in range(2):
                dve.wait_ge(q_psum, half + 1)
                dve.tensor_scalar(v2(qa[half]), ps[half][:, :, 0:HALF], g.cols[:, half, 0:1], None, ALU.add)\
                   .then_inc(q_ready, 1)
                if half == 0:
                    dve.wait_ge(wk_psum, 1)
                    dve.tensor_copy(wkc[:, :, :], ps[2][:, 0, :].rearrange("p (a n) -> p a n", a=2)[:, :, 0:C + 1])\
                       .then_inc(wk_ready, 1)
            for half in range(2):
                dve.wait_ge(sq_ready, half + 1)
                dve.tensor_copy(v2(qc[half]), ps[2 + half][:, :, 0:HALF]).then_inc(c_ready, 1)
            dve.wait_ge(wk_ready, 1)
            dve.wait_ge(mask_ready, 2)
            dve.wait_ge(b_steps, 1)
            for half in range(2):
                ins = dve.tensor_scalar(lb[:, half, 8 * half:8 * half + 8], mkw[:, half, :],
                                        wkc[:, half, C:C + 1], None, ALU.mult)
            ins.then_inc(lb_ready, 1)
            for half in range(2):
                dve.wait_ge(rooted, half + 1)
                dve.reciprocal(rq[half][:, :], rq[half][:, :]).then_inc(inverted, 1)
                dve.wait_ge(inverted, half + 1)
                dve.wait_ge(c_ready, half + 1)
                dve.tensor_tensor(qc[half][:, :], qc[half][:, :], rq[half][:, :], ALU.mult).then_inc(qn_ready, 1)
                dve.wait_ge(qn_ready, half + 1)
                dve.tensor_scalar(g.qs[half][:, :], qc[half][:, :], g.cols[:, half, 1:2], g.cols[:, half, 2:3],
                                  ALU.mult, ALU.add).then_inc(qs_ready, 1)
            def weights(half, u, i):
                dve.tensor_scalar(lhk[i][:, :], wkc[:, half, 0:C], mkw[:, half, bass.ds(2 * u + i, 1)],
                                  None, ALU.mult).then_inc(lh_ready, 1)
            dve.wait_ge(b_psum, 1)
            dve.tensor_copy(bt[:, :].rearrange("p (a n) -> p a n", a=2), ps[0][0:H, :, 0:HALF]).then_inc(b_steps, 1)
            dve.wait_ge(b_steps, 2)
            for n in range(3):
                dve.tensor_copy(parts[:, n, :], bt[:, :]).then_inc(b_steps, 1)
                if n < 2:
                    dve.wait_ge(b_steps, 3 + 2 * n)
                    dve.tensor_tensor(bt[:, :], bt[:, :], parts[:, n, :], ALU.subtract).then_inc(b_steps, 1)
                    dve.wait_ge(b_steps, 4 + 2 * n)
            for half in range(2):
                with dve.Fori(0, 4) as u:
                    for i in range(2):
                        h = 8 * half + 2 * u + i
                        dve.wait_ge(copied, h)
                        weights(half, u, i)


def phase_dca(nc, g):
    NKD = B * DCA
    GB = 4
    with ExitStack() as ctx:
        sb = lambda n, s, d=F32: ctx.enter_context(nc.sbuf_tensor(f"d_{n}", s, d))
        S = lambda n: g.sem(f"d_{n}")
        ydT, wkd, wvd = sb("ydT", [P, NKD]), sb("wkd", [P, D]), sb("wvd", [P, D])
        yrep = sb("yrep", [P, B, 8, DCA])
        kk, ksq = sb("kk", [P, 2, D]), sb("ksq", [P, 2, D])
        kmean, krs = sb("kmean", [P, 2 * H]), sb("krs", [P, 2 * H])
        kT = sb("kT", [P, 2, NKD])
        km = sb("km", [P, 2, B, 8, DCA])
        vm = sb("vm", [P, B, D])
        eps = sb("eps", [P, 1])
        pr = [sb(f"pr{i}", [NQ, GB, H, DCA]) for i in range(2)]
        smax, den = [[sb(f"{n}{i}", [NQ, GB * H]) for i in range(2)] for n in ("smax", "den")]
        pT = [sb(f"pT{i}", [P, 2, GB * NQ]) for i in range(2)]
        oT = sb("oT", [P, 2, T])
        sc = [ctx.enter_context(nc.psum_tensor(f"d_sc{i}", [P, 1024], F32)) for i in range(2)]
        pt, pv = ctx.enter_context(nc.psum_tensor("d_pt", [P, 512], F32)), ctx.enter_context(nc.psum_tensor("d_pv", [P, 512], F32))
        po = [ctx.enter_context(nc.psum_tensor(f"d_po{i}", [P, 512], F32)) for i in range(2)]
        y_in, w_in, eps_set, rep_ready = S("y_in"), S("w_in"), S("eps_set"), S("rep_ready")
        k_psum, k_steps, v_var, rooted, kT_psum, kT_ready, km_ready = [
            S(n) for n in ("k_psum", "k_steps", "v_var", "rooted", "kT_psum", "kT_ready", "km_ready")]
        v_psum, v_ready, s_psum, s_max, s_ready, p_ready, p_sum, p_inv, pn_ready = [
            S(n) for n in ("v_psum", "v_ready", "s_psum", "s_max", "s_ready", "p_ready", "p_sum", "p_inv", "pn_ready")]
        pT_psum, pT_ready, o_psum, o_ready, stored = [
            S(n) for n in ("pT_psum", "pT_ready", "o_psum", "o_ready", "stored")]
        block = ctx.enter_context(nc.Block())
        G = B // GB
        f = lambda t: t[:, :, :].rearrange("p a n -> p (a n)")

        @block.sync
        def _(sp):
            sp.dma_start(ydT[:, :], g.a["ydT"]).then_inc(y_in, 16)
            sp.dma_start(wkd[:, :], g.a["L0_Wkd"]).then_inc(w_in, 16)
            sp.dma_start(wvd[:, :], g.a["L0_Wvd"]).then_inc(w_in, 16)
            sp.wait_ge(o_ready, G)
            sp.dma_start(g.ddram, oT[:, :, :]).then_inc(stored, 16)
            sp.wait_ge(stored, 16)

        @block.tensor
        def _(pe):
            pe.wait_ge(y_in, 16)
            pe.wait_ge(w_in, 32)
            for t in range(2):
                pe.matmul(pt[:, t * D:(t + 1) * D], ydT[:, t * P:(t + 1) * P], wkd[:, :], start=True, stop=False)
                mm = pe.matmul(pt[:, t * D:(t + 1) * D], g.ones[0:1, :], g.bkdrow[0:1, :], start=False, stop=True)
            mm.then_inc(k_psum, 1)
            pe.wait_ge(rep_ready, 1)

            def values(n):
                pe.wait_ge(v_ready, n)
                for k in range(2):
                    mm = pe.matmul(pv[:, k * D:(k + 1) * D],
                                   yrep[:, 2 * n + k, :, :].rearrange("p h k -> p (h k)"), wvd[:, :],
                                   start=True, stop=True)
                mm.then_inc(v_psum, 1)
            values(0)
            pe.wait_ge(k_steps, 5)
            for t in range(2):
                for half in range(2):
                    mm = pe.transpose(pt[:, half * NKD + t * P:half * NKD + (t + 1) * P],
                                      kk[:, t, half * P:(half + 1) * P], g.ident[:, :])
            mm.then_inc(kT_psum, 1)
            pe.wait_ge(km_ready, 2)

            def scores(n):
                if n >= 2:
                    pe.wait_ge(s_ready, n - 1)
                for k in range(GB):
                    b = GB * n + k
                    for half in range(2):
                        mm = pe.matmul(sc[n % 2][0:NQ, (2 * k + half) * P:(2 * k + half + 1) * P],
                                       g.qs[half][:, b * NQ:(b + 1) * NQ],
                                       km[:, half, b, :, :].rearrange("p h k -> p (h k)"), start=True, stop=True)
                mm.then_inc(s_psum, 1)
            scores(0)
            for n in range(G):
                if n + 1 < G:
                    scores(n + 1)
                values(2 * n + 1)
                pe.wait_ge(pn_ready, n + 1)
                pe.wait_ge(pT_ready, n)
                for half in range(2):
                    for k in range(GB):
                        mm = pe.transpose(pt[:, (half * GB + k) * NQ:(half * GB + k + 1) * NQ],
                                          pr[n % 2][:, k, half * 8:(half + 1) * 8, :].rearrange("p h k -> p (h k)"),
                                          g.ident[0:NQ, 0:NQ])
                mm.then_inc(pT_psum, 1)
                if n + 1 < G:
                    values(2 * n + 2)
                pe.wait_ge(pT_ready, n + 1)
                pe.wait_ge(v_ready, 2 * n + 2)
                if n >= 2:
                    pe.wait_ge(o_ready, n - 1)
                for half in range(2):
                    for k in range(GB):
                        mm = pe.matmul(po[n % 2][:, (half * GB + k) * NQ:(half * GB + k + 1) * NQ],
                                       vm[:, GB * n + k, half * P:(half + 1) * P],
                                       pT[n % 2][:, half, k * NQ:(k + 1) * NQ], start=True, stop=True)
                mm.then_inc(o_psum, 1)

        @block.scalar
        def _(act):
            act.wait_ge(eps_set, 1)
            act.wait_ge(v_var, 1)
            act.activation(krs[:, :], krs[:, :], ACT.Sqrt, scale=1.0 / HD0, bias=eps[:, 0:1]).then_inc(rooted, 1)
            for n in range(G):
                act.wait_ge(s_ready, n + 1)
                p2 = pr[n % 2][:, :, :, :].rearrange("p b h k -> p (b h k)")
                act.activation(p2, p2, ACT.Exp).then_inc(p_ready, 1)
                act.wait_ge(pT_psum, n + 1)
                if n >= 2:
                    act.wait_ge(o_psum, n - 1)
                act.activation(f(pT[n % 2]), pt[:, 0:2 * GB * NQ], ACT.Copy).then_inc(pT_ready, 1)
                act.wait_ge(o_psum, n + 1)
                act.activation(oT[:, :, n * GB * NQ:(n + 1) * GB * NQ],
                               po[n % 2][:, 0:2 * GB * NQ].rearrange("p (a n) -> p a n", a=2), ACT.Copy).then_inc(o_ready, 1)

        @block.gpsimd
        def _(pool):
            pool.memset(eps[:, :], 1e-6).then_inc(eps_set, 1)
            pool.wait_ge(y_in, 16)
            pool.tensor_copy(yrep[:, :, :, :], ydT[:, :].rearrange("p (b k) -> p b k", b=B).unsqueeze(2)
                             .broadcast_to([P, B, 8, DCA])).then_inc(rep_ready, 1)

        @block.vector
        def _(dve):
            kh = kk[:, :, :].rearrange("p t (h d) -> p (t h) d", d=HD0)
            sh = ksq[:, :, :].rearrange("p t (h d) -> p (t h) d", d=HD0)
            wide = lambda col: col.unsqueeze(2).broadcast_to([P, 2 * H, HD0])
            dve.wait_ge(k_psum, 1)
            dve.tensor_reduce(kmean[:, :], pt[:, :].rearrange("p (h d) -> p h d", d=HD0), X, ALU.add).then_inc(k_steps, 1)
            dve.wait_ge(k_steps, 1)
            dve.scalar_tensor_tensor(out=kh, in0=wide(kmean[:, :]), scalar=-1.0 / HD0,
                                     in1=pt[:, :].rearrange("p (h d) -> p h d", d=HD0), op0=ALU.mult, op1=ALU.add)\
               .then_inc(k_steps, 1)
            dve.wait_ge(k_steps, 2)
            dve.tensor_tensor(sh, kh, kh, ALU.mult).then_inc(k_steps, 1)
            dve.wait_ge(k_steps, 3)
            dve.tensor_reduce(krs[:, :], sh, X, ALU.add).then_inc(v_var, 1)
            dve.wait_ge(rooted, 1)
            dve.reciprocal(krs[:, :], krs[:, :]).then_inc(k_steps, 1)
            dve.wait_ge(k_steps, 4)
            dve.tensor_tensor(kh, kh, wide(krs[:, :]), ALU.mult).then_inc(k_steps, 1)

            def masked_values(n):
                dve.wait_ge(v_psum, n + 1)
                dve.tensor_tensor(vm[:, 2 * n:2 * n + 2, :].rearrange("p b (a c) -> p (b a) c", a=2),
                                  pv[:, :].rearrange("p (a c) -> p a c", a=4),
                                  g.blk[:, :].unsqueeze(1).broadcast_to([P, 4, P]), ALU.mult).then_inc(v_ready, 1)
            masked_values(0)
            dve.wait_ge(kT_psum, 1)
            for half in range(2):
                dve.tensor_scalar(kT[:, half, :], pt[:, half * NKD:(half + 1) * NKD], g.cols[:, half, 4:5], HD0 ** -0.5,
                                  ALU.mult, ALU.mult).then_inc(kT_ready, 1)
            dve.wait_ge(kT_ready, 2)
            for half in range(2):
                dve.tensor_tensor(km[:, half, :, :, :],
                                  kT[:, half, :].rearrange("p (b k) -> p b k", b=B).unsqueeze(2).broadcast_to([P, B, 8, DCA]),
                                  g.hmask[:, :].unsqueeze(1).unsqueeze(3).broadcast_to([P, B, 8, DCA]), ALU.mult)\
                   .then_inc(km_ready, 1)
            p3 = lambda n: pr[n % 2][:, :, :, :].rearrange("p b h k -> p (b h) k")
            along = lambda col: col.unsqueeze(2).broadcast_to([NQ, GB * H, DCA])

            def shift(n):
                s3 = sc[n % 2][0:NQ, :].rearrange("p (m k) -> p m k", k=DCA)
                dve.wait_ge(s_psum, n + 1)
                dve.tensor_reduce(smax[n % 2][:, :], s3, X, ALU.max).then_inc(s_max, 1)
                dve.wait_ge(s_max, n + 1)
                if n >= 2:
                    dve.wait_ge(pT_psum, n - 1)
                dve.tensor_tensor(p3(n), s3, along(smax[n % 2][:, :]), ALU.subtract).then_inc(s_ready, 1)
            shift(0)
            for n in range(G):
                masked_values(2 * n + 1)
                if n + 1 < G:
                    shift(n + 1)
                dve.wait_ge(p_ready, n + 1)
                dve.tensor_reduce(den[n % 2][:, :], p3(n), X, ALU.add).then_inc(p_sum, 1)
                dve.wait_ge(p_sum, n + 1)
                dve.reciprocal(den[n % 2][:, :], den[n % 2][:, :]).then_inc(p_inv, 1)
                dve.wait_ge(p_inv, n + 1)
                dve.tensor_tensor(p3(n), p3(n), along(den[n % 2][:, :]), ALU.mult).then_inc(pn_ready, 1)
                if n + 1 < G:
                    masked_values(2 * n + 2)


def phase_queries1(nc, g):
    with ExitStack() as ctx:
        sb = lambda n, s, d=F32: ctx.enter_context(nc.sbuf_tensor(f"q1_{n}", s, d))
        S = lambda n: g.sem(f"q1_{n}")
        two = lambda n, s: [sb(f"{n}{i}", s) for i in range(2)]
        wq, wk, wks = two("wq", [P, 2, P]), two("wk", [P, C]), two("wks", [P, C])
        scale, eps = sb("scale", [P, 3]), sb("eps", [P, 1])
        qT, sq, rq, qn = two("qT", [P, T]), two("sq", [P, T]), two("rq", [P, T]), two("qn", [P, T])
        qall = sb("qall", [P, B, HQ])
        ps = [ctx.enter_context(nc.psum_tensor(f"q1_ps{i}", [P, 2, 512], F32)) for i in range(4)]
        pq, psum, pout = [ps[0], ps[1]], ps[2], ps[3]
        wq_in, wk_in, sc_in = [S("wq_in0"), S("wq_in1")], [S("wk_in0"), S("wk_in1")], S("sc_in")
        sc_ready, wk_ready, q_psum, q_ready, sq_ready = S("sc_ready"), S("wk_ready"), S("q_psum"), S("q_ready"), S("sq_ready")
        sum_psum, rooted, inverted, qn_ready = S("sum_psum"), S("rooted"), S("inverted"), S("qn_ready")
        out_psum, copied, stored = S("out_psum"), S("copied"), S("stored")
        block = ctx.enter_context(nc.Block())
        v2 = lambda t: t[:, :].rearrange("p (a n) -> p a n", a=2)
        LAG = 3

        def steps(step):
            for h in range(4):
                step(h, h // 2, h % 2, True, h >= 1, h >= LAG)
            yield
            for h in range(H, H + LAG):
                step(h, h // 2, h % 2, False, h == H, True)

        @block.sync
        def _(sp):
            with nc.allow_non_contiguous_dma(reason="columns of 128 scales"):
                sp.dma_start(scale[:, 0:1], g.a["gq"]).then_inc(sc_in, 16)
                sp.dma_start(scale[:, 1:2], g.a["gk"]).then_inc(sc_in, 16)
            for i in range(2):
                sp.dma_start(wq[i][:, :, :], g.a["L1_Wq"][i]).then_inc(wq_in[i], 16)
                sp.dma_start(wk[i][:, :], g.a["L1_WkT"][i]).then_inc(wk_in[i], 16)
            with sp.Fori(0, H // 2 - 1) as u:
                for i in range(2):
                    sp.wait_ge(q_psum, 2 * u + i + 1)
                    sp.dma_start(wq[i][:, :, :], g.a["L1_Wq"][2 * u + i + 2]).then_inc(wq_in[i], 16)
                    sp.wait_ge(wk_ready, 2 * u + i + 1)
                    sp.dma_start(wk[i][:, :], g.a["L1_WkT"][2 * u + i + 2]).then_inc(wk_in[i], 16)
            for half in range(2):
                sp.wait_ge(copied, 8 * half + 8 + 2)
                sp.dma_start(g.qdram[1][:, :, half * HALF:(half + 1) * HALF].rearrange("b c n -> c b n"),
                             qall[:, :, half * HALF:(half + 1) * HALF]).then_inc(stored, 16)
            sp.wait_ge(stored, 32)

        @block.tensor
        def _(pe):
            def step(h, pair, i, front, middle, back):
                if front:
                    pe.wait_ge(wq_in[i], 16 * pair + 16)
                    if not isinstance(h, int) or h >= 2:
                        pe.wait_ge(q_ready, h - 1)
                    for n in range(2):
                        for k in range(2):
                            mm = pe.matmul(pq[i][:, n, 0:HALF], wq[i][:, k, :],
                                           g.xnT[:, k, n * HALF:(n + 1) * HALF], start=(k == 0), stop=(k == 1))
                    mm.then_inc(q_psum, 1)
                if back:
                    pe.wait_ge(qn_ready, h - LAG + 1)
                    pe.wait_ge(wk_ready, h - LAG + 1)
                    pe.wait_ge(copied, h - LAG + 2)
                    for n in range(2):
                        mm = pe.matmul(pout[:, n, 0:HALF], wks[1 - i][:, :], qn[1 - i][:, n * HALF:(n + 1) * HALF],
                                       start=True, stop=True)
                    mm.then_inc(out_psum, 1)
                if middle:
                    pe.wait_ge(sq_ready, h)
                    pe.wait_ge(rooted, h - 1)
                    for n in range(2):
                        mm = pe.matmul(psum[:, n, 0:HALF], g.ones[:, :], sq[1 - i][:, n * HALF:(n + 1) * HALF],
                                       start=True, stop=True)
                    mm.then_inc(sum_psum, 1)
            s = steps(step)
            next(s)
            with pe.Fori(0, H // 2 - 2) as u:
                for i in range(2):
                    step(2 * u + 4 + i, u + 2, i, True, True, True)
            for _ in s:
                pass

        @block.scalar
        def _(act):
            act.wait_ge(sc_ready, 2)
            def step(h, pair, i, front, middle, back):
                if front:
                    act.wait_ge(q_psum, h + 1)
                    if not isinstance(h, int) or h >= 2:
                        act.wait_ge(qn_ready, h - 1)
                    act.activation(sq[i][:, :].rearrange("p (a n) -> p a n", a=2), pq[i][:, :, 0:HALF], ACT.Square)\
                       .then_inc(sq_ready, 1)
                    act.activation(v2(qT[i]), pq[i][:, :, 0:HALF], ACT.Copy).then_inc(q_ready, 1)
                if back:
                    act.wait_ge(out_psum, h - LAG + 1)
                    for n in range(2):
                        ins = act.activation(qall[:, 8 * n:8 * n + 8, (h - LAG) * NQ:(h - LAG + 1) * NQ] if isinstance(h, int)
                                             else qall[:, 8 * n:8 * n + 8, bass.ds((h - LAG) * NQ, NQ)],
                                             pout[:, n, 0:HALF].rearrange("p (b q) -> p b q", q=NQ), ACT.Copy)
                    ins.then_inc(copied, 1)
                if middle:
                    act.wait_ge(sum_psum, h)
                    act.activation(v2(rq[1 - i]), psum[:, :, 0:HALF], ACT.Sqrt, scale=1.0 / HD1, bias=eps[:, 0:1])\
                       .then_inc(rooted, 1)
            s = steps(step)
            next(s)
            with act.Fori(0, H // 2 - 2) as u:
                for i in range(2):
                    step(2 * u + 4 + i, u + 2, i, True, True, True)
            for _ in s:
                pass

        @block.vector
        def _(dve):
            dve.memset(eps[:, :], 1e-5).then_inc(sc_ready, 1)
            dve.wait_ge(sc_in, 32)
            dve.tensor_scalar(scale[:, 2:3], scale[:, 0:1], scale[:, 1:2], HD1 ** -0.5,
                              ALU.mult, ALU.mult).then_inc(sc_ready, 1)
            dve.wait_ge(sc_ready, 2)
            with dve.Fori(0, H // 2) as u:
                for i in range(2):
                    h = 2 * u + i
                    dve.wait_ge(wk_in[i], 16 * u + 16)
                    dve.wait_ge(copied, h + 1)
                    dve.tensor_scalar(wks[i][:, :], wk[i][:, :], scale[:, 2:3], None, ALU.mult).then_inc(wk_ready, 1)
                    dve.wait_ge(rooted, h + 1)
                    dve.reciprocal(rq[i][:, :], rq[i][:, :]).then_inc(inverted, 1)

        @block.gpsimd
        def _(pool):
            pool.sem_inc(copied, 2)
            with pool.Fori(0, H // 2) as u:
                for i in range(2):
                    h = 2 * u + i
                    pool.wait_ge(inverted, h + 1)
                    pool.wait_ge(copied, h + 1)
                    pool.tensor_tensor(qn[i][:, :], qT[i][:, :], rq[i][:, :], ALU.mult).then_inc(qn_ready, 1)


def phase_attention(nc, g, layer):
    KR = KR1 if layer else KR0
    rows = lambda j: P if j < NK - 1 else KR
    AT = NK // 2
    PART = [(0, AT * P), (AT * P, SEQ)]
    LAG = 3
    SC = 2 * NK
    USES = SC + 2
    OI = [(0, 3), (3, 6), (6, 7)]
    TI = [(0, 4), (4, 7)]
    qd, od = g.qdram[layer], g.odram[layer]
    with ExitStack() as ctx:
        sb = lambda n, s, d=F32: ctx.enter_context(nc.sbuf_tensor(f"a{layer}_{n}", s, d))
        two = lambda n, s, d=F32: [sb(f"{n}{i}", s, d) for i in range(2)]
        yT, yh, yl = sb("yT", [P, SEQ]), sb("yh", [P, SEQ], F32R), sb("yl", [P, SEQ], F32R)
        Q, Qh, Ql = sb("Q", [P, HQ]), two("Qh", [P, HQ], F32R), two("Ql", [P, HQ], F32R)
        y1 = two("y1", [P, NK, C + 1])
        if not layer:
            bias, ones3 = two("bias", [3, HQ], BF16), sb("ones3", [3, P], BF16)
        S = two("S", [P, NK, HQ])
        mx, mb = sb("mx", [P, HQ]), sb("mb", [P, HQ])
        mcol, diag = sb("mcol", [P, FT]), sb("diag", [P, FT, P])
        rden, on, oT = sb("rden", [P, FT]), sb("on", [P, FT, C]), sb("oT", [P, HQ])
        ring = [ctx.enter_context(nc.psum_tensor(f"a{layer}_ring{i}", [P, 512], F32)) for i in range(RING)]
        tb = ctx.enter_context(nc.psum_tensor(f"a{layer}_tb", [P, 512], F32))
        ob = [ctx.enter_context(nc.psum_tensor(f"a{layer}_ob{i}", [P, 512], F32)) for i in range(3)]
        N = lambda n: g.sem(f"a{layer}_{n}")
        yT_in, q_in, bias_in, y1_in = N("yT_in"), N("q_in"), [N("bias_in0"), N("bias_in1")], [N("y1_in0"), N("y1_in1")]
        one_set, y_high, y_split, q_high, q_split = N("one_set"), N("y_high"), N("y_split"), N("q_high"), N("q_split")
        s_ready, s_scaled, mx_ready = N("s_ready"), N("s_scaled"), N("mx_ready")
        mT_ready, mT_taken, diag_ready = N("mT_ready"), N("mT_taken"), N("diag_ready")
        mb_psum, mb_ready, shifted, p_ready, p_used = N("mb_psum"), N("mb_ready"), N("shifted"), N("p_ready"), N("p_used")
        rden_ready, on_ready = N("rden_ready"), N("on_ready")
        oT_ready, oT_copied, stored = N("oT_ready"), N("oT_copied"), N("stored")
        block = ctx.enter_context(nc.Block())
        from_ = lambda b, least: not isinstance(b, int) or b >= least

        def steps(step):
            step(0, 0, 0, True, True, False, False)
            step(1, 0, 1, True, True, True, False)
            yield
            step(B - 2, B // 2 - 1, 0, True, True, True, True)
            step(B - 1, B // 2 - 1, 1, True, False, True, True)
            step(B, B // 2, 0, False, False, True, True)
            step(B + 1, B // 2, 1, False, False, False, True)

        @block.sync
        def _(sp):
            def load(b, i):
                sp.dma_start(yT[:, :], g.a["ctxT"][b]).then_inc(yT_in, 16)
                sp.dma_start(Q[:, :], qd[b]).then_inc(q_in, 16)
                if not layer:
                    sp.dma_start(bias[i][:, :], g.bdram[b]).then_inc(bias_in[i], 16)

            def load_y1(b, i):
                sp.dma_start(y1[i][:, 0:NK - 1, 0:C],
                             g.a["ctx"][b, 0:(NK - 1) * P, :].rearrange("(j p) c -> p j c", p=P)).then_inc(y1_in[i], 16)
                sp.dma_start(y1[i][0:KR, NK - 1, 0:C],
                             g.a["ctx"][b, (NK - 1) * P:(NK - 1) * P + KR, :]).then_inc(y1_in[i], 16)

            def load_next(b, i):
                sp.wait_ge(y_split, 2 * b)
                sp.wait_ge(q_split, b)
                load(b, i)

            def refill(b, i):
                sp.wait_ge(p_used, NK * (b - 1))
                load_y1(b, i)
            load(0, 0)
            sp.wait_ge(one_set, 3)
            for i in range(2):
                load_y1(i, i)
            load_next(1, 1)
            load_next(2, 0)
            with sp.Fori(0, B // 2 - 2) as u:
                for i in range(2):
                    refill(2 * u + 2 + i, i)
                    load_next(2 * u + 3 + i, 1 - i)
            refill(B - 2, 0)
            load_next(B - 1, 1)
            refill(B - 1, 1)
            sp.wait_ge(stored, 16 * B)

        @block.tensor
        def _(pe):
            def step(b, pair, i, front, nxt, back, end):
                def scores(j):
                    n = rows(j)
                    if j == 0:
                        pe.wait_ge(y_split, 2 * b + 1)
                        pe.wait_ge(q_split, b + 1)
                        if not layer:
                            pe.wait_ge(bias_in[i], 16 * pair + 16)
                    if j == AT:
                        pe.wait_ge(y_split, 2 * b + 2)
                    for half in range(2):
                        use = 2 * j + half + (2 if j >= 2 else 0)
                        r = (USES * i + use) % RING
                        if use < 4:
                            if from_(b, 1):
                                pe.wait_ge(s_scaled, SC * b - 3 + use)
                        elif use in (8, 9):
                            if from_(b, 1):
                                pe.wait_ge(mb_ready, 2 * (b - 1) + use - 7)
                        else:
                            pe.wait_ge(s_scaled, SC * b + (use - 4 if use < 8 else use - 6) + 1)
                        cols = slice(half * HALF, (half + 1) * HALF)
                        dst = ring[r][0:n, 0:HALF]
                        high, low = yh[:, j * P:j * P + n], yl[:, j * P:j * P + n]
                        pe.matmul(dst, high, Qh[i][:, cols], start=True, stop=False)
                        pe.matmul(dst, high, Ql[i][:, cols], start=False, stop=False)
                        mm = pe.matmul(dst, low, Qh[i][:, cols], start=False, stop=bool(layer))
                        if not layer:
                            mm = pe.matmul(dst, ones3[:, 0:n], bias[i][:, cols], start=False, stop=True)
                        mm.then_inc(s_ready, 1)

                def output(bb, j, k_):
                    n = rows(j)
                    pe.wait_ge(p_ready, NK * bb + j + 1)
                    for k, (lo, hi) in enumerate(OI):
                        for q in range(lo, hi):
                            mm = pe.matmul(ob[k][:, (q - lo) * (C + 1):(q - lo + 1) * (C + 1)],
                                           S[k_][0:n, j, q * P:(q + 1) * P], y1[k_][0:n, j, :],
                                           start=(j == 0 and q == lo), stop=(j == NK - 1),
                                           skip_group_check=True)
                    mm.then_inc(p_used, 1)

                def maxima(k):
                    if k:
                        pe.wait_ge(mT_taken, 2 * (b - 1) + 1)
                    else:
                        pe.wait_ge(mx_ready, NK * b)
                        if from_(b, 3):
                            pe.wait_ge(oT_copied, 2 * (b - 2))
                    lo, hi = TI[k]
                    for q in range(lo, hi):
                        mm = pe.transpose(tb[:, (q - lo) * P:(q - lo + 1) * P], mx[:, q * P:(q + 1) * P], g.ident[:, :])
                    mm.then_inc(mT_ready, 1)

                def spread():
                    pe.wait_ge(diag_ready, b)
                    for half in range(2):
                        if front:
                            pe.wait_ge(s_scaled, SC * b + half + 1)
                        r = (USES * i + 4 + half) % RING
                        mm = pe.matmul(ring[r][:, 0:HALF], g.ones[:, :],
                                       diag[:, :, :].rearrange("p a n -> p (a n)")[:, half * HALF:(half + 1) * HALF],
                                       start=True, stop=True)
                        mm.then_inc(mb_psum, 1)

                def transposes_out(k):
                    lo, hi = TI[k]
                    pe.wait_ge(on_ready, 3 * (b - 1))
                    if k:
                        pe.wait_ge(oT_copied, 2 * (b - 2) + 1)
                    else:
                        pe.wait_ge(mT_taken, 2 * b if back else 2 * B)
                    for q in range(lo, hi):
                        mm = pe.transpose(tb[:, (q - lo) * P:(q - lo + 1) * P], on[:, q, :], g.ident[:, :])
                    mm.then_inc(oT_ready, 1)

                for j in range(NK):
                    if front:
                        scores(j)
                    if back and j == 0:
                        maxima(0)
                    if end and j < LAG:
                        for t in ((NK - LAG - 1 + j,) if j < LAG - 1 else (NK - 2, NK - 1)):
                            output(b - 2, t, i)
                    if back and j == 0:
                        maxima(1)
                    if back and j == 1:
                        spread()
                    if back and j > LAG:
                        if j == LAG + 1:
                            pe.wait_ge(y1_in[1 - i], 32 * (pair + i))
                            if from_(b, 2):
                                pe.wait_ge(on_ready, 3 * (b - 1))
                        output(b - 1, j - LAG - 1, 1 - i)
                    if end and j in (LAG + 1, LAG + 2):
                        transposes_out(j - LAG - 1)
            s = steps(step)
            next(s)
            with pe.Fori(0, B // 2 - 2) as u:
                for i in range(2):
                    step(2 * u + 2 + i, u + 1, i, True, True, True, True)
            for _ in s:
                pass

        @block.vector
        def _(dve):
            if not layer:
                dve.memset(ones3[:, :], 1.0).then_inc(one_set, 1)
            for i in range(2):
                dve.memset(y1[i][:, :, C:C + 1], 1.0).then_inc(one_set, 1)
            if layer:
                dve.sem_inc(one_set, 1)
            hoff = 0 if layer else H

            def low_q(b, i):
                dve.wait_ge(q_high, b + 1)
                dve.tensor_tensor(Ql[i][:, :], Q[:, :], Qh[i][:, :], ALU.subtract).then_inc(q_split, 1)

            def step(b, pair, i, front, nxt, back, end):
                for j in range(NK):
                    n = rows(j)
                    if end and j == LAG:
                        dve.wait_ge(p_used, NK * (b - 1))
                        if from_(b, 3):
                            dve.wait_ge(oT_ready, 2 * (b - 2))
                        for k, (lo, hi) in enumerate(OI):
                            den = ob[k][:, 0:(hi - lo) * (C + 1)].rearrange("p (a n) -> p a n", n=C + 1)
                            ins = dve.reciprocal(rden[:, lo:hi], den[:, :, C])
                        ins.then_inc(rden_ready, 1)
                        dve.wait_ge(rden_ready, b - 1)
                        for k, (lo, hi) in enumerate(OI):
                            den = ob[k][:, 0:(hi - lo) * (C + 1)].rearrange("p (a n) -> p a n", n=C + 1)
                            dve.tensor_tensor(on[:, lo:hi, :], den[:, :, 0:C],
                                              rden[:, lo:hi].unsqueeze(2).broadcast_to([P, hi - lo, C]), ALU.mult)\
                               .then_inc(on_ready, 1)
                    if front:
                        if from_(b, 2):
                            dve.wait_ge(p_used, NK * (b - 2) + j + 1)
                        for half in range(2):
                            r = (USES * i + 2 * j + half + (2 if j >= 2 else 0)) % RING
                            dve.wait_ge(s_ready, SC * b + 2 * j + half + 1)
                            rk = g.rk[0:n, b, j, hoff + 8 * half:hoff + 8 * half + 8]
                            dve.tensor_tensor(
                                S[i][0:n, j, half * HALF:(half + 1) * HALF].rearrange("p (h q) -> p h q", h=8),
                                ring[r][0:n, 0:HALF].rearrange("p (h q) -> p h q", h=8),
                                rk.unsqueeze(2).broadcast_to([n, 8, NQ]), ALU.mult).then_inc(s_scaled, 1)
                    if back and j == 0:
                        for k, (lo, hi) in enumerate(TI):
                            dve.wait_ge(mT_ready, 2 * (b - 1) + k + 1)
                            dve.tensor_reduce(mcol[:, lo:hi],
                                              tb[:, 0:(hi - lo) * P].rearrange("p (a n) -> p a n", n=P),
                                              X, ALU.max).then_inc(mT_taken, 1)
                        dve.wait_ge(mT_taken, 2 * b)
                        if from_(b, 2):
                            dve.wait_ge(mb_psum, 2 * (b - 1))
                        dve.tensor_tensor(diag[:, :, :], g.ident[:, None, :].broadcast_to([P, FT, P]),
                                          mcol[:, :, None].broadcast_to([P, FT, P]), ALU.mult).then_inc(diag_ready, 1)
                    if front:
                        dve.wait_ge(s_scaled, SC * b + 2 * j + 2)
                        if j == 0:
                            dve.tensor_copy(mx[:, :], S[i][:, 0, :]).then_inc(mx_ready, 1)
                        else:
                            dve.wait_ge(mx_ready, NK * b + j)
                            dve.tensor_tensor(mx[0:n, :], mx[0:n, :], S[i][0:n, j, :], ALU.max).then_inc(mx_ready, 1)
                    if nxt and j == NK - 3:
                        low_q(b + 1, 1 - i)
            low_q(0, 0)
            s = steps(step)
            next(s)
            with dve.Fori(0, B // 2 - 2) as u:
                for i in range(2):
                    step(2 * u + 2 + i, u + 1, i, True, True, True, True)
            for _ in s:
                pass

        @block.gpsimd
        def _(pool):
            def low_y(b, part):
                lo, hi = PART[part]
                pool.wait_ge(y_high, 2 * b + part + 1)
                pool.tensor_tensor(yl[:, lo:hi], yT[:, lo:hi], yh[:, lo:hi], ALU.subtract).then_inc(y_split, 1)

            def step(b, pair, i, front, nxt, back, end):
                for j in range(NK):
                    n = rows(j)
                    if nxt and j == AT:
                        low_y(b + 1, 0)
                    if back:
                        if j == 0:
                            pool.wait_ge(mb_ready, 2 * b)
                        pool.tensor_tensor(S[1 - i][0:n, j, :], S[1 - i][0:n, j, :], mb[0:n, :], ALU.subtract)\
                            .then_inc(shifted, 1)
                if nxt:
                    low_y(b + 1, 1)
            for part in range(2):
                low_y(0, part)
            s = steps(step)
            next(s)
            with pool.Fori(0, B // 2 - 2) as u:
                for i in range(2):
                    step(2 * u + 2 + i, u + 1, i, True, True, True, True)
            for _ in s:
                pass

        @block.scalar
        def _(act):
            def high_y(b, part):
                lo, hi = PART[part]
                act.wait_ge(yT_in, 16 * b + 16)
                if from_(b, 1):
                    act.wait_ge(s_ready, SC * (b - 1) + (NK if part == 0 else SC))
                act.activation(yh[:, lo:hi], yT[:, lo:hi], ACT.Copy).then_inc(y_high, 1)

            def high_q(b, i):
                act.wait_ge(q_in, 16 * b + 16)
                act.activation(Qh[i][:, :], Q[:, :], ACT.Copy).then_inc(q_high, 1)

            def step(b, pair, i, front, nxt, back, end):
                if back:
                    if from_(b, 2):
                        act.wait_ge(shifted, NK * (b - 1))
                    for half in range(2):
                        r = (USES * i + 4 + half) % RING
                        act.wait_ge(mb_psum, 2 * (b - 1) + half + 1)
                        act.activation(mb[:, half * HALF:(half + 1) * HALF], ring[r][:, 0:HALF], ACT.Copy)\
                           .then_inc(mb_ready, 1)
                for j in range(NK):
                    n = rows(j)
                    if back:
                        act.wait_ge(shifted, NK * (b - 1) + j + 1)
                        act.activation(S[1 - i][0:n, j, :], S[1 - i][0:n, j, :], ACT.Exp).then_inc(p_ready, 1)
                    if end and j in (1, 2):
                        k = j - 1
                        lo, hi = TI[k]
                        if k == 0 and from_(b, 3):
                            act.wait_ge(stored, 16 * (b - 2))
                        act.wait_ge(oT_ready, 2 * (b - 2) + k + 1)
                        act.activation(oT[:, lo * P:hi * P], tb[:, 0:(hi - lo) * P], ACT.Copy).then_inc(oT_copied, 1)
                        if k:
                            act.wait_ge(oT_copied, 2 * (b - 1))
                            act.dma_start(od[b - 2], oT[:, :]).then_inc(stored, 16)
                    if nxt and j == AT - 2:
                        high_y(b + 1, 0)
                        high_q(b + 1, 1 - i)
                if nxt:
                    high_y(b + 1, 1)
            high_q(0, 0)
            for part in range(2):
                high_y(0, part)
            s = steps(step)
            next(s)
            with act.Fori(0, B // 2 - 2) as u:
                for i in range(2):
                    step(2 * u + 2 + i, u + 1, i, True, True, True, True)
            for _ in s:
                pass


def phase_project(nc, g, layer):
    with ExitStack() as ctx:
        sb = lambda n, s, d=F32: ctx.enter_context(nc.sbuf_tensor(f"p{layer}_{n}", s, d))
        src = g.odram[layer]
        M = sb("M", [P, H, D])
        wv = sb("wv", [P, H, C])
        wo = sb("wo", [P, H if layer else 2, D])
        NB = B // 2
        ot = [sb(f"ot{i}", [P, NB, HQ]) for i in range(2)]
        sumT = sb("sumT", [P, 2, T])
        ps = [ctx.enter_context(nc.psum_tensor(f"p{layer}_ps{i}", [P, 512], F32)) for i in range(8)]
        N = lambda n: g.sem(f"p{layer}_{n}")
        w_in, ot_in, masked = N("w_in"), [N("ot_in0"), N("ot_in1")], N("masked")
        m_ready, m_copied, acc_ready, added = N("m_ready"), N("m_copied"), N("acc_ready"), N("added")
        sum_ready, back = N("sum_ready"), N("back")
        if not layer:
            v0, od = sb("v0", [P, 2, C]), sb("od", [P, 2, T])
            bv, bvs, bo, bias = sb("bv", [P, 2, 2]), sb("bvs", [P, 2]), sb("bo", [1, D]), sb("bias", [P, 2])
            bias_steps = N("bias_steps")
        block = ctx.enter_context(nc.Block())
        NM = H // 2

        @block.sync
        def _(sp):
            if layer:
                sp.dma_start(wv[:, :, :], g.a["L1_WvT"].rearrange("h d c -> d h c")).then_inc(w_in, 16)
                sp.dma_start(wo[:, :, :], g.a["L1_Wo"].rearrange("h d n -> d h n")).then_inc(w_in, 16)
            else:
                sp.dma_start(v0[:, :, :], g.a["v0T"]).then_inc(w_in, 16)
                sp.dma_start(wo[:, :, :], g.a["L0_Wo"]).then_inc(w_in, 16)
                sp.dma_start(bv[:, :, :], g.a["bv0"]).then_inc(w_in, 16)
                sp.dma_start(bo[:, :], g.a["bo0"]).then_inc(w_in, 16)
                sp.dma_start(od[:, :, :], g.ddram).then_inc(w_in, 16)

            for half in range(2):
                sp.dma_start(ot[half][:, :, :], src[half * NB:(half + 1) * NB].rearrange("b c n -> c b n"))\
                    .then_inc(ot_in[half], 16)

        @block.tensor
        def _(pe):
            pe.wait_ge(w_in, 32 if layer else 80)
            if not layer:
                pe.wait_ge(masked, 1)
                pe.wait_ge(bias_steps, 1)
                for dk in range(2):
                    cols = slice(dk * P, (dk + 1) * P)
                    for half in range(2):
                        pe.matmul(ps[7][:, dk:dk + 1], wo[:, half, cols], bvs[:, half:half + 1],
                                  start=(half == 0), stop=False)
                    mm = pe.matmul(ps[7][:, dk:dk + 1], bo[0:1, cols], g.ones[0:1, 0:1], start=False, stop=True)
                mm.then_inc(bias_steps, 1)
            for m in range(NM):
                if m >= 4:
                    pe.wait_ge(m_copied, m - 3)
                for k in range(2):
                    h = 2 * m + k
                    rhs = wo[:, h, :] if layer else wo[:, h // 8, :]
                    mm = pe.matmul(ps[m % 4][:, k * D:(k + 1) * D], wv[:, h, :], rhs, start=True, stop=True)
                mm.then_inc(m_ready, 1)
            pe.wait_ge(m_copied, NM)
            if not layer:
                pe.wait_ge(bias_steps, 3)
            for half in range(2):
                acc = [ps[4 + 2 * half + dk][:, 0:HALF] for dk in range(2)]
                if not layer:
                    for k in range(2):
                        for dk in range(2):
                            pe.matmul(acc[dk], wo[:, k, dk * P:(dk + 1) * P], od[:, k, half * HALF:(half + 1) * HALF],
                                      start=(k == 0), stop=False, skip_group_check=True)
                pe.wait_ge(ot_in[half], 16)
                for h in range(H):
                    rhs = ot[half][:, :, h * NQ:(h + 1) * NQ]
                    for dk in range(2):
                        mm = pe.matmul(acc[dk].rearrange("p (b q) -> p b q", b=NB),
                                       M[:, h, dk * P:(dk + 1) * P], rhs,
                                       start=(bool(layer) and h == 0), stop=(h == H - 1), skip_group_check=True)
                mm.then_inc(acc_ready, 1)
            for m in range(NT // 2):
                pe.wait_ge(sum_ready, 2 if m < 2 else 4)
                for k in range(2):
                    t = 2 * m + k
                    for dk in range(2):
                        mm = pe.transpose(ps[m][0:TT, (2 * k + dk) * P:(2 * k + dk + 1) * P],
                                          sumT[:, dk, t * TT:(t + 1) * TT], g.ident[:, :])
                mm.then_inc(back, 1)

        @block.scalar
        def _(act):
            for m in range(1, NM, 2):
                act.wait_ge(m_ready, m + 1)
                act.wait_ge(m_copied, m)
                act.activation(M[:, 2 * m:2 * m + 2, :].rearrange("p a n -> p (a n)"), ps[m % 4][:, :], ACT.Copy)\
                    .then_inc(m_copied, 1)

        @block.vector
        def _(dve):
            if not layer:
                dve.wait_ge(w_in, 80)
                for h in range(H):
                    ins = dve.tensor_scalar(wv[:, h, :], v0[:, h // 8, :], g.hmask[:, h % 8:h % 8 + 1], None,
                                            ALU.mult)
                ins.then_inc(masked, 1)
                dve.tensor_tensor(bvs[:, :], bv[:, 0, :], bv[:, 1, :], ALU.add).then_inc(bias_steps, 1)
            for m in range(0, NM, 2):
                dve.wait_ge(m_ready, m + 1)
                if m:
                    dve.wait_ge(m_copied, m)
                dve.tensor_copy(M[:, 2 * m:2 * m + 2, :].rearrange("p a n -> p (a n)"), ps[m % 4][:, :])\
                    .then_inc(m_copied, 1)
            if not layer:
                dve.wait_ge(bias_steps, 2)
                dve.tensor_copy(bias[:, :], ps[7][:, 0:2]).then_inc(bias_steps, 1)
                dve.wait_ge(bias_steps, 3)
            for half in range(2):
                dve.wait_ge(acc_ready, half + 1)
                for dk in range(2):
                    dst = sumT[:, dk, half * HALF:(half + 1) * HALF]
                    if layer:
                        dve.tensor_copy(dst, ps[4 + 2 * half + dk][:, 0:HALF]).then_inc(sum_ready, 1)
                    else:
                        dve.tensor_scalar(dst, ps[4 + 2 * half + dk][:, 0:HALF], bias[:, dk:dk + 1], None, ALU.add)\
                           .then_inc(sum_ready, 1)
            for m in range(NT // 2):
                dve.wait_ge(back, m + 1)
                xs = g.x[:, 2 * m:2 * m + 2, :]
                dve.tensor_tensor(xs, xs, ps[m][0:TT, :].rearrange("p (a n) -> p a n", a=2), ALU.add).then_inc(added, 1)


def phase_moe(nc, g):
    SLOTS = E * CAP
    NOE = 99.0
    with ExitStack() as ctx:
        sb = lambda n, s, d=F32: ctx.enter_context(nc.sbuf_tensor(f"m_{n}", s, d))
        N = lambda n: g.sem(f"m_{n}")
        r3 = lambda n: sb(n, [TT, NT, E])
        gw, gb, eid, trash, low = sb("gw", [P, 2, E]), sb("gb", [TT, E]), sb("eid", [TT, E]), \
            sb("trash", [TT, 2, NT]), sb("low", [TT, TT])
        lg, ab, ex, up, ln, dd, sc, sk = [r3(n) for n in ("lg", "ab", "ex", "up", "ln", "dd", "sc", "sk")]
        oh, tmp, A, pos = [r3("oh0"), r3("oh1")], r3("tmp"), r3("A"), r3("pos")
        mcol, ei, w, den = sb("mcol", [TT, NT]), sb("ei", [TT, 2, NT]), sb("w", [TT, 2, NT]), sb("den", [TT, NT])
        ps_, valid, base, sidx, gidx = [sb(n, [TT, 2, NT]) for n in ("pcol", "valid", "base", "sidx", "gidx")]
        su, gu = sb("su", [TT, 2 * NT], U32), sb("gu", [TT, 2 * NT], U32)
        zero = sb("zero", [P, 2048])
        FB = FF - P
        w13 = sb("w13", [P, E + 1, 2, 2, FF])
        w2a, w2b = sb("w2a", [P, E + 1, D]), sb("w2b", [FB, E + 1, D])
        xe, xeT, ye = [[sb(f"{n}{i}", [P, 2 * P]) for i in range(2)] for n in ("xe", "xeT", "ye")]
        th, he = [[sb(f"{n}{i}", [P, FF]) for i in range(2)] for n in ("th", "he")]
        heT = [sb(f"heT{i}", [P, 2, P]) for i in range(2)]
        hs, ts = sb("hs", [P, 2, T]), sb("ts", [P, T])
        yg = sb("yg", [TT, 2 * NT, D])
        ps = [ctx.enter_context(nc.psum_tensor(f"m_ps{i}", [P, 512], F32)) for i in range(8)]
        c_in, w_in, x_in = N("c_in"), [N("w_in0"), N("w_in1")], [N("x_in0"), N("x_in1")]
        shared_in = N("shared_in")
        zeroed, zero_out, scattered = N("zeroed"), N("zero_out"), N("scattered")
        gathered = [N("gathered0"), N("gathered1")]
        lg_psum, act_steps, steps, count_psum = N("lg_psum"), N("act_steps"), N("router_steps"), N("count_psum")
        sh_psum, sh_tanh, sh_steps, sh_out, sh_added = N("sh_psum"), N("sh_tanh"), N("sh_steps"), N("sh_out"), N("sh_added")
        side = N("side_steps")
        xT_psum, xT_ready, gu_psum, e_tanh, gated, h_ready, hT_psum, hT_ready, y_psum, y_ready = [
            N(n) for n in ("xT_psum", "xT_ready", "gu_psum", "e_tanh", "gated", "h_ready", "hT_psum", "hT_ready",
                           "y_psum", "y_ready")]
        y_stored, summed = [N("y_stored0"), N("y_stored1")], N("summed")
        block = ctx.enter_context(nc.Block())
        xbuf, ybuf = g.xbuf, g.ybuf
        bT, bGU, bH, bY = [(ps[k], ps[k + 1]) for k in (0, 2, 4, 6)]
        SPLIT = [(0, E // 2), (E // 2, E)]
        from_ = lambda e, least: not isinstance(e, int) or e >= least

        def stages(step):
            for n in range(4):
                step(n, n // 2, n % 2)
            yield
            for n in range(E, E + 3):
                step(n, n // 2, n % 2)
        at_stage = lambda n, lag: not isinstance(n, int) or lag <= n < E + lag

        @block.sync
        def _(sp):
            consts = [(gw, g.a["gw"]), (gb, g.a["gb"]), (eid, g.a["eid"]), (trash, g.a["trash"]), (low, g.a["low"])]
            for dst, src in consts:
                sp.dma_start(dst[tuple(slice(None) for _ in dst.shape)], src).then_inc(c_in, 16)

            def load_w(lo, hi, sem):
                sp.dma_start(w13[:, lo:hi, :, :, :], g.a["W13"][:, lo:hi]).then_inc(sem, 16)
                sp.dma_start(w2a[:, lo:hi, :], g.a["W2a"][:, lo:hi]).then_inc(sem, 16)
                sp.dma_start(w2b[:, lo:hi, :], g.a["W2b"][:, lo:hi]).then_inc(sem, 16)
            load_w(E, E + 1, shared_in)
            sp.wait_ge(zeroed, 1)
            for n in range(0, SLOTS, 1024):
                sp.dma_start(xbuf[n:n + 1024, :].rearrange("(p a) d -> p (a d)", p=P), zero[:, :]).then_inc(zero_out, 16)
            for n in range(2):
                load_w(*SPLIT[n], w_in[n])
            sp.wait_ge(scattered, 16 * 2 * NT)
            for i in range(2):
                sp.dma_start(xe[i][:, :], xbuf[i * CAP:(i + 1) * CAP, :]).then_inc(x_in[i], 16)
            with sp.Fori(0, E // 2 - 1) as u:
                for i in range(2):
                    e = 2 * u + i
                    sp.wait_ge(xT_psum, e + 1)
                    sp.dma_start(xe[i][:, :], xbuf[bass.ds((e + 2) * CAP, CAP), :]).then_inc(x_in[i], 16)

        @block.gpsimd
        def _(pool):
            pool.memset(zero[:, :], 0.0).then_inc(zeroed, 1)
            pool.wait_ge(zero_out, 16 * (SLOTS // 1024))
            pool.wait_ge(steps, 29)
            for t in range(NT):
                for k in range(2):
                    pool.indirect_dma_start(
                        out=xbuf, out_offset=bass.IndirectOffsetOnAxis(ap=su[:, k * NT + t:k * NT + t + 1], axis=0),
                        in_=g.xn[:, t, :], in_offset=None).then_inc(scattered, 16)
            for i in range(2):
                pool.wait_ge(y_stored[i], 16 * (E // 2))
            for t in range(NT):
                for k in range(2):
                    n = k * NT + t
                    pool.indirect_dma_start(
                        out=yg[:, n, :], out_offset=None, in_=ybuf,
                        in_offset=bass.IndirectOffsetOnAxis(ap=gu[:, n:n + 1], axis=0)).then_inc(gathered[t // 4], 16)
            for i in range(2):
                pool.wait_ge(gathered[i], 16 * NT)

        @block.tensor
        def _(pe):
            pe.wait_ge(c_in, 16 * 5)
            for t in range(NT):
                for k in range(2):
                    mm = pe.matmul(ps[0][0:TT, t * E:(t + 1) * E], g.xnT[:, k, t * TT:(t + 1) * TT], gw[:, k, :],
                                   start=(k == 0), stop=(k == 1), skip_group_check=True)
            mm.then_inc(lg_psum, 1)
            pe.wait_ge(shared_in, 48)
            def shared_part(part):
                m = FB if part else P
                for gu_ in range(2):
                    for half in range(2):
                        for k in range(2):
                            mm = pe.matmul(ps[1 + 2 * gu_ + half][0:m, 0:HALF],
                                           w13[:, E, k, gu_, part * P:part * P + m],
                                           g.xnT[:, k, half * HALF:(half + 1) * HALF], start=(k == 0), stop=(k == 1))
                mm.then_inc(sh_psum, 1)
            shared_part(0)
            pe.wait_ge(steps, 19)
            flat = A[:, :, :].rearrange("p t e -> p (t e)")
            pe.matmul(ps[0][0:TT, 0:E], low[:, :], flat[:, 0:E], start=True, stop=True, skip_group_check=True)
            pe.matmul(ps[0][0:TT, E:NT * E], low[:, :], flat[:, E:NT * E], start=True, stop=False,
                      skip_group_check=True)
            for t in reversed(range(NT - 1)):
                mm = pe.matmul(ps[0][0:TT, (t + 1) * E:NT * E].rearrange("p (t e) -> p t e", e=E), g.ones[0:TT, 0:TT],
                               A[:, t:t + 1, :].broadcast_to([TT, NT - 1 - t, E]), start=False, stop=(t == 0),
                               skip_group_check=True)
            mm.then_inc(count_psum, 1)
            pe.wait_ge(sh_steps, 4)
            shared_part(1)
            pe.wait_ge(sh_steps, 8)
            for t in range(NT):
                if t >= 2:
                    pe.wait_ge(sh_added, t - 1)
                pe.matmul(ps[5 + t % 2][0:TT, 0:D], hs[:, 0, t * TT:(t + 1) * TT], w2a[:, E, :], start=True, stop=False)
                pe.matmul(ps[5 + t % 2][0:TT, 0:D], hs[0:FB, 1, t * TT:(t + 1) * TT], w2b[:, E, :],
                          start=False, stop=True).then_inc(sh_out, 1)
            pe.wait_ge(sh_added, NT)

            at = lambda t, e: t[:, e:e + 1] if isinstance(e, int) else t[:, bass.ds(e, 1)]

            def step(n, pair, i):
                if at_stage(n, 0):
                    pe.wait_ge(x_in[i], 16 * pair + 16)
                    if from_(n, 2):
                        pe.wait_ge(xT_ready, n - 1)
                    for d in range(2):
                        mm = pe.transpose(bT[i][:, d * P:(d + 1) * P], xe[i][:, d * P:(d + 1) * P], g.ident[:, :])
                    mm.then_inc(xT_psum, 1)
                if at_stage(n, 1):
                    e = n - 1
                    pe.wait_ge(xT_ready, e + 1)
                    if from_(n, 3):
                        pe.wait_ge(h_ready, e - 1)
                    for d in range(2):
                        mm = pe.matmul(bGU[1 - i][:, 0:2 * FF], xeT[1 - i][:, d * P:(d + 1) * P],
                                       at(w13, e)[:, 0, d].rearrange("p g f -> p (g f)"),
                                       start=(d == 0), stop=(d == 1))
                    mm.then_inc(gu_psum, 1)
                if at_stage(n, 2):
                    e = n - 2
                    pe.wait_ge(h_ready, e + 1)
                    if from_(n, 4):
                        pe.wait_ge(hT_ready, 2 * (e - 1))
                    pe.transpose(bH[i][:, 0:P], he[i][:, 0:P], g.ident[:, :])
                    pe.transpose(bH[i][0:FB, P:2 * P], he[i][:, P:FF], g.ident[:, :]).then_inc(hT_psum, 1)
                if at_stage(n, 3):
                    e = n - 3
                    pe.wait_ge(hT_ready, 2 * (e + 1))
                    if from_(n, 5):
                        pe.wait_ge(y_ready, e - 1)
                    pe.matmul(bY[1 - i][:, 0:D], heT[1 - i][:, 0, :], at(w2a, e)[:, 0], start=True, stop=False)
                    pe.matmul(bY[1 - i][:, 0:D], heT[1 - i][0:FB, 1, :], at(w2b, e)[:, 0], start=False, stop=True)\
                      .then_inc(y_psum, 1)
            for n in range(2):
                pe.wait_ge(w_in[n], 48)
            s = stages(step)
            next(s)
            with pe.Fori(0, E // 2 - 2) as u:
                for i in range(2):
                    step(2 * u + 4 + i, u + 2, i)
            for _ in s:
                pass

        @block.scalar
        def _(act):
            act.wait_ge(steps, 2)
            act.activation(ex[:, :, :], ab[:, :, :], ACT.Exp, scale=-1.0).then_inc(act_steps, 1)
            for part in range(2):
                m = FB if part else P
                if part:
                    act.wait_ge(steps, 3)
                    act.activation(ln[:, :, :], up[:, :, :], ACT.Ln).then_inc(act_steps, 1)
                    act.wait_ge(steps, 8)
                    act.activation(sc[:, :, :], sc[:, :, :], ACT.Sqrt).then_inc(act_steps, 1)
                for half in range(2):
                    act.wait_ge(sh_psum, part + 1)
                    if part:
                        act.wait_ge(sh_steps, 2 * half + 2)
                    act.activation(ts[0:m, half * HALF:(half + 1) * HALF], ps[1 + half][0:m, 0:HALF], ACT.Tanh, scale=0.5)\
                       .then_inc(sh_tanh, 1)

            def step(n, pair, i):
                if at_stage(n, 1):
                    e = n - 1
                    act.wait_ge(gu_psum, e + 1)
                    if from_(n, 3):
                        act.wait_ge(gated, e - 1)
                    act.activation(th[1 - i][:, :], bGU[1 - i][:, 0:FF], ACT.Tanh, scale=0.5).then_inc(e_tanh, 1)
                if at_stage(n, 2):
                    e = n - 2
                    act.wait_ge(hT_psum, e + 1)
                    if from_(n, 4):
                        act.wait_ge(y_psum, e - 1)
                    act.activation(heT[i][:, 0, :], bH[i][:, 0:P], ACT.Copy).then_inc(hT_ready, 1)
                    act.activation(heT[i][0:FB, 1, :], bH[i][0:FB, P:2 * P], ACT.Copy).then_inc(hT_ready, 1)
                if at_stage(n, 3):
                    e = n - 3
                    act.wait_ge(y_psum, e + 1)
                    if from_(n, 5):
                        act.wait_ge(y_stored[1 - i], 16 * (pair - 2 + i))
                    act.activation(ye[1 - i][:, :], bY[1 - i][:, 0:D], ACT.Copy, scale=0.5).then_inc(y_ready, 1)
                    act.wait_ge(y_ready, e + 1)
                    act.dma_start(ybuf[e * CAP:(e + 1) * CAP, :] if isinstance(e, int) else ybuf[bass.ds(e * CAP, CAP), :],
                                  ye[1 - i][:, :]).then_inc(y_stored[1 - i], 16)
            s = stages(step)
            next(s)
            with act.Fori(0, E // 2 - 2) as u:
                for i in range(2):
                    step(2 * u + 4 + i, u + 2, i)
            for _ in s:
                pass

        @block.vector
        def _(dve):
            at = [0]

            def step(ins):
                at[0] += 1
                ins.then_inc(steps, 1)
                dve.wait_ge(steps, at[0])

            def bt(col):
                return col.unsqueeze(2).broadcast_to([TT, NT, E])

            def be(row):
                return row.unsqueeze(1).broadcast_to([TT, NT, E])
            a3 = lambda t: t[:, :, :]
            dve.wait_ge(lg_psum, 1)
            dve.wait_ge(c_in, 16 * 5)
            step(dve.tensor_copy(lg[:, :, :], ps[0][0:TT, 0:NT * E].rearrange("p (t e) -> p t e", e=E)))
            step(dve.scalar_tensor_tensor(out=a3(ab), in0=a3(lg), scalar=-1.0, in1=a3(lg), op0=ALU.mult,
                                          op1=ALU.max))
            dve.wait_ge(act_steps, 1)
            step(dve.tensor_scalar(a3(up), a3(ex), 1.0, None, ALU.add))
            step(dve.tensor_scalar(a3(dd), a3(up), 1.0, 1e-30, ALU.subtract, ALU.max))
            dve.reciprocal(a3(sk), a3(dd)).then_inc(side, 1)
            dve.tensor_scalar(a3(tmp), a3(up), 1.0, None, ALU.is_equal).then_inc(side, 1)
            dve.wait_ge(act_steps, 2)
            dve.wait_ge(side, 2)
            step(dve.tensor_tensor(a3(sk), a3(sk), a3(ln), ALU.mult))
            step(dve.tensor_tensor(a3(sk), a3(sk), a3(tmp), ALU.add))
            step(dve.tensor_tensor(a3(sk), a3(sk), a3(ex), ALU.mult))
            step(dve.scalar_tensor_tensor(out=a3(sc), in0=a3(lg), scalar=0.0, in1=a3(sk), op0=ALU.max,
                                          op1=ALU.add))
            dve.wait_ge(act_steps, 3)
            step(dve.tensor_tensor(a3(sk), a3(sc), be(gb[:, :]), ALU.add))
            for k in range(2):
                step(dve.tensor_reduce(mcol[:, :], a3(sk), X, ALU.max))
                step(dve.tensor_tensor(a3(tmp), a3(sk), bt(mcol[:, :]), ALU.is_equal))
                step(dve.tensor_tensor(a3(tmp), a3(tmp), be(eid[:, :]), ALU.mult))
                step(dve.tensor_reduce(ei[:, k, :], a3(tmp), X, ALU.min))
                if k == 0:
                    step(dve.tensor_tensor(a3(oh[0]), be(eid[:, :]), bt(ei[:, 0, :]), ALU.is_equal))
                    dve.scalar_tensor_tensor(out=a3(sk), in0=a3(oh[0]), scalar=-3e38, in1=a3(sk), op0=ALU.mult,
                                             op1=ALU.add).then_inc(side, 1)
                    dve.wait_ge(side, 3)
                else:
                    dve.tensor_tensor(a3(oh[1]), be(eid[:, :]), bt(ei[:, 1, :]), ALU.is_equal).then_inc(side, 1)
                    dve.wait_ge(side, 4)
                    step(dve.tensor_tensor(a3(A), a3(oh[0]), a3(oh[1]), ALU.add))
            for k in range(2):
                dve.tensor_tensor(a3(tmp if k else up), a3(oh[k]), a3(sc), ALU.mult).then_inc(side, 1)
                dve.wait_ge(side, 5 + 2 * k)
                dve.tensor_reduce(w[:, k, :], a3(tmp if k else up), X, ALU.add).then_inc(side, 1)
            dve.wait_ge(side, 8)
            step(dve.tensor_tensor(den[:, :], w[:, 0, :], w[:, 1, :], ALU.add))
            step(dve.reciprocal(den[:, :], den[:, :]))
            dve.wait_ge(count_psum, 1)
            step(dve.tensor_copy(a3(pos), ps[0][0:TT, 0:NT * E].rearrange("p (t e) -> p t e", e=E)))
            for k in range(2):
                dve.tensor_tensor(a3(tmp if k else up), a3(oh[k]), a3(pos), ALU.mult).then_inc(side, 1)
                dve.wait_ge(side, 9 + 2 * k)
                dve.tensor_reduce(ps_[:, k, :], a3(tmp if k else up), X, ALU.add).then_inc(side, 1)
            dve.wait_ge(side, 12)
            step(dve.tensor_scalar(a3(valid), a3(ps_), float(CAP), None, ALU.is_lt))
            step(dve.tensor_scalar(a3(base), a3(ei), NOE, float(CAP), ALU.add, ALU.mult))
            step(dve.tensor_tensor(a3(gidx), a3(ps_), a3(valid), ALU.mult))
            step(dve.tensor_tensor(a3(sidx), a3(base), a3(ps_), ALU.add))
            dve.tensor_tensor(a3(gidx), a3(gidx), a3(base), ALU.add).then_inc(side, 1)
            dve.tensor_tensor(a3(sidx), a3(sidx), a3(trash), ALU.subtract).then_inc(side, 1)
            dve.wait_ge(side, 14)
            step(dve.tensor_tensor(a3(sidx), a3(sidx), a3(valid), ALU.mult))
            step(dve.tensor_tensor(a3(sidx), a3(sidx), a3(trash), ALU.add))
            dve.tensor_copy(gu[:, :], gidx[:, :, :].rearrange("p k t -> p (k t)")).then_inc(side, 1)
            step(dve.tensor_copy(su[:, :], sidx[:, :, :].rearrange("p k t -> p (k t)")))
            dve.tensor_tensor(a3(w), a3(w), a3(valid), ALU.mult).then_inc(side, 1)
            dve.wait_ge(side, 16)
            dve.tensor_tensor(a3(w), a3(w), den[:, :].unsqueeze(1).broadcast_to([TT, 2, NT]), ALU.mult).then_inc(side, 1)

            for part in range(2):
                m = FB if part else P
                for half in range(2):
                    t_ = ts[0:m, half * HALF:(half + 1) * HALF]
                    h_ = hs[0:m, part, half * HALF:(half + 1) * HALF]
                    dve.wait_ge(sh_tanh, 2 * part + half + 1)
                    dve.scalar_tensor_tensor(out=h_, in0=t_, scalar=1.0, in1=ps[1 + half][0:m, 0:HALF],
                                             op0=ALU.add, op1=ALU.mult).then_inc(sh_steps, 1)
                    dve.wait_ge(sh_steps, 4 * part + 2 * half + 1)
                    dve.tensor_tensor(h_, h_, ps[3 + half][0:m, 0:HALF], ALU.mult).then_inc(sh_steps, 1)
            for t in range(NT):
                dve.wait_ge(sh_out, t + 1)
                dve.scalar_tensor_tensor(out=g.x[:, t, :], in0=ps[5 + t % 2][0:TT, 0:D], scalar=0.5, in1=g.x[:, t, :],
                                         op0=ALU.mult, op1=ALU.add).then_inc(sh_added, 1)

            def step(n, pair, i):
                if at_stage(n, 0):
                    dve.wait_ge(xT_psum, n + 1)
                    if from_(n, 2):
                        dve.wait_ge(gu_psum, n - 1)
                    dve.tensor_copy(xeT[i][:, :], bT[i][:, 0:2 * P]).then_inc(xT_ready, 1)
                if at_stage(n, 1):
                    e = n - 1
                    dve.wait_ge(e_tanh, e + 1)
                    if from_(n, 3):
                        dve.wait_ge(hT_psum, e - 1)
                    dve.scalar_tensor_tensor(out=he[1 - i][:, :], in0=th[1 - i][:, :], scalar=1.0,
                                             in1=bGU[1 - i][:, 0:FF], op0=ALU.add, op1=ALU.mult).then_inc(gated, 1)
                    dve.wait_ge(gated, e + 1)
                    dve.tensor_tensor(he[1 - i][:, :], he[1 - i][:, :], bGU[1 - i][:, FF:2 * FF], ALU.mult)\
                       .then_inc(h_ready, 1)
            s = stages(step)
            next(s)
            with dve.Fori(0, E // 2 - 2) as u:
                for i in range(2):
                    step(2 * u + 4 + i, u + 2, i)
            for _ in s:
                pass
            for t in range(NT):
                for k in range(2):
                    n = k * NT + t
                    dve.wait_ge(gathered[t // 4], 16 * NT)
                    if t or k:
                        dve.wait_ge(summed, 2 * t + k)
                    dve.scalar_tensor_tensor(out=g.x[:, t, :], in0=yg[:, n, :], scalar=w[:, k, t:t + 1],
                                             in1=g.x[:, t, :], op0=ALU.mult, op1=ALU.add).then_inc(summed, 1)


def phase_bitlinear(nc, g):
    with ExitStack() as ctx:
        sb = lambda n, s, d=F32: ctx.enter_context(nc.sbuf_tensor(f"b_{n}", s, d))
        N = lambda n: g.sem(f"b_{n}")
        wf = [sb("wg", [P, 2, FI]), sb("wu", [P, 2, FI]), sb("wd", [P, FT, D])]
        wq = [sb("wgq", [P, 2, FI], BF16), sb("wuq", [P, 2, FI], BF16), sb("wdq", [P, FT, D], BF16)]
        wabs, wm, wsc = sb("wabs", [P, 3]), sb("wm", [P, 3]), sb("wsc", [P, 3])
        ma, sx, sg, cc = sb("ma", [TT, NT]), sb("sx", [TT, NT]), sb("sg", [TT, NT]), sb("cc", [TT, NT])
        xq = sb("xq", [TT, NT, D])
        xqT = sb("xqT", [P, 2, T], BF16)
        th, hh, hm = sb("th", [TT, FI]), sb("hh", [TT, FI]), sb("hm", [TT, 4])
        hT = sb("hT", [P, FT, TT], BF16)
        pgu = [ctx.enter_context(nc.psum_tensor(f"b_pgu{i}", [P, 1024], F32)) for i in range(2)]
        pt = ctx.enter_context(nc.psum_tensor("b_pt", [P, 1024], F32))
        pd = ctx.enter_context(nc.psum_tensor("b_pd", [P, 512], F32))
        pw = ctx.enter_context(nc.psum_tensor("b_pw", [P, 512], F32))
        w_in, wd_zero, sums, w_steps, wsum_psum = N("w_in"), N("wd_zero"), N("sums"), N("w_steps"), N("wsum_psum")
        x_steps, xT_psum, xT_ready = N("x_steps"), N("xT_psum"), N("xT_ready")
        gu_psum, tanh_ready, h_steps, hT_psum, hT_ready, d_psum, added, stored = [
            N(n) for n in ("gu_psum", "tanh_ready", "h_steps", "hT_psum", "hT_ready", "d_psum", "added", "stored")]
        block = ctx.enter_context(nc.Block())
        h_sc = N("h_scaled")
        HS = 7
        FC = [(0, 512), (512, FI)]

        @block.sync
        def _(sp):
            sp.dma_start(wf[0][:, :, :], g.a["WgT"]).then_inc(w_in, 16)
            sp.dma_start(wf[1][:, :, :], g.a["WuT"]).then_inc(w_in, 16)
            sp.wait_ge(wd_zero, 1)
            sp.dma_start(wf[2][:, 0:FT - 1, :], g.a["WdT"][0:(FT - 1) * P, :].rearrange("(f p) d -> p f d", p=P))\
              .then_inc(w_in, 16)
            sp.dma_start(wf[2][0:LASTF, FT - 1, :], g.a["WdT"][(FT - 1) * P:FI, :]).then_inc(w_in, 16)
            o = g.out.rearrange("b q d -> (b q) d").rearrange("(t p) d -> p t d", p=TT)
            for half in range(2):
                sp.wait_ge(added, 4 * half + 4)
                sp.dma_start(o[:, 4 * half:4 * half + 4, :], g.x[:, 4 * half:4 * half + 4, :]).then_inc(stored, 16)
            sp.wait_ge(stored, 32)

        @block.gpsimd
        def _(pool):
            pool.memset(wf[2][:, FT - 1, :], 0.0).then_inc(wd_zero, 1)

        @block.tensor
        def _(pe):
            pe.wait_ge(sums, 3)
            pe.matmul(pw[:, 0:3], g.ones[:, :], wabs[:, :], start=True, stop=True).then_inc(wsum_psum, 1)
            pe.wait_ge(x_steps, 13)
            for n in range(4):
                k, half = n // 2, n % 2
                bank = [pt[:, 0:512], pt[:, 512:1024], pd[:, :], pw[:, :]][n]
                if n == 3:
                    pe.wait_ge(w_steps, 1)
                for t in range(4):
                    mm = pe.transpose(bank[:, t * TT:(t + 1) * TT], xq[:, 4 * half + t, k * P:(k + 1) * P],
                                      g.ident[0:TT, 0:TT])
                mm.then_inc(xT_psum, 1)

            def gate_up(t):
                for m in range(2):
                    for lo, hi in FC:
                        for k in range(2):
                            mm = pe.matmul(pgu[m][0:TT, lo:hi], xqT[:, k, bass.ds(t * TT, TT)], wq[m][:, k, lo:hi],
                                           start=(k == 0), stop=(k == 1))
                mm.then_inc(gu_psum, 1)

            def tile(t, last):
                if not last:
                    pe.wait_ge(h_steps, HS * t + 2)
                    gate_up(t + 1)
                pe.wait_ge(h_steps, HS * t + HS)
                for f in range(FT):
                    n = P if f < FT - 1 else LASTF
                    lo = f * TT if f < 4 else 512 + (f - 4) * TT
                    mm = pe.transpose(pt[0:n, lo:lo + TT], hh[:, f * P:f * P + n], g.ident[0:TT, 0:TT])
                mm.then_inc(hT_psum, 1)
                pe.wait_ge(hT_ready, 3 * t + 3)
                for f in range(FT):
                    n = P if f < FT - 1 else LASTF
                    mm = pe.matmul(pd[0:TT, 0:D], hT[0:n, f, :], wq[2][0:n, f, :], start=(f == 0), stop=(f == FT - 1))
                mm.then_inc(d_psum, 1)
            pe.wait_ge(w_steps, 12)
            pe.wait_ge(xT_ready, 4)
            gate_up(0)
            with pe.Fori(0, 3) as u:
                for i in range(2):
                    tile(2 * u + i, False)
            tile(NT - 2, False)
            tile(NT - 1, True)

        @block.scalar
        def _(act):
            with act.Fori(0, NT) as t:
                act.wait_ge(gu_psum, t + 1)
                act.wait_ge(x_steps, 15)
                act.activation(th[:, :], pgu[0][0:TT, 0:FI], ACT.Tanh, scale=sg[:, bass.ds(t, 1)]).then_inc(tanh_ready, 1)

        @block.vector
        def _(dve):
            count = float(FI * D)
            for m in range(3):
                dve.wait_ge(w_in, 64)
                dve.tensor_reduce(wabs[:, m:m + 1], wf[m][:, :, :], mybir.AxisListType.XY, ALU.add,
                                  apply_absolute_value=True).then_inc(sums, 1)
            dve.tensor_reduce(ma[:, :], g.xn[:, :, :], X, ALU.max, apply_absolute_value=True).then_inc(x_steps, 1)
            dve.wait_ge(x_steps, 1)
            dve.tensor_scalar(ma[:, :], ma[:, :], 1e-5, None, ALU.max).then_inc(x_steps, 1)
            dve.wait_ge(x_steps, 2)
            dve.reciprocal(sx[:, :], ma[:, :]).then_inc(x_steps, 1)
            dve.wait_ge(x_steps, 3)
            dve.tensor_scalar(sx[:, :], sx[:, :], 127.0, None, ALU.mult).then_inc(x_steps, 1)
            dve.wait_ge(x_steps, 4)
            for t in range(NT):
                ins = dve.tensor_scalar(xq[:, t, :], g.xn[:, t, :], sx[:, t:t + 1], 127.0, ALU.mult, ALU.min)
                ins.then_inc(x_steps, 1)
            dve.wait_ge(x_steps, 12)
            dve.tensor_scalar(xq[:, :, :], xq[:, :, :], -128.0, MAGIC, ALU.max, ALU.add).then_inc(sums, 1)
            dve.wait_ge(sums, 4)
            dve.tensor_scalar(xq[:, :, :], xq[:, :, :], MAGIC, None, ALU.subtract).then_inc(x_steps, 1)

            dve.wait_ge(wsum_psum, 1)
            dve.tensor_scalar(wm[:, :], pw[:, 0:3], 1.0 / count, 1e-5, ALU.mult, ALU.max).then_inc(w_steps, 1)
            dve.wait_ge(w_steps, 1)
            dve.reciprocal(wsc[:, :], wm[:, :]).then_inc(w_steps, 1)
            dve.wait_ge(w_steps, 2)
            for m in range(3):
                w = wf[m][:, :, :]
                dve.tensor_scalar(w, w, wsc[:, m:m + 1], 1.0, ALU.mult, ALU.min).then_inc(w_steps, 1)
                dve.wait_ge(w_steps, 3 * m + 3)
                dve.tensor_scalar(w, w, -1.0, MAGIC, ALU.max, ALU.add).then_inc(w_steps, 1)
                dve.wait_ge(w_steps, 3 * m + 4)
                dve.tensor_scalar(wq[m][:, :, :], w, MAGIC, None, ALU.subtract).then_inc(w_steps, 1)
            for n in range(4):
                k, half = n // 2, n % 2
                bank = [pt[:, 0:512], pt[:, 512:1024], pd[:, :], pw[:, :]][n]
                dve.wait_ge(xT_psum, n + 1)
                dve.tensor_copy(xqT[:, k, half * HALF:(half + 1) * HALF], bank[:, 0:HALF]).then_inc(xT_ready, 1)
            dve.wait_ge(x_steps, 13)
            dve.tensor_scalar(sg[:, :], ma[:, :], wm[0:TT, 0:1], 0.5 / 127.0, ALU.mult, ALU.mult).then_inc(x_steps, 1)
            dve.wait_ge(w_steps, 11)
            dve.wait_ge(x_steps, 14)
            dve.tensor_tensor(cc[:, :], sg[:, :], ma[:, :], ALU.mult).then_inc(x_steps, 1)
            dve.wait_ge(x_steps, 15)
            dve.tensor_scalar(cc[:, :], cc[:, :], wm[0:TT, 1:2], 1.0 / 127.0, ALU.mult, ALU.mult).then_inc(w_steps, 1)
            dve.wait_ge(w_steps, 12)

            with dve.Fori(0, NT) as t:
                c = cc[:, bass.ds(t, 1)]
                dve.wait_ge(tanh_ready, t + 1)
                dve.wait_ge(hT_psum, t)
                dve.scalar_tensor_tensor(out=hh[:, :], in0=th[:, :], scalar=1.0, in1=pgu[0][0:TT, 0:FI],
                                         op0=ALU.add, op1=ALU.mult).then_inc(h_steps, 1)
                dve.wait_ge(h_steps, HS * t + 1)
                dve.tensor_tensor(hh[:, :], hh[:, :], pgu[1][0:TT, 0:FI], ALU.mult).then_inc(h_steps, 1)
                dve.wait_ge(h_steps, HS * t + 2)
                dve.tensor_reduce(hm[:, 0:1], hh[:, :], X, ALU.max, apply_absolute_value=True).then_inc(h_steps, 1)
                dve.wait_ge(h_steps, HS * t + 3)
                dve.tensor_scalar(hm[:, 1:2], hm[:, 0:1], c, 1e-5, ALU.mult, ALU.max).then_inc(h_steps, 1)
                dve.wait_ge(h_steps, HS * t + 4)
                dve.reciprocal(hm[:, 2:3], hm[:, 1:2]).then_inc(h_steps, 1)
                dve.wait_ge(h_steps, HS * t + 5)
                dve.tensor_scalar(hm[:, 3:4], hm[:, 2:3], c, 127.0, ALU.mult, ALU.mult).then_inc(h_sc, 1)
                dve.wait_ge(h_sc, 3 * t + 1)
                dve.tensor_scalar(hh[:, :], hh[:, :], hm[:, 3:4], 127.0, ALU.mult, ALU.min).then_inc(h_sc, 1)
                dve.wait_ge(h_sc, 3 * t + 2)
                dve.tensor_scalar(hh[:, :], hh[:, :], -128.0, MAGIC, ALU.max, ALU.add).then_inc(h_sc, 1)
                dve.wait_ge(h_sc, 3 * t + 3)
                dve.tensor_scalar(hh[:, :], hh[:, :], MAGIC, None, ALU.subtract).then_inc(h_steps, 1)
                dve.tensor_scalar(hm[:, 2:3], hm[:, 1:2], wm[0:TT, 2:3], 1.0 / 127.0, ALU.mult, ALU.mult)\
                   .then_inc(h_steps, 1)
                dve.wait_ge(hT_psum, t + 1)
                dve.tensor_copy(hT[:, 0:4, :].rearrange("p f n -> p (f n)"), pt[:, 0:4 * TT]).then_inc(hT_ready, 1)
                dve.tensor_copy(hT[:, 4:6, :].rearrange("p f n -> p (f n)"), pt[:, 512:512 + 2 * TT]).then_inc(hT_ready, 1)
                dve.tensor_copy(hT[0:LASTF, 6, :], pt[0:LASTF, 512 + 2 * TT:512 + 3 * TT]).then_inc(hT_ready, 1)
                dve.wait_ge(d_psum, t + 1)
                dve.wait_ge(h_steps, HS * t + 7)
                dve.scalar_tensor_tensor(out=g.x[:, t, :], in0=pd[0:TT, 0:D], scalar=hm[:, 2:3], in1=g.x[:, t, :],
                                         op0=ALU.mult, op1=ALU.add).then_inc(added, 1)


def phase_setup(nc, g):
    loaded = g.sem("loaded")
    n = 0
    with nc.Block() as block:
        @block.sync
        def _(sp):
            items = [(g.x, g.a["x"]), (g.ident, g.a["ident"]), (g.ones, g.a["ones"]), (g.cen, g.a["cen"]), (g.blk, g.a["blk"]),
                     (g.hmask, g.a["hmask"]), (g.bk0row, g.a["bk0"]), (g.bkdrow, g.a["bkd"])]
            for dst, src in items:
                sp.dma_start(dst[tuple(slice(None) for _ in dst.shape)], src).then_inc(loaded, 16)
            sp.wait_ge(loaded, 16 * len(items))


def build(nc, a, out):
    with ExitStack() as ctx:
        sb = lambda n, s, d=F32: ctx.enter_context(nc.sbuf_tensor(n, s, d))
        g = Shared()
        g.a, g.out = a, out
        g.sem = nc.alloc_semaphore
        g.x = sb("x", [TT, NT, D])
        g.rk_all = sb("rk", [P, B + 1, NK, 2 * H])
        g.rk = g.rk_all[:, 1:, :, :]
        g.ident, g.ones = sb("ident", [P, P]), sb("ones", [P, P])
        g.cen, g.blk, g.hmask = sb("cen", [P, P]), sb("blk", [P, P]), sb("hmask", [P, 8])
        g.bk0row, g.bkdrow = sb("bk0row", [1, D]), sb("bkdrow", [1, D])
        g.qdram = [nc.dram_tensor(f"qdram{l}", [B, P, HQ], F32).ap() for l in range(2)]
        g.odram = [nc.dram_tensor(f"odram{l}", [B, P, HQ], F32).ap() for l in range(2)]
        g.bdram = nc.dram_tensor("bdram", [B, 3, HQ], BF16).ap()
        g.xbuf = nc.dram_tensor("xbuf", [E * CAP + 2 * T, D], F32).ap()
        g.ybuf = nc.dram_tensor("ybuf", [E * CAP, D], F32).ap()
        g.ddram = nc.dram_tensor("ddram", [P, 2, T], F32).ap()

        def with_normed(name, *phases):
            with nc.sbuf_tensor(f"{name}_xn", [TT, NT, D], F32) as g.xn, nc.sbuf_tensor(f"{name}_xnT", [P, 2, T], F32) as g.xnT:
                phase_layernorm(nc, g, name)
                for phase in phases:
                    phase()
        with nc.cleanup_on_exit():
            phase_setup(nc, g)
            phase_norms(nc, g)
            with nc.sbuf_tensor("qs0", [P, T], F32) as qs0, nc.sbuf_tensor("qs1", [P, T], F32) as qs1, \
                    nc.sbuf_tensor("cols", [P, 2, 5], F32) as g.cols:
                g.qs = [qs0, qs1]
                with_normed("l0", lambda: phase_queries0(nc, g))
                phase_dca(nc, g)
            phase_attention(nc, g, 0)
            phase_project(nc, g, 0)
            with_normed("l1", lambda: phase_moe(nc, g))
        with nc.cleanup_on_exit():
            with_normed("l2", lambda: phase_queries1(nc, g))
            phase_attention(nc, g, 1)
            phase_project(nc, g, 1)
            with_normed("l3", lambda: phase_bitlinear(nc, g))


def laid_out(i):
    rows = lambda w: w.reshape(2, P, -1).transpose(1, 0, 2)
    wkv = np.concatenate([i["L0_xattn_Wk"], i["L0_xattn_Wv"]], 1).reshape(C, H, 2, HD0)
    bkv = np.concatenate([i["L0_xattn_bk"], i["L0_xattn_bv"]]).reshape(H, 2, HD0)
    wk0, wv0 = wkv[:, :, 0].reshape(C, D), wkv[:, :, 1].reshape(C, D)
    bk0, bv0 = bkv[:, 0].reshape(D), bkv[:, 1].reshape(D)
    wkd, wvd = i["L0_xattn_Wkv_dca"][:, :D], i["L0_xattn_Wkv_dca"][:, D:]
    bkd, bvd = i["L0_xattn_bkv_dca"][:D], i["L0_xattn_bkv_dca"][D:]
    k0T = np.concatenate([wk0, bk0[None]], 0).T.reshape(2, P, C + 1)
    rep = lambda w: np.tile(w, 8)
    bq = i["L0_xattn_bq"].reshape(2, P)
    cols = np.stack([np.stack([bq[s], rep(i["L0_xattn_qn_w"]), rep(i["L0_xattn_qn_b"]),
                               rep(i["L0_xattn_kn_w"]), rep(i["L0_xattn_kn_dca_w"])], 1) for s in range(2)])
    head = np.arange(P) // HD0
    same = (head[:, None] == head[None, :]).astype(np.float32)
    a = {
        "x": i["x"].reshape(NT, TT, D).transpose(1, 0, 2),
        "ctx": i["ctx_1024"], "ctxT": i["ctx_1024"].transpose(0, 2, 1),
        "ident": np.eye(P, dtype=np.float32), "ones": np.ones((P, P), np.float32),
        "cen": np.eye(P, dtype=np.float32) - same / np.float32(HD0), "blk": same,
        "hmask": (head[:, None] == np.arange(8)[None, :]).astype(np.float32),
        "low": np.triu(np.ones((TT, TT), np.float32), 1),
        "L0_Wk": wk0, "L0_Wkd": wkd, "L0_Wvd": wvd, "ydT": i["ctx_1024"][:, SEQ - DCA:].transpose(2, 0, 1).reshape(C, B * DCA), "bk0": bk0[None], "bkd": bkd[None],
        "k0T": k0T.transpose(1, 0, 2), "cols0": cols.transpose(1, 0, 2),
        "L0_Wq": rows(i["L0_xattn_Wq"]),
        "v0T": wv0.T.reshape(2, P, C).transpose(1, 0, 2),
        "bv0": np.stack([bv0.reshape(2, P).T, bvd.reshape(2, P).T], 1), "L0_Wo": rows(i["L0_xattn_Wo"]),
        "bo0": i["L0_xattn_bo"][None],
        "L1_Wk": i["L1_xattn_Wk"],
        "L1_Wq": i["L1_xattn_Wq"].reshape(2, P, H, P).transpose(2, 1, 0, 3),
        "L1_WkT": i["L1_xattn_Wk"].T.reshape(H, P, C),
        "gq": i["L1_xattn_gq"][:, None], "gk": i["L1_xattn_gk"][:, None],
        "L1_WvT": i["L1_xattn_Wv"].T.reshape(H, P, C), "L1_Wo": i["L1_xattn_Wo"].reshape(H, P, D),
    }
    kxn = lambda w: w.transpose(0, 2, 1).reshape(E + 1, 2, P, FF).transpose(2, 0, 1, 3)
    a["W13"] = np.stack([kxn(np.concatenate([i[f"L0_ffn_W{n}"], i[f"L0_ffn_Ws{n}"][None]])) for n in (1, 3)], 3)
    w2 = np.concatenate([i["L0_ffn_W2"], i["L0_ffn_Ws2"][None]]).transpose(2, 0, 1)
    a["W2a"], a["W2b"] = w2[:P], w2[P:]
    a["gw"] = rows(i["L0_ffn_gate_w"].T)
    a["gb"] = np.broadcast_to(i["L0_ffn_gate_b"], (TT, E))
    a["eid"] = np.broadcast_to(np.arange(E, dtype=np.float32) - 99, (TT, E))
    token = np.arange(NT)[None, None, :] * TT + np.arange(TT)[:, None, None]
    a["WgT"], a["WuT"] = rows(i["L1_ffn_w_gate"].T), rows(i["L1_ffn_w_up"].T)
    a["WdT"] = i["L1_ffn_w_down"].T
    a["trash"] = (E * CAP + 2 * token + np.arange(2)[None, :, None]).astype(np.float32)
    return a


_OUTS = [((B, NQ, D), "float32")]


def kernel(**inputs):
    import numpy as _np
    import concourse.bacc as _bacc
    from concourse import mybir as _mybir
    from concourse.bass_utils import run_bass_kernel_spmd as _run

    nc = _bacc.Bacc("TRN2", target_bir_lowering=False, num_devices=1)
    arrays, aps = {}, {}
    for name, arr in laid_out({k: _np.asarray(v) for k, v in inputs.items()}).items():
        arr = _np.ascontiguousarray(arr)
        arrays[f"in_{name}"] = arr
        aps[name] = nc.dram_tensor(f"in_{name}", arr.shape, _mybir.dt.from_np(arr.dtype), kind="ExternalInput").ap()
    out = nc.dram_tensor("out_0", _OUTS[0][0], F32, kind="ExternalOutput").ap()
    build(nc, aps, out)
    return _run(nc, [arrays], core_ids=[0]).results[0]["out_0"]
```

```python
from contextlib import ExitStack

import numpy as np

import concourse.bass as bass
from concourse import mybir

F32 = mybir.dt.float32
BF16 = mybir.dt.bfloat16
F32R = mybir.dt.float32r
U32 = mybir.dt.uint32
ALU = mybir.AluOpType
ACT = mybir.ActivationFunctionType
X = mybir.AxisListType.X

P = 128
B, NQ, D = 16, 56, 256
C, H = 128, 16
HQ = H * NQ
HALF = HQ // 2
SEQ, DCA = 1500, 16
NK = 12
TT = 2 * NQ
NT = B // 2
T = B * NQ
HD0, HD1 = D // H, 128
E, CAP, FF = 16, 128, 176
FI = 832
FT = 7
LASTF = FI - 6 * P
KR1 = SEQ - (NK - 1) * P
KR0 = KR1 - DCA
RING = 4
HEAD_GROUPS = [(0, 5), (5, 9), (9, 12), (12, 14), (14, 16)]
MAGIC = 12582912.0


class Shared:
    pass


def phase_norms(nc, g):
    with ExitStack() as ctx:
        sb = lambda n, s, d=F32: ctx.enter_context(nc.sbuf_tensor(n, s, d))
        WN = (H * HD1 + D)
        wall = sb("n_wall", [P, WN])
        wh, wl = sb("n_wh", [P, WN], F32R), sb("n_wl", [P, WN], F32R)
        yT = [sb(f"n_yT{i}", [P, SEQ]) for i in range(2)]
        yh, yl = [[sb(f"n_{n}{i}", [P, SEQ], F32R) for i in range(2)] for n in ("yh", "yl")]
        sq = sb("n_sq", [P, 3, 1024])
        km = sb("n_km", [P, H])
        bkm = sb("n_bkm", [1, H])
        bpart, bparts, ones3 = sb("n_bpart", [1, 3, D], BF16), sb("n_bparts", [3, D], BF16), sb("n_ones3", [3, P], BF16)
        slot = [ctx.enter_context(nc.psum_tensor(f"n_slot{i}", [P, 1024], F32)) for i in range(3)]
        W = [1024, 1024, 256]
        w_in, yT_in = g.sem("n_w_in"), [g.sem("n_yT_in0"), g.sem("n_yT_in1")]
        w_ready, cent, w_split = g.sem("n_w_ready"), g.sem("n_cent"), g.sem("n_w_split")
        b_steps, b_in, y_high, y_split = g.sem("n_b_steps"), g.sem("n_b_in"), g.sem("n_y_high"), g.sem("n_y_split")
        parts_used, w0_high, w1_high = g.sem("n_parts_used"), g.sem("n_w0_high"), g.sem("n_w1_high")
        prod, slot_free = g.sem("n_prod"), g.sem("n_slot_free")
        sq_free, scaled = g.sem("n_sq_free"), g.sem("n_scaled")
        rooted, inverted = g.sem("n_rooted"), g.sem("n_inverted")
        block = ctx.enter_context(nc.Block())
        k0 = wall[:, 2048:2304].rearrange("p (h d) -> p h d", h=H)
        bk0 = g.bk0row[0:1, :].rearrange("p (h d) -> p h d", h=H)

        @block.sync
        def _(sp):
            sp.dma_start(wall[:, 0:2048], g.a["L1_Wk"]).then_inc(w_in, 16)
            sp.dma_start(wall[:, 2048:2304], g.a["L0_Wk"]).then_inc(w_in, 16)
            for i in range(2):
                sp.dma_start(yT[i][:, :], g.a["ctxT"][i]).then_inc(yT_in[i], 16)
            sp.wait_ge(b_steps, 6)
            for n in range(3):
                sp.dma_start(bparts[n:n + 1, :], bpart[0:1, n, :]).then_inc(b_in, 16)
            with sp.Fori(0, B // 2 - 1) as u:
                for i in range(2):
                    sp.wait_ge(y_split, 2 * u + i + 1)
                    sp.dma_start(yT[i][:, :], g.a["ctxT"][2 * u + 2 + i]).then_inc(yT_in[i], 16)
            sp.wait_ge(b_in, 48)

        @block.gpsimd
        def _(pool):
            pool.sem_inc(parts_used, 2)
            with pool.Fori(0, B // 2) as u:
                for i in range(2):
                    pool.wait_ge(yT_in[i], 16 * u + 16)
                    pool.wait_ge(parts_used, 2 * u + i + 1)
                    pool.tensor_tensor(yh[i][:, :], yT[i][:, :], g.ones[:, 0:1].broadcast_to([P, SEQ]), ALU.mult)\
                        .then_inc(y_high, 1)
                    pool.wait_ge(y_high, 2 * u + i + 1)
                    pool.tensor_tensor(yl[i][:, :], yT[i][:, :], yh[i][:, :], ALU.subtract).then_inc(y_split, 1)

        @block.tensor
        def _(pe):
            pe.wait_ge(w_split, 2)
            pe.wait_ge(b_in, 48)
            with pe.Fori(0, B // 2) as u:
                for i in range(2):
                    pe.wait_ge(y_split, 2 * u + i + 1)
                    for j in range(NK):
                        n = P if j < NK - 1 else KR1
                        tile = (2 * u + i) * NK + j
                        high, low = yh[i][:, j * P:j * P + n], yl[i][:, j * P:j * P + n]
                        for s in range(3):
                            pe.wait_ge(slot_free, tile * 3 + s + 1)
                            for c in range(0, W[s], 512):
                                w = min(512, W[s] - c)
                                cols = slice(1024 * s + c, 1024 * s + c + w)
                                dst = slot[s][0:n, c:c + w]
                                pe.matmul(dst, high, wh[:, cols], start=True, stop=False)
                                pe.matmul(dst, high, wl[:, cols], start=False, stop=False)
                                mm = pe.matmul(dst, low, wh[:, cols], start=False, stop=(s < 2))
                                if s == 2 and j == NK - 1:
                                    mm.then_inc(parts_used, 1)
                            if s == 2:
                                mm = pe.matmul(slot[s][0:n, 0:256], ones3[:, 0:n], bparts[:, :], start=False, stop=True)
                            mm.then_inc(prod, 1)

        @block.scalar
        def _(act):
            def roots(b):
                act.wait_ge(scaled, 2 * (b + 2))
                act.activation(g.rk_all[:, b + 1, :, :], g.rk_all[:, b + 1, :, :], ACT.Sqrt).then_inc(rooted, 1)
            act.sem_inc(slot_free, 3)
            act.wait_ge(w_in, 32)
            act.activation(wh[:, 0:2048], wall[:, 0:2048], ACT.Copy).then_inc(w1_high, 1)
            with act.Fori(0, B // 2) as u:
                for i in range(2):
                    b = 2 * u + i
                    for j in range(NK):
                        if j == 4:
                            roots(b - 1)
                        n = P if j < NK - 1 else KR1
                        tile = b * NK + j
                        for s in range(3):
                            act.wait_ge(prod, tile * 3 + s + 1)
                            act.wait_ge(sq_free, tile * 3 + s + 1)
                            act.activation(sq[0:n, s, 0:W[s]], slot[s][0:n, 0:W[s]], ACT.Square)\
                               .then_inc(slot_free, 1)
            roots(B - 1)

        @block.vector
        def _(dve):
            dve.tensor_reduce(bkm[:, :], bk0, X, ALU.add).then_inc(cent, 1)
            dve.wait_ge(cent, 1)
            dve.scalar_tensor_tensor(out=bk0, in0=bkm[:, :, None].broadcast_to([1, H, HD0]),
                                     scalar=-1.0 / HD0, in1=bk0, op0=ALU.mult, op1=ALU.add).then_inc(w_ready, 1)
            dve.wait_ge(w_ready, 1)
            dve.memset(ones3[:, :], 1.0).then_inc(b_steps, 1)
            for n in range(3):
                dve.tensor_copy(bpart[:, n, :], g.bk0row[:, :]).then_inc(b_steps, 1)
                dve.wait_ge(b_steps, 2 + 2 * n)
                if n < 2:
                    dve.tensor_tensor(g.bk0row[:, :], g.bk0row[:, :], bpart[:, n, :], ALU.subtract).then_inc(b_steps, 1)
                    dve.wait_ge(b_steps, 3 + 2 * n)
            dve.memset(g.rk_all[:, :, NK - 1, :], 1.0).then_inc(cent, 1)
            dve.memset(g.rk_all[:, 0, 0:NK - 1, :], 1.0).then_inc(cent, 1)
            dve.wait_ge(w_in, 32)
            dve.wait_ge(cent, 3)
            dve.tensor_reduce(km[:, :], k0, X, ALU.add).then_inc(cent, 1)
            dve.wait_ge(cent, 4)
            dve.scalar_tensor_tensor(out=k0, in0=km[:, :, None].broadcast_to([P, H, HD0]),
                                     scalar=-1.0 / HD0, in1=k0, op0=ALU.mult, op1=ALU.add).then_inc(w_ready, 1)
            dve.wait_ge(w_ready, 2)
            dve.tensor_copy(wh[:, 2048:2304], wall[:, 2048:2304]).then_inc(w0_high, 1)
            dve.wait_ge(w0_high, 1)
            dve.tensor_tensor(wl[:, 2048:2304], wall[:, 2048:2304], wh[:, 2048:2304], ALU.subtract).then_inc(w_split, 1)
            dve.wait_ge(w1_high, 1)
            dve.tensor_tensor(wl[:, 0:2048], wall[:, 0:2048], wh[:, 0:2048], ALU.subtract).then_inc(w_split, 1)

            def scale(b):
                dve.wait_ge(sq_free, (b + 1) * NK * 3 + 3)
                r1, r0 = g.rk_all[:, b + 1, :, 0:H], g.rk_all[:, b + 1, :, H:2 * H]
                dve.tensor_scalar(r1, r1, 1.0 / HD1, 1e-5, ALU.mult, ALU.add).then_inc(scaled, 1)
                dve.tensor_scalar(r0, r0, 1.0 / HD0, 1e-6, ALU.mult, ALU.add).then_inc(scaled, 1)

            def invert(b, j):
                dve.reciprocal(g.rk_all[:, b + 1, j:j + 3, :], g.rk_all[:, b + 1, j:j + 3, :]).then_inc(inverted, 1)
            dve.sem_inc(sq_free, 3)
            with dve.Fori(0, B // 2) as u:
                for i in range(2):
                    b = 2 * u + i
                    for j in range(NK):
                        if j == 1:
                            scale(b - 1)
                        if j == 6:
                            dve.wait_ge(rooted, b + 1)
                        n = P if j < NK - 1 else KR1
                        tile = b * NK + j
                        for s in range(3):
                            dve.wait_ge(slot_free, tile * 3 + s + 1 + 3)
                            heads = 8 if s < 2 else H
                            dve.tensor_reduce(
                                g.rk[0:n, b, j, 8 * s:8 * s + heads],
                                sq[0:n, s, 0:W[s]].rearrange("p (h d) -> p h d", h=heads),
                                X, ALU.add).then_inc(sq_free, 1)
                        if 6 <= j < 10:
                            invert(b - 1, 3 * (j - 6))
            scale(B - 1)
            dve.wait_ge(rooted, B + 1)
            for j in range(0, NK, 3):
                invert(B - 1, j)


def phase_layernorm(nc, g, name):
    with ExitStack() as ctx:
        sb = lambda n, s, d=F32: ctx.enter_context(nc.sbuf_tensor(f"{name}_{n}", s, d))
        st, mv, rs = sb("st", [TT, NT, 6]), sb("mv", [TT, NT, 2]), sb("rs", [TT, NT])
        ps = [ctx.enter_context(nc.psum_tensor(f"{name}_ps{i}", [P, 512], F32)) for i in range(4)]
        stats, std, xn_ready = g.sem(f"{name}_stats"), g.sem(f"{name}_std"), g.sem(f"{name}_xn_ready")
        tr, copied = g.sem(f"{name}_tr"), g.sem(f"{name}_copied")
        block = ctx.enter_context(nc.Block())

        @block.vector
        def _(dve):
            for t in range(NT):
                dve.bn_stats(st[:, t, :], g.x[:, t, :]).then_inc(stats, 1)
            dve.wait_ge(stats, NT)
            for t in range(NT):
                dve.bn_aggr(mv[:, t, :], st[:, t, :]).then_inc(stats, 1)
            dve.wait_ge(stats, 2 * NT)
            dve.tensor_scalar(rs[:, :], mv[:, :, 1], 1e-5, None, ALU.add).then_inc(std, 1)
            dve.wait_ge(std, 2)
            dve.reciprocal(rs[:, :], rs[:, :]).then_inc(std, 1)
            dve.wait_ge(std, 3)
            for t in range(NT):
                dve.tensor_scalar(g.xn[:, t, :], g.x[:, t, :], mv[:, t, 0:1], rs[:, t:t + 1],
                                  ALU.subtract, ALU.mult).then_inc(xn_ready, 1)
            for n in range(0, 4, 2):
                dve.wait_ge(tr, n + 1)
                dve.tensor_copy(g.xnT[:, n // 2, 0:HALF], ps[n][:, 0:HALF]).then_inc(copied, 1)

        @block.scalar
        def _(act):
            act.wait_ge(std, 1)
            act.activation(rs[:, :], rs[:, :], ACT.Sqrt).then_inc(std, 1)
            for n in range(1, 4, 2):
                act.wait_ge(tr, n + 1)
                act.activation(g.xnT[:, n // 2, HALF:T], ps[n][:, 0:HALF], ACT.Copy).then_inc(copied, 1)

        @block.tensor
        def _(pe):
            for n in range(4):
                k, half = n // 2, n % 2
                pe.wait_ge(xn_ready, 4 * half + 4)
                for t in range(4):
                    mm = pe.transpose(ps[n][:, t * TT:(t + 1) * TT],
                                      g.xn[:, 4 * half + t, k * P:(k + 1) * P], g.ident[0:TT, 0:TT])
                mm.then_inc(tr, 1)


def phase_queries0(nc, g):
    with ExitStack() as ctx:
        sb = lambda n, s, d=F32: ctx.enter_context(nc.sbuf_tensor(f"q0_{n}", s, d))
        S = lambda n: g.sem(f"q0_{n}")
        wk_in, wkc = sb("wk_in", [P, 2, C + 1]), sb("wkc", [P, 2, C + 1])
        wqa = sb("wqa", [P, 2, D])
        mkw = sb("mkw", [P, 2, 8])
        lb = sb("lb", [P, 2, H])
        lhk = [sb(f"lhk{i}", [P, C]) for i in range(2)]
        eps = sb("eps", [P, 1])
        qa, qc, sq, rq = [[sb(f"{n}{i}", [P, T]) for i in range(2)] for n in ("qa", "qc", "sq", "rq")]
        qall = sb("qall", [P, B, HQ])
        bt = sb("bt", [H, T])
        parts = sb("parts", [H, 3, T], BF16)
        ps = [ctx.enter_context(nc.psum_tensor(f"q0_ps{i}", [P, 2, 512], F32)) for i in range(4)]
        in_done, wk_psum, wk_ready = S("in_done"), S("wk_psum"), S("wk_ready")
        q_psum, q_ready, c_psum, c_ready, sq_ready = S("q_psum"), S("q_ready"), S("c_psum"), S("c_ready"), S("sq_ready")
        sum_psum, rooted, inverted = S("sum_psum"), S("rooted"), S("inverted")
        qn_ready, qs_ready = S("qn_ready"), S("qs_ready")
        mask_ready, lb_ready, b_psum, b_steps = S("mask_ready"), S("lb_ready"), S("b_psum"), S("b_steps")
        lh_ready, hq_psum, copied, stored = S("lh_ready"), S("hq_psum"), S("copied"), S("stored")
        block = ctx.enter_context(nc.Block())
        v2 = lambda t: t[:, :].rearrange("p (a n) -> p a n", a=2)

        @block.sync
        def _(sp):
            sp.dma_start(wqa[:, :, :], g.a["L0_Wq"]).then_inc(in_done, 16)
            sp.dma_start(g.cols[:, :, :], g.a["cols0"]).then_inc(in_done, 16)
            sp.dma_start(wk_in[:, :, :], g.a["k0T"]).then_inc(in_done, 16)
            sp.wait_ge(b_steps, 7)
            for n in range(3):
                sp.dma_start(g.bdram[:, n, :].rearrange("b (h q) -> h b q", h=H),
                             parts[:, n, :].rearrange("h (b q) -> h b q", b=B)).then_inc(stored, 16)
            for lo, hi in HEAD_GROUPS:
                cols = slice(lo * NQ, hi * NQ)
                sp.wait_ge(copied, hi + 1)
                sp.dma_start(g.qdram[0][:, :, cols].rearrange("b c n -> c b n"), qall[:, :, cols]).then_inc(stored, 16)
            sp.wait_ge(stored, 16 * (3 + len(HEAD_GROUPS)))

        @block.tensor
        def _(pe):
            def both(dst, lhs, rhs):
                for n in range(2):
                    mm = pe.matmul(dst[:, n, 0:HALF], lhs, rhs[:, n * HALF:(n + 1) * HALF], start=True, stop=True)
                return mm
            pe.wait_ge(in_done, 48)
            for half in range(2):
                for n in range(2):
                    for k in range(2):
                        mm = pe.matmul(ps[half][:, n, 0:HALF], wqa[:, k, half * P:(half + 1) * P],
                                       g.xnT[:, k, n * HALF:(n + 1) * HALF], start=(k == 0), stop=(k == 1))
                mm.then_inc(q_psum, 1)
            for half in range(2):
                mm = pe.matmul(ps[2][:, 0, half * 256:half * 256 + C + 1], g.cen[:, :], wk_in[:, half, :],
                               start=True, stop=True)
            mm.then_inc(wk_psum, 1)
            pe.wait_ge(wk_ready, 1)
            for half in range(2):
                pe.wait_ge(q_ready, half + 1)
                both(ps[2 + half], g.cen[:, :], qa[half]).then_inc(c_psum, 1)
            for half in range(2):
                pe.wait_ge(sq_ready, half + 1)
                both(ps[half], g.blk[:, :], sq[half]).then_inc(sum_psum, 1)
            pe.wait_ge(qs_ready, 2)
            pe.wait_ge(lb_ready, 1)
            pe.wait_ge(rooted, 2)
            for n in range(2):
                for half in range(2):
                    mm = pe.matmul(ps[0][0:H, n, 0:HALF], lb[:, half, :], g.qs[half][:, n * HALF:(n + 1) * HALF],
                                   start=(half == 0), stop=(half == 1))
            mm.then_inc(b_psum, 1)
            for half in range(2):
                with pe.Fori(0, 4) as u:
                    for i in range(2):
                        h = 8 * half + 2 * u + i
                        pe.wait_ge(lh_ready, h + 1)
                        pe.wait_ge(copied, h)
                        both(ps[2 + i], lhk[i][:, :], g.qs[half]).then_inc(hq_psum, 1)

        @block.scalar
        def _(act):
            for half in range(2):
                act.wait_ge(c_psum, half + 1)
                act.activation(v2(sq[half]), ps[2 + half][:, :, 0:HALF], ACT.Square).then_inc(sq_ready, 1)
            act.wait_ge(mask_ready, 2)
            for half in range(2):
                act.wait_ge(sum_psum, half + 1)
                act.activation(v2(rq[half]), ps[half][:, :, 0:HALF], ACT.Sqrt, scale=1.0 / HD0, bias=eps[:, 0:1])\
                   .then_inc(rooted, 1)
            act.wait_ge(c_ready, 2)
            act.sem_inc(copied, 1)
            with act.Fori(0, 8) as u:
                for i in range(2):
                    h = 2 * u + i
                    act.wait_ge(hq_psum, h + 1)
                    for n in range(2):
                        ins = act.activation(qall[:, 8 * n:8 * n + 8, bass.ds(h * NQ, NQ)],
                                             ps[2 + i][:, n, 0:HALF].rearrange("p (b q) -> p b q", q=NQ), ACT.Copy)
                    ins.then_inc(copied, 1)

        @block.vector
        def _(dve):
            dve.memset(eps[:, :], 1e-6).then_inc(mask_ready, 1)
            dve.wait_ge(in_done, 48)
            for half in range(2):
                ins = dve.tensor_scalar(mkw[:, half, :], g.hmask[:, :], g.cols[:, half, 3:4], HD0 ** -0.5,
                                        ALU.mult, ALU.mult)
            ins.then_inc(mask_ready, 1)
            dve.memset(lb[:, :, :], 0.0).then_inc(b_steps, 1)
            for half in range(2):
                dve.wait_ge(q_psum, half + 1)
                dve.tensor_scalar(v2(qa[half]), ps[half][:, :, 0:HALF], g.cols[:, half, 0:1], None, ALU.add)\
                   .then_inc(q_ready, 1)
                if half == 0:
                    dve.wait_ge(wk_psum, 1)
                    dve.tensor_copy(wkc[:, :, :], ps[2][:, 0, :].rearrange("p (a n) -> p a n", a=2)[:, :, 0:C + 1])\
                       .then_inc(wk_ready, 1)
            for half in range(2):
                dve.wait_ge(sq_ready, half + 1)
                dve.tensor_copy(v2(qc[half]), ps[2 + half][:, :, 0:HALF]).then_inc(c_ready, 1)
            dve.wait_ge(wk_ready, 1)
            dve.wait_ge(mask_ready, 2)
            dve.wait_ge(b_steps, 1)
            for half in range(2):
                ins = dve.tensor_scalar(lb[:, half, 8 * half:8 * half + 8], mkw[:, half, :],
                                        wkc[:, half, C:C + 1], None, ALU.mult)
            ins.then_inc(lb_ready, 1)
            for half in range(2):
                dve.wait_ge(rooted, half + 1)
                dve.reciprocal(rq[half][:, :], rq[half][:, :]).then_inc(inverted, 1)
                dve.wait_ge(inverted, half + 1)
                dve.wait_ge(c_ready, half + 1)
                dve.tensor_tensor(qc[half][:, :], qc[half][:, :], rq[half][:, :], ALU.mult).then_inc(qn_ready, 1)
                dve.wait_ge(qn_ready, half + 1)
                dve.tensor_scalar(g.qs[half][:, :], qc[half][:, :], g.cols[:, half, 1:2], g.cols[:, half, 2:3],
                                  ALU.mult, ALU.add).then_inc(qs_ready, 1)
            def weights(half, u, i):
                dve.tensor_scalar(lhk[i][:, :], wkc[:, half, 0:C], mkw[:, half, bass.ds(2 * u + i, 1)],
                                  None, ALU.mult).then_inc(lh_ready, 1)
            dve.wait_ge(b_psum, 1)
            dve.tensor_copy(bt[:, :].rearrange("p (a n) -> p a n", a=2), ps[0][0:H, :, 0:HALF]).then_inc(b_steps, 1)
            dve.wait_ge(b_steps, 2)
            for n in range(3):
                dve.tensor_copy(parts[:, n, :], bt[:, :]).then_inc(b_steps, 1)
                if n < 2:
                    dve.wait_ge(b_steps, 3 + 2 * n)
                    dve.tensor_tensor(bt[:, :], bt[:, :], parts[:, n, :], ALU.subtract).then_inc(b_steps, 1)
                    dve.wait_ge(b_steps, 4 + 2 * n)
            for half in range(2):
                with dve.Fori(0, 4) as u:
                    for i in range(2):
                        h = 8 * half + 2 * u + i
                        dve.wait_ge(copied, h)
                        weights(half, u, i)


def phase_dca(nc, g):
    NKD = B * DCA
    GB = 4
    with ExitStack() as ctx:
        sb = lambda n, s, d=F32: ctx.enter_context(nc.sbuf_tensor(f"d_{n}", s, d))
        S = lambda n: g.sem(f"d_{n}")
        ydT, wkd, wvd = sb("ydT", [P, NKD]), sb("wkd", [P, D]), sb("wvd", [P, D])
        yrep = sb("yrep", [P, B, 8, DCA])
        kk, ksq = sb("kk", [P, 2, D]), sb("ksq", [P, 2, D])
        kmean, krs = sb("kmean", [P, 2 * H]), sb("krs", [P, 2 * H])
        kT = sb("kT", [P, 2, NKD])
        km = sb("km", [P, 2, B, 8, DCA])
        vm = sb("vm", [P, B, D])
        eps = sb("eps", [P, 1])
        pr = [sb(f"pr{i}", [NQ, GB, H, DCA]) for i in range(2)]
        smax, den = [[sb(f"{n}{i}", [NQ, GB * H]) for i in range(2)] for n in ("smax", "den")]
        pT = [sb(f"pT{i}", [P, 2, GB * NQ]) for i in range(2)]
        oT = sb("oT", [P, 2, T])
        sc = [ctx.enter_context(nc.psum_tensor(f"d_sc{i}", [P, 1024], F32)) for i in range(2)]
        pt, pv = [ctx.enter_context(nc.psum_tensor(f"d_{n}", [P, 512], F32)) for n in ("pt", "pv")]
        po = [ctx.enter_context(nc.psum_tensor(f"d_po{i}", [P, 512], F32)) for i in range(2)]
        y_in, w_in, eps_set, rep_ready = S("y_in"), S("w_in"), S("eps_set"), S("rep_ready")
        k_psum, k_steps, v_var, rooted, kT_psum, kT_ready, km_ready = [
            S(n) for n in ("k_psum", "k_steps", "v_var", "rooted", "kT_psum", "kT_ready", "km_ready")]
        v_psum, v_ready, s_psum, s_max, s_ready, p_ready, p_sum, p_inv, pn_ready = [
            S(n) for n in ("v_psum", "v_ready", "s_psum", "s_max", "s_ready", "p_ready", "p_sum", "p_inv", "pn_ready")]
        pT_psum, pT_ready, o_psum, o_ready, stored = [
            S(n) for n in ("pT_psum", "pT_ready", "o_psum", "o_ready", "stored")]
        block = ctx.enter_context(nc.Block())
        G = B // GB
        f = lambda t: t[:, :, :].rearrange("p a n -> p (a n)")

        @block.sync
        def _(sp):
            sp.dma_start(ydT[:, :], g.a["ydT"]).then_inc(y_in, 16)
            sp.dma_start(wkd[:, :], g.a["L0_Wkd"]).then_inc(w_in, 16)
            sp.dma_start(wvd[:, :], g.a["L0_Wvd"]).then_inc(w_in, 16)
            load_first_context(sp, g, KR0)
            sp.wait_ge(o_ready, G)
            sp.dma_start(g.ddram, oT[:, :, :]).then_inc(stored, 16)
            sp.wait_ge(stored, 16)

        @block.tensor
        def _(pe):
            pe.wait_ge(y_in, 16)
            pe.wait_ge(w_in, 32)
            for t in range(2):
                pe.matmul(pt[:, t * D:(t + 1) * D], ydT[:, t * P:(t + 1) * P], wkd[:, :], start=True, stop=False)
                mm = pe.matmul(pt[:, t * D:(t + 1) * D], g.ones[0:1, :], g.bkdrow[0:1, :], start=False, stop=True)
            mm.then_inc(k_psum, 1)
            pe.wait_ge(rep_ready, 1)

            def values(n):
                pe.wait_ge(v_ready, n)
                for k in range(2):
                    mm = pe.matmul(pv[:, k * D:(k + 1) * D],
                                   yrep[:, 2 * n + k, :, :].rearrange("p h k -> p (h k)"), wvd[:, :],
                                   start=True, stop=True)
                mm.then_inc(v_psum, 1)
            values(0)
            pe.wait_ge(k_steps, 5)
            for t in range(2):
                for half in range(2):
                    mm = pe.transpose(pt[:, half * NKD + t * P:half * NKD + (t + 1) * P],
                                      kk[:, t, half * P:(half + 1) * P], g.ident[:, :])
            mm.then_inc(kT_psum, 1)
            pe.wait_ge(km_ready, 2)

            def scores(n):
                if n >= 2:
                    pe.wait_ge(s_ready, n - 1)
                for k in range(GB):
                    b = GB * n + k
                    for half in range(2):
                        mm = pe.matmul(sc[n % 2][0:NQ, (2 * k + half) * P:(2 * k + half + 1) * P],
                                       g.qs[half][:, b * NQ:(b + 1) * NQ],
                                       km[:, half, b, :, :].rearrange("p h k -> p (h k)"), start=True, stop=True)
                mm.then_inc(s_psum, 1)
            scores(0)
            scores(1)
            for n in range(G):
                values(2 * n + 1)
                pe.wait_ge(pn_ready, n + 1)
                pe.wait_ge(pT_ready, n)
                for half in range(2):
                    for k in range(GB):
                        mm = pe.transpose(pt[:, (half * GB + k) * NQ:(half * GB + k + 1) * NQ],
                                          pr[n % 2][:, k, half * 8:(half + 1) * 8, :].rearrange("p h k -> p (h k)"),
                                          g.ident[0:NQ, 0:NQ])
                mm.then_inc(pT_psum, 1)
                if n + 1 < G:
                    values(2 * n + 2)
                if n + 2 < G:
                    scores(n + 2)
                pe.wait_ge(pT_ready, n + 1)
                pe.wait_ge(v_ready, 2 * n + 2)
                if n >= 2:
                    pe.wait_ge(o_ready, n - 1)
                for half in range(2):
                    for k in range(GB):
                        mm = pe.matmul(po[n % 2][:, (half * GB + k) * NQ:(half * GB + k + 1) * NQ],
                                       vm[:, GB * n + k, half * P:(half + 1) * P],
                                       pT[n % 2][:, half, k * NQ:(k + 1) * NQ], start=True, stop=True)
                mm.then_inc(o_psum, 1)

        @block.scalar
        def _(act):
            act.wait_ge(eps_set, 1)
            act.wait_ge(v_var, 1)
            act.activation(krs[:, :], krs[:, :], ACT.Sqrt, scale=1.0 / HD0, bias=eps[:, 0:1]).then_inc(rooted, 1)
            for n in range(G):
                act.wait_ge(s_ready, n + 1)
                p2 = pr[n % 2][:, :, :, :].rearrange("p b h k -> p (b h k)")
                act.activation(p2, p2, ACT.Exp).then_inc(p_ready, 1)
                act.wait_ge(pT_psum, n + 1)
                if n >= 2:
                    act.wait_ge(o_psum, n - 1)
                act.activation(f(pT[n % 2]), pt[:, 0:2 * GB * NQ], ACT.Copy).then_inc(pT_ready, 1)
                act.wait_ge(o_psum, n + 1)
                act.activation(oT[:, :, n * GB * NQ:(n + 1) * GB * NQ],
                               po[n % 2][:, 0:2 * GB * NQ].rearrange("p (a n) -> p a n", a=2), ACT.Copy).then_inc(o_ready, 1)

        @block.gpsimd
        def _(pool):
            pool.memset(eps[:, :], 1e-6).then_inc(eps_set, 1)
            pool.wait_ge(y_in, 16)
            pool.tensor_copy(yrep[:, :, :, :], ydT[:, :].rearrange("p (b k) -> p b k", b=B).unsqueeze(2)
                             .broadcast_to([P, B, 8, DCA])).then_inc(rep_ready, 1)

        @block.vector
        def _(dve):
            kh = kk[:, :, :].rearrange("p t (h d) -> p (t h) d", d=HD0)
            sh = ksq[:, :, :].rearrange("p t (h d) -> p (t h) d", d=HD0)
            wide = lambda col: col.unsqueeze(2).broadcast_to([P, 2 * H, HD0])
            dve.wait_ge(k_psum, 1)
            dve.tensor_reduce(kmean[:, :], pt[:, :].rearrange("p (h d) -> p h d", d=HD0), X, ALU.add).then_inc(k_steps, 1)
            dve.wait_ge(k_steps, 1)
            dve.scalar_tensor_tensor(out=kh, in0=wide(kmean[:, :]), scalar=-1.0 / HD0,
                                     in1=pt[:, :].rearrange("p (h d) -> p h d", d=HD0), op0=ALU.mult, op1=ALU.add)\
               .then_inc(k_steps, 1)
            dve.wait_ge(k_steps, 2)
            dve.tensor_tensor(sh, kh, kh, ALU.mult).then_inc(k_steps, 1)
            dve.wait_ge(k_steps, 3)
            dve.tensor_reduce(krs[:, :], sh, X, ALU.add).then_inc(v_var, 1)
            dve.wait_ge(rooted, 1)
            dve.reciprocal(krs[:, :], krs[:, :]).then_inc(k_steps, 1)
            dve.wait_ge(k_steps, 4)
            dve.tensor_tensor(kh, kh, wide(krs[:, :]), ALU.mult).then_inc(k_steps, 1)

            def masked_values(n):
                dve.wait_ge(v_psum, n + 1)
                dve.tensor_tensor(vm[:, 2 * n:2 * n + 2, :].rearrange("p b (a c) -> p (b a) c", a=2),
                                  pv[:, :].rearrange("p (a c) -> p a c", a=4),
                                  g.blk[:, :].unsqueeze(1).broadcast_to([P, 4, P]), ALU.mult).then_inc(v_ready, 1)
            masked_values(0)
            dve.wait_ge(kT_psum, 1)
            for half in range(2):
                dve.tensor_scalar(kT[:, half, :], pt[:, half * NKD:(half + 1) * NKD], g.cols[:, half, 4:5], HD0 ** -0.5,
                                  ALU.mult, ALU.mult).then_inc(kT_ready, 1)
            dve.wait_ge(kT_ready, 2)
            for half in range(2):
                dve.tensor_tensor(km[:, half, :, :, :],
                                  kT[:, half, :].rearrange("p (b k) -> p b k", b=B).unsqueeze(2).broadcast_to([P, B, 8, DCA]),
                                  g.hmask[:, :].unsqueeze(1).unsqueeze(3).broadcast_to([P, B, 8, DCA]), ALU.mult)\
                   .then_inc(km_ready, 1)
            p3 = lambda n: pr[n % 2][:, :, :, :].rearrange("p b h k -> p (b h) k")
            along = lambda col: col.unsqueeze(2).broadcast_to([NQ, GB * H, DCA])

            def shift(n):
                s3 = sc[n % 2][0:NQ, :].rearrange("p (m k) -> p m k", k=DCA)
                dve.wait_ge(s_psum, n + 1)
                dve.tensor_reduce(smax[n % 2][:, :], s3, X, ALU.max).then_inc(s_max, 1)
                dve.wait_ge(s_max, n + 1)
                if n >= 2:
                    dve.wait_ge(pT_psum, n - 1)
                dve.tensor_tensor(p3(n), s3, along(smax[n % 2][:, :]), ALU.subtract).then_inc(s_ready, 1)
            shift(0)
            for n in range(G):
                masked_values(2 * n + 1)
                if n + 1 < G:
                    shift(n + 1)
                dve.wait_ge(p_ready, n + 1)
                dve.tensor_reduce(den[n % 2][:, :], p3(n), X, ALU.add).then_inc(p_sum, 1)
                dve.wait_ge(p_sum, n + 1)
                dve.reciprocal(den[n % 2][:, :], den[n % 2][:, :]).then_inc(p_inv, 1)
                dve.wait_ge(p_inv, n + 1)
                dve.tensor_tensor(p3(n), p3(n), along(den[n % 2][:, :]), ALU.mult).then_inc(pn_ready, 1)
                if n + 1 < G:
                    masked_values(2 * n + 2)


def phase_queries1(nc, g):
    with ExitStack() as ctx:
        sb = lambda n, s, d=F32: ctx.enter_context(nc.sbuf_tensor(f"q1_{n}", s, d))
        S = lambda n: g.sem(f"q1_{n}")
        two = lambda n, s: [sb(f"{n}{i}", s) for i in range(2)]
        wq, wk, wks = two("wq", [P, 2, P]), two("wk", [P, C]), two("wks", [P, C])
        scale, eps = sb("scale", [P, 3]), sb("eps", [P, 1])
        qT, sq, rq, qn = two("qT", [P, T]), two("sq", [P, T]), two("rq", [P, T]), two("qn", [P, T])
        qall = sb("qall", [P, B, HQ])
        ps = [ctx.enter_context(nc.psum_tensor(f"q1_ps{i}", [P, 2, 512], F32)) for i in range(4)]
        pq, psum, pout = [ps[0], ps[1]], ps[2], ps[3]
        wq_in, wk_in, sc_in = [S("wq_in0"), S("wq_in1")], [S("wk_in0"), S("wk_in1")], S("sc_in")
        sc_ready, wk_ready = S("sc_ready"), S("wk_ready")
        q_psum, q_ready, sq_ready = S("q_psum"), S("q_ready"), S("sq_ready")
        sum_psum, rooted, inverted, qn_ready = S("sum_psum"), S("rooted"), S("inverted"), S("qn_ready")
        out_psum, copied, stored = S("out_psum"), S("copied"), S("stored")
        block = ctx.enter_context(nc.Block())
        v2 = lambda t: t[:, :].rearrange("p (a n) -> p a n", a=2)
        LAG = 3

        def steps(step):
            for h in range(4):
                step(h, h // 2, h % 2, True, h >= 1, h >= LAG)
            yield
            for h in range(H, H + LAG):
                step(h, h // 2, h % 2, False, h == H, True)

        @block.sync
        def _(sp):
            with nc.allow_non_contiguous_dma(reason="columns of 128 scales"):
                sp.dma_start(scale[:, 0:1], g.a["gq"]).then_inc(sc_in, 16)
                sp.dma_start(scale[:, 1:2], g.a["gk"]).then_inc(sc_in, 16)
            for i in range(2):
                sp.dma_start(wq[i][:, :, :], g.a["L1_Wq"][i]).then_inc(wq_in[i], 16)
                sp.dma_start(wk[i][:, :], g.a["L1_WkT"][i]).then_inc(wk_in[i], 16)
            load_first_context(sp, g, KR1)
            with sp.Fori(0, H // 2 - 1) as u:
                for i in range(2):
                    sp.wait_ge(q_psum, 2 * u + i + 1)
                    sp.dma_start(wq[i][:, :, :], g.a["L1_Wq"][2 * u + i + 2]).then_inc(wq_in[i], 16)
                    sp.wait_ge(wk_ready, 2 * u + i + 1)
                    sp.dma_start(wk[i][:, :], g.a["L1_WkT"][2 * u + i + 2]).then_inc(wk_in[i], 16)
            for lo, hi in HEAD_GROUPS:
                cols = slice(lo * NQ, hi * NQ)
                sp.wait_ge(copied, hi + 2)
                sp.dma_start(g.qdram[1][:, :, cols].rearrange("b c n -> c b n"), qall[:, :, cols]).then_inc(stored, 16)
            sp.wait_ge(stored, 16 * len(HEAD_GROUPS))

        @block.tensor
        def _(pe):
            def step(h, pair, i, front, middle, back):
                if middle:
                    pe.wait_ge(sq_ready, h)
                    pe.wait_ge(rooted, h - 1)
                    for n in range(2):
                        mm = pe.matmul(psum[:, n, 0:HALF], g.ones[:, :], sq[1 - i][:, n * HALF:(n + 1) * HALF],
                                       start=True, stop=True)
                    mm.then_inc(sum_psum, 1)
                if front:
                    pe.wait_ge(wq_in[i], 16 * pair + 16)
                    if not isinstance(h, int) or h >= 2:
                        pe.wait_ge(q_ready, h - 1)
                    for n in range(2):
                        for k in range(2):
                            mm = pe.matmul(pq[i][:, n, 0:HALF], wq[i][:, k, :],
                                           g.xnT[:, k, n * HALF:(n + 1) * HALF], start=(k == 0), stop=(k == 1))
                    mm.then_inc(q_psum, 1)
                if back:
                    pe.wait_ge(qn_ready, h - LAG + 1)
                    pe.wait_ge(wk_ready, h - LAG + 1)
                    pe.wait_ge(copied, h - LAG + 2)
                    for n in range(2):
                        mm = pe.matmul(pout[:, n, 0:HALF], wks[1 - i][:, :], qn[1 - i][:, n * HALF:(n + 1) * HALF],
                                       start=True, stop=True)
                    mm.then_inc(out_psum, 1)
            s = steps(step)
            next(s)
            with pe.Fori(0, H // 2 - 2) as u:
                for i in range(2):
                    step(2 * u + 4 + i, u + 2, i, True, True, True)
            for _ in s:
                pass

        @block.scalar
        def _(act):
            act.wait_ge(sc_ready, 2)
            def step(h, pair, i, front, middle, back):
                if middle:
                    act.wait_ge(sum_psum, h)
                    if not isinstance(h, int) or h >= 3:
                        act.wait_ge(qn_ready, h - 2)
                    act.activation(v2(rq[1 - i]), psum[:, :, 0:HALF], ACT.Sqrt, scale=1.0 / HD1, bias=eps[:, 0:1])\
                       .then_inc(rooted, 1)
                if front:
                    act.wait_ge(q_psum, h + 1)
                    if not isinstance(h, int) or h >= 2:
                        act.wait_ge(qn_ready, h - 1)
                    act.activation(sq[i][:, :].rearrange("p (a n) -> p a n", a=2), pq[i][:, :, 0:HALF], ACT.Square)\
                       .then_inc(sq_ready, 1)
                    act.activation(v2(qT[i]), pq[i][:, :, 0:HALF], ACT.Copy).then_inc(q_ready, 1)
                if back:
                    act.wait_ge(out_psum, h - LAG + 1)
                    for n in range(2):
                        ins = act.activation(qall[:, 8 * n:8 * n + 8, bass.ds((h - LAG) * NQ, NQ)],
                                             pout[:, n, 0:HALF].rearrange("p (b q) -> p b q", q=NQ), ACT.Copy)
                    ins.then_inc(copied, 1)
            s = steps(step)
            next(s)
            with act.Fori(0, H // 2 - 2) as u:
                for i in range(2):
                    step(2 * u + 4 + i, u + 2, i, True, True, True)
            for _ in s:
                pass

        @block.vector
        def _(dve):
            dve.memset(eps[:, :], 1e-5).then_inc(sc_ready, 1)
            dve.wait_ge(sc_in, 32)
            dve.tensor_scalar(scale[:, 2:3], scale[:, 0:1], scale[:, 1:2], HD1 ** -0.5,
                              ALU.mult, ALU.mult).then_inc(sc_ready, 1)
            dve.wait_ge(sc_ready, 2)
            with dve.Fori(0, H // 2) as u:
                for i in range(2):
                    h = 2 * u + i
                    dve.wait_ge(rooted, h + 1)
                    dve.reciprocal(rq[i][:, :], rq[i][:, :]).then_inc(inverted, 1)
                    dve.wait_ge(wk_in[i], 16 * u + 16)
                    dve.wait_ge(copied, h + 1)
                    dve.tensor_scalar(wks[i][:, :], wk[i][:, :], scale[:, 2:3], None, ALU.mult).then_inc(wk_ready, 1)

        @block.gpsimd
        def _(pool):
            pool.sem_inc(copied, 2)
            with pool.Fori(0, H // 2) as u:
                for i in range(2):
                    h = 2 * u + i
                    pool.wait_ge(inverted, h + 1)
                    pool.wait_ge(copied, h + 1)
                    pool.tensor_tensor(qn[i][:, :], qT[i][:, :], rq[i][:, :], ALU.mult).then_inc(qn_ready, 1)


def first_context(nc, g, ctx, layer):
    sb = lambda n, s: ctx.enter_context(nc.sbuf_tensor(f"a{layer}_{n}", s, F32))
    g.yT, g.y1 = sb("yT", [P, SEQ]), [sb(f"y1{i}", [P, NK, C + 1]) for i in range(2)]
    g.yT_in, g.y1_in = g.sem(f"a{layer}_yT_in"), [g.sem(f"a{layer}_y1_in0"), g.sem(f"a{layer}_y1_in1")]


def load_rows(sp, g, b, i, KR):
    sp.dma_start(g.y1[i][:, 0:NK - 1, 0:C],
                 g.a["ctx"][b, 0:(NK - 1) * P, :].rearrange("(j p) c -> p j c", p=P)).then_inc(g.y1_in[i], 16)
    sp.dma_start(g.y1[i][0:KR, NK - 1, 0:C],
                 g.a["ctx"][b, (NK - 1) * P:(NK - 1) * P + KR, :]).then_inc(g.y1_in[i], 16)


def load_first_context(sp, g, KR):
    sp.dma_start(g.yT[:, :], g.a["ctxT"][0]).then_inc(g.yT_in, 16)
    for i in range(2):
        load_rows(sp, g, i, i, KR)


def phase_attention(nc, g, layer):
    KR = KR1 if layer else KR0
    rows = lambda j: P if j < NK - 1 else KR
    AT = NK // 2
    PART = [(0, AT * P), (AT * P, SEQ)]
    LAG = 3
    SC = 2 * NK
    USES = SC + 2
    OI = [(0, 3), (3, 6), (6, 7)]
    TI = [(0, 4), (4, 7)]
    qd, od = g.qdram[layer], g.odram[layer]
    with ExitStack() as ctx:
        sb = lambda n, s, d=F32: ctx.enter_context(nc.sbuf_tensor(f"a{layer}_{n}", s, d))
        two = lambda n, s, d=F32: [sb(f"{n}{i}", s, d) for i in range(2)]
        yT, y1, yT_in, y1_in = g.yT, g.y1, g.yT_in, g.y1_in
        yh, yl = sb("yh", [P, SEQ], F32R), sb("yl", [P, SEQ], F32R)
        Q, Qh, Ql = sb("Q", [P, HQ]), two("Qh", [P, HQ], F32R), two("Ql", [P, HQ], F32R)
        if not layer:
            bias, ones3 = two("bias", [3, HQ], BF16), sb("ones3", [3, P], BF16)
        S = two("S", [P, NK, HQ])
        mx, mb = sb("mx", [P, HQ]), sb("mb", [P, HQ])
        mcol, mh, ml = sb("mcol", [P, FT]), sb("mh", [P, FT], F32R), sb("ml", [P, FT], F32R)
        identr = sb("identr", [P, P], F32R)
        rden, on, oT = sb("rden", [P, FT]), sb("on", [P, FT, C]), sb("oT", [P, HQ])
        ring = [ctx.enter_context(nc.psum_tensor(f"a{layer}_ring{i}", [P, 512], F32)) for i in range(RING)]
        tb = ctx.enter_context(nc.psum_tensor(f"a{layer}_tb", [P, 512], F32))
        ob = [ctx.enter_context(nc.psum_tensor(f"a{layer}_ob{i}", [P, 512], F32)) for i in range(3)]
        N = lambda n: g.sem(f"a{layer}_{n}")
        q_in, bias_in = N("q_in"), [N("bias_in0"), N("bias_in1")]
        one_set, y_high, y_split, q_high, q_split = N("one_set"), N("y_high"), N("y_split"), N("q_high"), N("q_split")
        s_ready, s_scaled, mx_ready = N("s_ready"), N("s_scaled"), N("mx_ready")
        mT_ready, mT_taken, m_high, m_split = N("mT_ready"), N("mT_taken"), N("m_high"), N("m_split")
        mb_psum, mb_ready, shifted = N("mb_psum"), N("mb_ready"), N("shifted")
        p_ready, p_used = N("p_ready"), N("p_used")
        rden_ready, on_ready = N("rden_ready"), N("on_ready")
        oT_ready, oT_copied, stored = N("oT_ready"), N("oT_copied"), N("stored")
        block = ctx.enter_context(nc.Block())
        from_ = lambda b, least: not isinstance(b, int) or b >= least

        def steps(step):
            step(0, 0, 0, True, True, False, False)
            step(1, 0, 1, True, True, True, False)
            yield
            step(B - 2, B // 2 - 1, 0, True, True, True, True)
            step(B - 1, B // 2 - 1, 1, True, False, True, True)
            step(B, B // 2, 0, False, False, True, True)
            step(B + 1, B // 2, 1, False, False, False, True)

        @block.sync
        def _(sp):
            def load_queries(b, i):
                sp.dma_start(Q[:, :], qd[b]).then_inc(q_in, 16)
                if not layer:
                    sp.dma_start(bias[i][:, :], g.bdram[b]).then_inc(bias_in[i], 16)

            def load_next(b, i):
                sp.wait_ge(y_split, 2 * b)
                sp.wait_ge(q_split, b)
                sp.dma_start(yT[:, :], g.a["ctxT"][b]).then_inc(yT_in, 16)
                load_queries(b, i)

            def refill(b, i):
                sp.wait_ge(p_used, NK * (b - 1))
                load_rows(sp, g, b, i, KR)
            load_queries(0, 0)
            load_next(1, 1)
            load_next(2, 0)
            with sp.Fori(0, B // 2 - 2) as u:
                for i in range(2):
                    refill(2 * u + 2 + i, i)
                    load_next(2 * u + 3 + i, 1 - i)
            refill(B - 2, 0)
            load_next(B - 1, 1)
            refill(B - 1, 1)
            sp.wait_ge(stored, 16 * B)

        @block.tensor
        def _(pe):
            def step(b, pair, i, front, nxt, back, end):
                def scores(j):
                    n = rows(j)
                    if j == 0:
                        pe.wait_ge(y_split, 2 * b + 1)
                        pe.wait_ge(q_split, b + 1)
                        if not layer:
                            pe.wait_ge(bias_in[i], 16 * pair + 16)
                    if j == AT:
                        pe.wait_ge(y_split, 2 * b + 2)
                    for half in range(2):
                        use = 2 * j + half + (2 if j >= 2 else 0)
                        r = (USES * i + use) % RING
                        if use < 4:
                            if from_(b, 1):
                                pe.wait_ge(s_scaled, SC * b - 3 + use)
                        elif use in (8, 9):
                            if from_(b, 1):
                                pe.wait_ge(mb_ready, 2 * (b - 1) + use - 7)
                        else:
                            pe.wait_ge(s_scaled, SC * b + (use - 4 if use < 8 else use - 6) + 1)
                        cols = slice(half * HALF, (half + 1) * HALF)
                        dst = ring[r][0:n, 0:HALF]
                        high, low = yh[:, j * P:j * P + n], yl[:, j * P:j * P + n]
                        pe.matmul(dst, high, Qh[i][:, cols], start=True, stop=False)
                        pe.matmul(dst, high, Ql[i][:, cols], start=False, stop=False)
                        mm = pe.matmul(dst, low, Qh[i][:, cols], start=False, stop=bool(layer))
                        if not layer:
                            mm = pe.matmul(dst, ones3[:, 0:n], bias[i][:, cols], start=False, stop=True)
                        mm.then_inc(s_ready, 1)

                def output(bb, j, k_):
                    n = rows(j)
                    pe.wait_ge(p_ready, NK * bb + j + 1)
                    for k, (lo, hi) in enumerate(OI):
                        for q in range(lo, hi):
                            mm = pe.matmul(ob[k][:, (q - lo) * (C + 1):(q - lo + 1) * (C + 1)],
                                           S[k_][0:n, j, q * P:(q + 1) * P], y1[k_][0:n, j, :],
                                           start=(j == 0 and q == lo), stop=(j == NK - 1),
                                           skip_group_check=True)
                    mm.then_inc(p_used, 1)

                def maxima(k):
                    if k:
                        pe.wait_ge(mT_taken, 2 * (b - 1) + 1)
                    else:
                        pe.wait_ge(mx_ready, NK * b)
                        if from_(b, 3):
                            pe.wait_ge(oT_copied, 2 * (b - 2))
                    lo, hi = TI[k]
                    for q in range(lo, hi):
                        mm = pe.transpose(tb[:, (q - lo) * P:(q - lo + 1) * P], mx[:, q * P:(q + 1) * P], g.ident[:, :])
                    mm.then_inc(mT_ready, 1)

                def spread():
                    pe.wait_ge(m_split, b)
                    for half in range(2):
                        if front:
                            pe.wait_ge(s_scaled, SC * b + half + 1)
                        r = (USES * i + 4 + half) % RING
                        for q in range(3 * half, 4 + 3 * half):
                            lo, hi = max(q * P, half * HALF), min((q + 1) * P, (half + 1) * HALF)
                            for m in (mh, ml):
                                mm = pe.matmul(ring[r][:, lo - half * HALF:hi - half * HALF],
                                               m[:, q:q + 1].broadcast_to([P, P]), identr[:, lo - q * P:hi - q * P],
                                               start=(m is mh), stop=(m is ml), skip_group_check=True)
                        mm.then_inc(mb_psum, 1)

                def transposes_out(k):
                    lo, hi = TI[k]
                    pe.wait_ge(on_ready, 3 * (b - 1))
                    if k:
                        pe.wait_ge(oT_copied, 2 * (b - 2) + 1)
                    else:
                        pe.wait_ge(mT_taken, 2 * b if back else 2 * B)
                    for q in range(lo, hi):
                        mm = pe.transpose(tb[:, (q - lo) * P:(q - lo + 1) * P], on[:, q, :], g.ident[:, :])
                    mm.then_inc(oT_ready, 1)

                for j in range(NK):
                    if front:
                        scores(j)
                    if back and j == 0:
                        maxima(0)
                    if end and j < LAG:
                        for t in ((NK - LAG - 1 + j,) if j < LAG - 1 else (NK - 2, NK - 1)):
                            output(b - 2, t, i)
                    if back and j == 0:
                        maxima(1)
                    if back and j == 1:
                        spread()
                    if back and j > LAG:
                        if j == LAG + 1:
                            pe.wait_ge(y1_in[1 - i], 32 * (pair + i))
                            if from_(b, 2):
                                pe.wait_ge(on_ready, 3 * (b - 1))
                        output(b - 1, j - LAG - 1, 1 - i)
                    if end and j in (LAG + 1, LAG + 2):
                        transposes_out(j - LAG - 1)
            pe.wait_ge(one_set, 4)
            s = steps(step)
            next(s)
            with pe.Fori(0, B // 2 - 2) as u:
                for i in range(2):
                    step(2 * u + 2 + i, u + 1, i, True, True, True, True)
            for _ in s:
                pass

        @block.vector
        def _(dve):
            if not layer:
                dve.memset(ones3[:, :], 1.0).then_inc(one_set, 1)
            for i in range(2):
                dve.memset(y1[i][:, :, C:C + 1], 1.0).then_inc(one_set, 1)
            if layer:
                dve.sem_inc(one_set, 1)
            dve.tensor_copy(identr[:, :], g.ident[:, :]).then_inc(one_set, 1)
            dve.wait_ge(one_set, 4)
            hoff = 0 if layer else H

            def low_q(b, i):
                dve.wait_ge(q_high, b + 1)
                dve.tensor_tensor(Ql[i][:, :], Q[:, :], Qh[i][:, :], ALU.subtract).then_inc(q_split, 1)

            def step(b, pair, i, front, nxt, back, end):
                for j in range(NK):
                    n = rows(j)
                    if end and j == LAG:
                        dve.wait_ge(p_used, NK * (b - 1))
                        if from_(b, 3):
                            dve.wait_ge(oT_ready, 2 * (b - 2))
                        for k, (lo, hi) in enumerate(OI):
                            den = ob[k][:, 0:(hi - lo) * (C + 1)].rearrange("p (a n) -> p a n", n=C + 1)
                            ins = dve.reciprocal(rden[:, lo:hi], den[:, :, C])
                        ins.then_inc(rden_ready, 1)
                        dve.wait_ge(rden_ready, b - 1)
                        for k, (lo, hi) in enumerate(OI):
                            den = ob[k][:, 0:(hi - lo) * (C + 1)].rearrange("p (a n) -> p a n", n=C + 1)
                            dve.tensor_tensor(on[:, lo:hi, :], den[:, :, 0:C],
                                              rden[:, lo:hi].unsqueeze(2).broadcast_to([P, hi - lo, C]), ALU.mult)\
                               .then_inc(on_ready, 1)
                    if front:
                        if from_(b, 2):
                            dve.wait_ge(p_used, NK * (b - 2) + j + 1)
                        for half in range(2):
                            r = (USES * i + 2 * j + half + (2 if j >= 2 else 0)) % RING
                            dve.wait_ge(s_ready, SC * b + 2 * j + half + 1)
                            rk = g.rk[0:n, b, j, hoff + 8 * half:hoff + 8 * half + 8]
                            dve.tensor_tensor(
                                S[i][0:n, j, half * HALF:(half + 1) * HALF].rearrange("p (h q) -> p h q", h=8),
                                ring[r][0:n, 0:HALF].rearrange("p (h q) -> p h q", h=8),
                                rk.unsqueeze(2).broadcast_to([n, 8, NQ]), ALU.mult).then_inc(s_scaled, 1)
                    if back and j == 0:
                        for k, (lo, hi) in enumerate(TI):
                            dve.wait_ge(mT_ready, 2 * (b - 1) + k + 1)
                            dve.tensor_reduce(mcol[:, lo:hi],
                                              tb[:, 0:(hi - lo) * P].rearrange("p (a n) -> p a n", n=P),
                                              X, ALU.max).then_inc(mT_taken, 1)
                        dve.wait_ge(mT_taken, 2 * b)
                        if from_(b, 2):
                            dve.wait_ge(mb_psum, 2 * (b - 1))
                        dve.tensor_copy(mh[:, :], mcol[:, :]).then_inc(m_high, 1)
                        dve.wait_ge(m_high, b)
                        dve.tensor_tensor(ml[:, :], mcol[:, :], mh[:, :], ALU.subtract).then_inc(m_split, 1)
                    if front:
                        dve.wait_ge(s_scaled, SC * b + 2 * j + 2)
                        if j == 0:
                            dve.tensor_copy(mx[:, :], S[i][:, 0, :]).then_inc(mx_ready, 1)
                        else:
                            dve.wait_ge(mx_ready, NK * b + j)
                            dve.tensor_tensor(mx[0:n, :], mx[0:n, :], S[i][0:n, j, :], ALU.max).then_inc(mx_ready, 1)
                    if nxt and j == NK - 3:
                        low_q(b + 1, 1 - i)
            low_q(0, 0)
            s = steps(step)
            next(s)
            with dve.Fori(0, B // 2 - 2) as u:
                for i in range(2):
                    step(2 * u + 2 + i, u + 1, i, True, True, True, True)
            for _ in s:
                pass

        @block.gpsimd
        def _(pool):
            def low_y(b, part):
                lo, hi = PART[part]
                pool.wait_ge(y_high, 2 * b + part + 1)
                pool.tensor_tensor(yl[:, lo:hi], yT[:, lo:hi], yh[:, lo:hi], ALU.subtract).then_inc(y_split, 1)

            def step(b, pair, i, front, nxt, back, end):
                for j in range(NK):
                    n = rows(j)
                    if nxt and j == AT:
                        low_y(b + 1, 0)
                    if back:
                        if j == 0:
                            pool.wait_ge(mb_ready, 2 * b)
                        pool.tensor_tensor(S[1 - i][0:n, j, :], S[1 - i][0:n, j, :], mb[0:n, :], ALU.subtract)\
                            .then_inc(shifted, 1)
                if nxt:
                    low_y(b + 1, 1)
            for part in range(2):
                low_y(0, part)
            s = steps(step)
            next(s)
            with pool.Fori(0, B // 2 - 2) as u:
                for i in range(2):
                    step(2 * u + 2 + i, u + 1, i, True, True, True, True)
            for _ in s:
                pass

        @block.scalar
        def _(act):
            def high_y(b, part):
                lo, hi = PART[part]
                act.wait_ge(yT_in, 16 * b + 16)
                if from_(b, 1):
                    act.wait_ge(s_ready, SC * (b - 1) + (NK if part == 0 else SC))
                act.activation(yh[:, lo:hi], yT[:, lo:hi], ACT.Copy).then_inc(y_high, 1)

            def high_q(b, i):
                act.wait_ge(q_in, 16 * b + 16)
                act.activation(Qh[i][:, :], Q[:, :], ACT.Copy).then_inc(q_high, 1)

            def step(b, pair, i, front, nxt, back, end):
                if back:
                    if from_(b, 2):
                        act.wait_ge(shifted, NK * (b - 1))
                    for half in range(2):
                        r = (USES * i + 4 + half) % RING
                        act.wait_ge(mb_psum, 2 * (b - 1) + half + 1)
                        act.activation(mb[:, half * HALF:(half + 1) * HALF], ring[r][:, 0:HALF], ACT.Copy)\
                           .then_inc(mb_ready, 1)
                for j in range(NK):
                    n = rows(j)
                    if back:
                        act.wait_ge(shifted, NK * (b - 1) + j + 1)
                        act.activation(S[1 - i][0:n, j, :], S[1 - i][0:n, j, :], ACT.Exp).then_inc(p_ready, 1)
                    if end and j in (1, 2):
                        k = j - 1
                        lo, hi = TI[k]
                        if k == 0 and from_(b, 3):
                            act.wait_ge(stored, 16 * (b - 2))
                        act.wait_ge(oT_ready, 2 * (b - 2) + k + 1)
                        act.activation(oT[:, lo * P:hi * P], tb[:, 0:(hi - lo) * P], ACT.Copy).then_inc(oT_copied, 1)
                        if k:
                            act.wait_ge(oT_copied, 2 * (b - 1))
                            act.dma_start(od[b - 2], oT[:, :]).then_inc(stored, 16)
                    if nxt and j == AT - 2:
                        high_y(b + 1, 0)
                        high_q(b + 1, 1 - i)
                if nxt:
                    high_y(b + 1, 1)
            high_q(0, 0)
            for part in range(2):
                high_y(0, part)
            s = steps(step)
            next(s)
            with act.Fori(0, B // 2 - 2) as u:
                for i in range(2):
                    step(2 * u + 2 + i, u + 1, i, True, True, True, True)
            for _ in s:
                pass


def phase_project0(nc, g):
    with ExitStack() as ctx:
        sb = lambda n, s, d=F32: ctx.enter_context(nc.sbuf_tensor(f"p0_{n}", s, d))
        N = lambda n: g.sem(f"p0_{n}")
        NB = B // 2
        v0, wv, wo = sb("v0", [P, D]), sb("wv", [P, 2, 8, P]), sb("wo", [P, 2, D])
        bv, bvs, bo = sb("bv", [P, 2, 2]), sb("bvs", [P, 2]), sb("bo", [TT, D])
        od, ov = sb("od", [P, 2, T]), sb("ov", [P, 2, T])
        ot = [sb(f"ot{i}", [P, NB, HQ]) for i in range(2)]
        pv = [ctx.enter_context(nc.psum_tensor(f"p0_pv{i}", [P, 512], F32)) for i in range(4)]
        po = [ctx.enter_context(nc.psum_tensor(f"p0_po{i}", [P, 512], F32)) for i in range(4)]
        w_in, v_in, b_in, od_in, ot_in = N("w_in"), N("v_in"), N("b_in"), N("od_in"), [N(f"ot_in{i}") for i in range(4)]
        zeroed, masked, bias_ready = N("zeroed"), N("masked"), N("bias_ready")
        v_psum, ov_ready = N("v_psum"), N("ov_ready")
        o_psum, added = N("o_psum"), N("added")
        block = ctx.enter_context(nc.Block())

        @block.sync
        def _(sp):
            sp.dma_start(v0[:, :], g.a["L0_Wv"]).then_inc(v_in, 16)

            def load(half, k):
                cols = slice(k * HALF, (k + 1) * HALF)
                sp.dma_start(ot[half][:, :, cols], g.odram[0][half * NB:(half + 1) * NB, :, cols].rearrange("b c n -> c b n"))\
                    .then_inc(ot_in[2 * half + k], 16)
            load(0, 0)
            load(0, 1)
            sp.dma_start(bv[:, :, :], g.a["bv0"]).then_inc(b_in, 16)
            sp.dma_start(bo[:, :], g.a["bo0"]).then_inc(b_in, 16)
            sp.dma_start(od[:, :, :], g.ddram).then_inc(od_in, 16)
            load(1, 0)
            load(1, 1)
            sp.dma_start(wo[:, :, :], g.a["L0_Wo"]).then_inc(w_in, 16)

        @block.tensor
        def _(pe):
            pe.wait_ge(masked, 1)
            for half in range(2):
                for k in range(2):
                    pe.wait_ge(ot_in[2 * half + k], 16)
                    for h in range(8):
                        mm = pe.matmul(pv[2 * half + k][:, 0:HALF].rearrange("p (b q) -> p b q", b=NB),
                                       wv[:, k, h, :], ot[half][:, :, (8 * k + h) * NQ:(8 * k + h + 1) * NQ],
                                       start=(h == 0), stop=(h == 7))
                    mm.then_inc(v_psum, 1)
            pe.wait_ge(w_in, 16)
            for m in range(NT // 2):
                pe.wait_ge(ov_ready, 2 if m < 2 else 4)
                for i in range(2):
                    t = 2 * m + i
                    for k in range(2):
                        mm = pe.matmul(po[m][0:TT, i * D:(i + 1) * D], ov[:, k, t * TT:(t + 1) * TT], wo[:, k, :],
                                       start=(k == 0), stop=(k == 1))
                mm.then_inc(o_psum, 1)

        @block.gpsimd
        def _(pool):
            pool.memset(wv[:, :, :, :], 0.0).then_inc(zeroed, 1)

        @block.vector
        def _(dve):
            dve.wait_ge(v_in, 16)
            dve.wait_ge(zeroed, 1)
            for h in range(H):
                ins = dve.tensor_copy(wv[:, h // 8, h % 8, (h % 8) * HD0:(h % 8 + 1) * HD0], v0[:, h * HD0:(h + 1) * HD0])
            ins.then_inc(masked, 1)
            dve.wait_ge(b_in, 32)
            dve.tensor_tensor(bvs[:, :], bv[:, 0, :], bv[:, 1, :], ALU.add).then_inc(bias_ready, 1)
            dve.tensor_tensor(g.x[:, :, :], g.x[:, :, :], bo[:, :].unsqueeze(1).broadcast_to([TT, NT, D]), ALU.add)\
               .then_inc(added, 1)
            dve.wait_ge(bias_ready, 1)
            dve.wait_ge(od_in, 16)
            for half in range(2):
                for k in range(2):
                    cols = slice(half * HALF, (half + 1) * HALF)
                    dve.wait_ge(v_psum, 2 * half + k + 1)
                    dve.scalar_tensor_tensor(out=ov[:, k, cols], in0=pv[2 * half + k][:, 0:HALF], scalar=bvs[:, k:k + 1],
                                             in1=od[:, k, cols], op0=ALU.add, op1=ALU.add).then_inc(ov_ready, 1)
            dve.wait_ge(added, 1)
            for m in range(NT // 2):
                dve.wait_ge(o_psum, m + 1)
                xs = g.x[:, 2 * m:2 * m + 2, :]
                dve.tensor_tensor(xs, xs, po[m][0:TT, :].rearrange("p (a n) -> p a n", a=2), ALU.add).then_inc(added, 1)


def phase_project1(nc, g):
    with ExitStack() as ctx:
        sb = lambda n, s, d=F32: ctx.enter_context(nc.sbuf_tensor(f"p1_{n}", s, d))
        N = lambda n: g.sem(f"p1_{n}")
        NB, NM = B // 2, H // 2
        M, wv, wo = sb("M", [P, H, D]), sb("wv", [P, H, C]), sb("wo", [P, H, D])
        ot = [sb(f"ot{i}", [P, NB, HQ]) for i in range(2)]
        sumT = sb("sumT", [P, 2, T])
        ps = [ctx.enter_context(nc.psum_tensor(f"p1_ps{i}", [P, 512], F32)) for i in range(8)]
        w_in, ot_in = N("w_in"), [N("ot_in0"), N("ot_in1")]
        m_psum, m_copied, acc_ready, sum_ready, back, added = [
            N(n) for n in ("m_psum", "m_copied", "acc_ready", "sum_ready", "back", "added")]
        block = ctx.enter_context(nc.Block())

        @block.sync
        def _(sp):
            sp.dma_start(wv[:, :, :], g.a["L1_WvT"].rearrange("h d c -> d h c")).then_inc(w_in, 16)
            sp.dma_start(wo[:, :, :], g.a["L1_Wo"].rearrange("h d n -> d h n")).then_inc(w_in, 16)
            for half in range(2):
                sp.dma_start(ot[half][:, :, :], g.odram[1][half * NB:(half + 1) * NB].rearrange("b c n -> c b n"))\
                    .then_inc(ot_in[half], 16)
            load_ternary(sp, g)

        @block.tensor
        def _(pe):
            pe.wait_ge(w_in, 32)
            for m in range(NM):
                if m >= 4:
                    pe.wait_ge(m_copied, m - 3)
                for k in range(2):
                    h = 2 * m + k
                    mm = pe.matmul(ps[m % 4][:, k * D:(k + 1) * D], wv[:, h, :], wo[:, h, :], start=True, stop=True)
                mm.then_inc(m_psum, 1)
            pe.wait_ge(m_copied, NM)
            for half in range(2):
                pe.wait_ge(ot_in[half], 16)
                for h in range(H):
                    for dk in range(2):
                        mm = pe.matmul(ps[4 + 2 * half + dk][:, 0:HALF].rearrange("p (b q) -> p b q", b=NB),
                                       M[:, h, dk * P:(dk + 1) * P], ot[half][:, :, h * NQ:(h + 1) * NQ],
                                       start=(h == 0), stop=(h == H - 1), skip_group_check=True)
                mm.then_inc(acc_ready, 1)
                if half == 0:
                    pe.wait_ge(g.wabs_sums, 3)
                    pe.matmul(ps[0][:, 0:3], g.ones[:, :], g.wabs[:, :], start=True, stop=True).then_inc(g.wsum_psum, 1)
            pe.wait_ge(g.w_steps, 1)
            for m in range(NT // 2):
                pe.wait_ge(sum_ready, 2 if m < 2 else 4)
                for k in range(2):
                    t = 2 * m + k
                    for dk in range(2):
                        mm = pe.transpose(ps[m][0:TT, (2 * k + dk) * P:(2 * k + dk + 1) * P],
                                          sumT[:, dk, t * TT:(t + 1) * TT], g.ident[:, :])
                mm.then_inc(back, 1)

        @block.gpsimd
        def _(pool):
            pool.memset(g.wf[2][:, FT - 1, :], 0.0).then_inc(g.wd_zero, 1)

        @block.scalar
        def _(act):
            for m in range(1, NM, 2):
                act.wait_ge(m_psum, m + 1)
                act.wait_ge(m_copied, m)
                act.activation(M[:, 2 * m:2 * m + 2, :].rearrange("p a n -> p (a n)"), ps[m % 4][:, :], ACT.Copy)\
                    .then_inc(m_copied, 1)

        @block.vector
        def _(dve):
            for m in range(0, NM, 2):
                dve.wait_ge(m_psum, m + 1)
                if m:
                    dve.wait_ge(m_copied, m)
                dve.tensor_copy(M[:, 2 * m:2 * m + 2, :].rearrange("p a n -> p (a n)"), ps[m % 4][:, :])\
                    .then_inc(m_copied, 1)
            sum_ternary(dve, g)
            for half in range(2):
                dve.wait_ge(acc_ready, half + 1)
                for dk in range(2):
                    dve.tensor_copy(sumT[:, dk, half * HALF:(half + 1) * HALF], ps[4 + 2 * half + dk][:, 0:HALF])\
                        .then_inc(sum_ready, 1)
                if half == 0:
                    round_ternary(dve, g, ps[0][:, 0:3])
            for m in range(NT // 2):
                dve.wait_ge(back, m + 1)
                xs = g.x[:, 2 * m:2 * m + 2, :]
                dve.tensor_tensor(xs, xs, ps[m][0:TT, :].rearrange("p (a n) -> p a n", a=2), ALU.add).then_inc(added, 1)


def phase_moe(nc, g):
    SLOTS = E * CAP
    NOE = 99.0
    with ExitStack() as ctx:
        sb = lambda n, s, d=F32: ctx.enter_context(nc.sbuf_tensor(f"m_{n}", s, d))
        N = lambda n: g.sem(f"m_{n}")
        r3 = lambda n: sb(n, [TT, NT, E])
        gw, gb, eid, trash, low = sb("gw", [P, 2, E]), sb("gb", [TT, E]), sb("eid", [TT, E]), \
            sb("trash", [TT, 2, NT]), sb("low", [TT, TT])
        lg, ab, ex, up, ln, dd, sc, sk = [r3(n) for n in ("lg", "ab", "ex", "up", "ln", "dd", "sc", "sk")]
        oh, tmp, A, pos = [r3("oh0"), r3("oh1")], r3("tmp"), r3("A"), r3("pos")
        mcol, ei, w, den = sb("mcol", [TT, NT]), sb("ei", [TT, 2, NT]), sb("w", [TT, 2, NT]), sb("den", [TT, NT])
        ps_, valid, base, sidx, gidx = [sb(n, [TT, 2, NT]) for n in ("pcol", "valid", "base", "sidx", "gidx")]
        su, gu = sb("su", [TT, 2 * NT], U32), sb("gu", [TT, 2 * NT], U32)
        zero = sb("zero", [P, 2048])
        FB = FF - P
        w13 = sb("w13", [P, E + 1, 2, 2, FF])
        w2a, w2b = sb("w2a", [P, E + 1, D]), sb("w2b", [FB, E + 1, D])
        xe, xeT, ye = [[sb(f"{n}{i}", [P, 2 * P]) for i in range(2)] for n in ("xe", "xeT", "ye")]
        th, he = [[sb(f"{n}{i}", [P, FF]) for i in range(2)] for n in ("th", "he")]
        heT = [sb(f"heT{i}", [P, 2, P]) for i in range(2)]
        hs, ts = sb("hs", [P, 2, T]), sb("ts", [P, T])
        yg = sb("yg", [TT, 2 * NT, D])
        ps = [ctx.enter_context(nc.psum_tensor(f"m_ps{i}", [P, 512], F32)) for i in range(8)]
        c_in, w_in, x_in = N("c_in"), [N("w_in0"), N("w_in1")], [N("x_in0"), N("x_in1")]
        shared_in = N("shared_in")
        zeroed, zero_out, scattered = N("zeroed"), N("zero_out"), N("scattered")
        gathered = [N("gathered0"), N("gathered1")]
        lg_psum, act_steps, steps, count_psum = N("lg_psum"), N("act_steps"), N("router_steps"), N("count_psum")
        sh_psum, sh_tanh, sh_steps, sh_out, sh_added = N("sh_psum"), N("sh_tanh"), N("sh_steps"), N("sh_out"), N("sh_added")
        side = N("side_steps")
        xT_psum, xT_ready, gu_psum, e_tanh, gated, h_ready, hT_psum, hT_ready, y_psum, y_ready = [
            N(n) for n in ("xT_psum", "xT_ready", "gu_psum", "e_tanh", "gated", "h_ready", "hT_psum", "hT_ready",
                           "y_psum", "y_ready")]
        y_stored, summed = [N("y_stored0"), N("y_stored1")], N("summed")
        block = ctx.enter_context(nc.Block())
        xbuf, ybuf = g.xbuf, g.ybuf
        bT, bGU, bH, bY = [(ps[k], ps[k + 1]) for k in (0, 2, 4, 6)]
        SPLIT = [(0, E // 2), (E // 2, E)]
        from_ = lambda e, least: not isinstance(e, int) or e >= least

        def stages(step):
            for n in range(4):
                step(n, n // 2, n % 2)
            yield
            for n in range(E, E + 3):
                step(n, n // 2, n % 2)
        at_stage = lambda n, lag: not isinstance(n, int) or lag <= n < E + lag

        @block.sync
        def _(sp):
            consts = [(gw, g.a["gw"]), (gb, g.a["gb"]), (eid, g.a["eid"]), (trash, g.a["trash"]), (low, g.a["low"])]
            for dst, src in consts:
                sp.dma_start(dst[tuple(slice(None) for _ in dst.shape)], src).then_inc(c_in, 16)

            def load_w(lo, hi, sem):
                sp.dma_start(w13[:, lo:hi, :, :, :], g.a["W13"][:, lo:hi]).then_inc(sem, 16)
                sp.dma_start(w2a[:, lo:hi, :], g.a["W2a"][:, lo:hi]).then_inc(sem, 16)
                sp.dma_start(w2b[:, lo:hi, :], g.a["W2b"][:, lo:hi]).then_inc(sem, 16)
            load_w(E, E + 1, shared_in)
            sp.wait_ge(zeroed, 1)
            for n in range(0, SLOTS, 1024):
                sp.dma_start(xbuf[n:n + 1024, :].rearrange("(p a) d -> p (a d)", p=P), zero[:, :]).then_inc(zero_out, 16)
            for n in range(2):
                load_w(*SPLIT[n], w_in[n])
            sp.wait_ge(scattered, 16 * 2 * NT)
            for i in range(2):
                sp.dma_start(xe[i][:, :], xbuf[i * CAP:(i + 1) * CAP, :]).then_inc(x_in[i], 16)
            with sp.Fori(0, E // 2 - 1) as u:
                for i in range(2):
                    e = 2 * u + i
                    sp.wait_ge(xT_psum, e + 1)
                    sp.dma_start(xe[i][:, :], xbuf[bass.ds((e + 2) * CAP, CAP), :]).then_inc(x_in[i], 16)

        @block.gpsimd
        def _(pool):
            pool.memset(zero[:, :], 0.0).then_inc(zeroed, 1)
            pool.wait_ge(zero_out, 16 * (SLOTS // 1024))
            pool.wait_ge(steps, 29)
            for t in range(NT):
                for k in range(2):
                    pool.indirect_dma_start(
                        out=xbuf, out_offset=bass.IndirectOffsetOnAxis(ap=su[:, k * NT + t:k * NT + t + 1], axis=0),
                        in_=g.xn[:, t, :], in_offset=None).then_inc(scattered, 16)
            for i in range(2):
                pool.wait_ge(y_stored[i], 16 * (E // 2))
            for t in range(NT):
                for k in range(2):
                    n = k * NT + t
                    pool.indirect_dma_start(
                        out=yg[:, n, :], out_offset=None, in_=ybuf,
                        in_offset=bass.IndirectOffsetOnAxis(ap=gu[:, n:n + 1], axis=0)).then_inc(gathered[t // 4], 16)
            for i in range(2):
                pool.wait_ge(gathered[i], 16 * NT)

        @block.tensor
        def _(pe):
            pe.wait_ge(c_in, 16 * 5)
            for t in range(NT):
                for k in range(2):
                    mm = pe.matmul(ps[0][0:TT, t * E:(t + 1) * E], g.xnT[:, k, t * TT:(t + 1) * TT], gw[:, k, :],
                                   start=(k == 0), stop=(k == 1), skip_group_check=True)
            mm.then_inc(lg_psum, 1)
            pe.wait_ge(shared_in, 48)
            def shared_part(part):
                m = FB if part else P
                for gu_ in range(2):
                    for half in range(2):
                        for k in range(2):
                            mm = pe.matmul(ps[1 + 2 * gu_ + half][0:m, 0:HALF],
                                           w13[:, E, k, gu_, part * P:part * P + m],
                                           g.xnT[:, k, half * HALF:(half + 1) * HALF], start=(k == 0), stop=(k == 1))
                mm.then_inc(sh_psum, 1)
            shared_part(0)
            pe.wait_ge(steps, 19)
            flat = A[:, :, :].rearrange("p t e -> p (t e)")
            pe.matmul(ps[0][0:TT, 0:E], low[:, :], flat[:, 0:E], start=True, stop=True, skip_group_check=True)
            pe.matmul(ps[0][0:TT, E:NT * E], low[:, :], flat[:, E:NT * E], start=True, stop=False,
                      skip_group_check=True)
            for t in reversed(range(NT - 1)):
                mm = pe.matmul(ps[0][0:TT, (t + 1) * E:NT * E].rearrange("p (t e) -> p t e", e=E), g.ones[0:TT, 0:TT],
                               A[:, t:t + 1, :].broadcast_to([TT, NT - 1 - t, E]), start=False, stop=(t == 0),
                               skip_group_check=True)
            mm.then_inc(count_psum, 1)
            pe.wait_ge(sh_steps, 4)
            shared_part(1)
            pe.wait_ge(sh_steps, 8)
            for t in range(NT):
                if t >= 2:
                    pe.wait_ge(sh_added, t - 1)
                pe.matmul(ps[5 + t % 2][0:TT, 0:D], hs[:, 0, t * TT:(t + 1) * TT], w2a[:, E, :], start=True, stop=False)
                pe.matmul(ps[5 + t % 2][0:TT, 0:D], hs[0:FB, 1, t * TT:(t + 1) * TT], w2b[:, E, :],
                          start=False, stop=True).then_inc(sh_out, 1)
            pe.wait_ge(sh_added, NT)

            at = lambda t, e: t[:, e:e + 1] if isinstance(e, int) else t[:, bass.ds(e, 1)]

            def step(n, pair, i):
                if at_stage(n, 0):
                    pe.wait_ge(x_in[i], 16 * pair + 16)
                    if from_(n, 2):
                        pe.wait_ge(xT_ready, n - 1)
                    for d in range(2):
                        mm = pe.transpose(bT[i][:, d * P:(d + 1) * P], xe[i][:, d * P:(d + 1) * P], g.ident[:, :])
                    mm.then_inc(xT_psum, 1)
                if at_stage(n, 1):
                    e = n - 1
                    pe.wait_ge(xT_ready, e + 1)
                    if from_(n, 3):
                        pe.wait_ge(h_ready, e - 1)
                    for d in range(2):
                        mm = pe.matmul(bGU[1 - i][:, 0:2 * FF], xeT[1 - i][:, d * P:(d + 1) * P],
                                       at(w13, e)[:, 0, d].rearrange("p g f -> p (g f)"),
                                       start=(d == 0), stop=(d == 1))
                    mm.then_inc(gu_psum, 1)
                if at_stage(n, 2):
                    e = n - 2
                    pe.wait_ge(h_ready, e + 1)
                    if from_(n, 4):
                        pe.wait_ge(hT_ready, 2 * (e - 1))
                    pe.transpose(bH[i][:, 0:P], he[i][:, 0:P], g.ident[:, :])
                    pe.transpose(bH[i][0:FB, P:2 * P], he[i][:, P:FF], g.ident[:, :]).then_inc(hT_psum, 1)
                if at_stage(n, 3):
                    e = n - 3
                    pe.wait_ge(hT_ready, 2 * (e + 1))
                    if from_(n, 5):
                        pe.wait_ge(y_ready, e - 1)
                    pe.matmul(bY[1 - i][:, 0:D], heT[1 - i][:, 0, :], at(w2a, e)[:, 0], start=True, stop=False)
                    pe.matmul(bY[1 - i][:, 0:D], heT[1 - i][0:FB, 1, :], at(w2b, e)[:, 0], start=False, stop=True)\
                      .then_inc(y_psum, 1)
            for n in range(2):
                pe.wait_ge(w_in[n], 48)
            s = stages(step)
            next(s)
            with pe.Fori(0, E // 2 - 2) as u:
                for i in range(2):
                    step(2 * u + 4 + i, u + 2, i)
            for _ in s:
                pass

        @block.scalar
        def _(act):
            act.wait_ge(steps, 2)
            act.activation(ex[:, :, :], ab[:, :, :], ACT.Exp, scale=-1.0).then_inc(act_steps, 1)
            for part in range(2):
                m = FB if part else P
                if part:
                    act.wait_ge(steps, 3)
                    act.activation(ln[:, :, :], up[:, :, :], ACT.Ln).then_inc(act_steps, 1)
                    act.wait_ge(steps, 8)
                    act.activation(sc[:, :, :], sc[:, :, :], ACT.Sqrt).then_inc(act_steps, 1)
                for half in range(2):
                    act.wait_ge(sh_psum, part + 1)
                    if part:
                        act.wait_ge(sh_steps, 2 * half + 2)
                    act.activation(ts[0:m, half * HALF:(half + 1) * HALF], ps[1 + half][0:m, 0:HALF], ACT.Tanh, scale=0.5)\
                       .then_inc(sh_tanh, 1)

            def step(n, pair, i):
                if at_stage(n, 1):
                    e = n - 1
                    act.wait_ge(gu_psum, e + 1)
                    if from_(n, 3):
                        act.wait_ge(gated, e - 1)
                    act.activation(th[1 - i][:, :], bGU[1 - i][:, 0:FF], ACT.Tanh, scale=0.5).then_inc(e_tanh, 1)
                if at_stage(n, 2):
                    e = n - 2
                    act.wait_ge(hT_psum, e + 1)
                    if from_(n, 4):
                        act.wait_ge(y_psum, e - 1)
                    act.activation(heT[i][:, 0, :], bH[i][:, 0:P], ACT.Copy).then_inc(hT_ready, 1)
                    act.activation(heT[i][0:FB, 1, :], bH[i][0:FB, P:2 * P], ACT.Copy).then_inc(hT_ready, 1)
                if at_stage(n, 3):
                    e = n - 3
                    act.wait_ge(y_psum, e + 1)
                    if from_(n, 5):
                        act.wait_ge(y_stored[1 - i], 16 * (pair - 2 + i))
                    act.activation(ye[1 - i][:, :], bY[1 - i][:, 0:D], ACT.Copy, scale=0.5).then_inc(y_ready, 1)
                    act.wait_ge(y_ready, e + 1)
                    act.dma_start(ybuf[e * CAP:(e + 1) * CAP, :] if isinstance(e, int) else ybuf[bass.ds(e * CAP, CAP), :],
                                  ye[1 - i][:, :]).then_inc(y_stored[1 - i], 16)
            s = stages(step)
            next(s)
            with act.Fori(0, E // 2 - 2) as u:
                for i in range(2):
                    step(2 * u + 4 + i, u + 2, i)
            for _ in s:
                pass

        @block.vector
        def _(dve):
            at = [0]

            def step(ins):
                at[0] += 1
                ins.then_inc(steps, 1)
                dve.wait_ge(steps, at[0])

            def bt(col):
                return col.unsqueeze(2).broadcast_to([TT, NT, E])

            def be(row):
                return row.unsqueeze(1).broadcast_to([TT, NT, E])
            a3 = lambda t: t[:, :, :]
            dve.wait_ge(lg_psum, 1)
            dve.wait_ge(c_in, 16 * 5)
            step(dve.tensor_copy(lg[:, :, :], ps[0][0:TT, 0:NT * E].rearrange("p (t e) -> p t e", e=E)))
            step(dve.scalar_tensor_tensor(out=a3(ab), in0=a3(lg), scalar=-1.0, in1=a3(lg), op0=ALU.mult,
                                          op1=ALU.max))
            dve.wait_ge(act_steps, 1)
            step(dve.tensor_scalar(a3(up), a3(ex), 1.0, None, ALU.add))
            step(dve.tensor_scalar(a3(dd), a3(up), 1.0, 1e-30, ALU.subtract, ALU.max))
            dve.reciprocal(a3(sk), a3(dd)).then_inc(side, 1)
            dve.tensor_scalar(a3(tmp), a3(up), 1.0, None, ALU.is_equal).then_inc(side, 1)
            dve.wait_ge(act_steps, 2)
            dve.wait_ge(side, 2)
            step(dve.tensor_tensor(a3(sk), a3(sk), a3(ln), ALU.mult))
            step(dve.tensor_tensor(a3(sk), a3(sk), a3(tmp), ALU.add))
            step(dve.tensor_tensor(a3(sk), a3(sk), a3(ex), ALU.mult))
            step(dve.scalar_tensor_tensor(out=a3(sc), in0=a3(lg), scalar=0.0, in1=a3(sk), op0=ALU.max,
                                          op1=ALU.add))
            dve.wait_ge(act_steps, 3)
            step(dve.tensor_tensor(a3(sk), a3(sc), be(gb[:, :]), ALU.add))
            for k in range(2):
                step(dve.tensor_reduce(mcol[:, :], a3(sk), X, ALU.max))
                step(dve.tensor_tensor(a3(tmp), a3(sk), bt(mcol[:, :]), ALU.is_equal))
                step(dve.tensor_tensor(a3(tmp), a3(tmp), be(eid[:, :]), ALU.mult))
                step(dve.tensor_reduce(ei[:, k, :], a3(tmp), X, ALU.min))
                if k == 0:
                    step(dve.tensor_tensor(a3(oh[0]), be(eid[:, :]), bt(ei[:, 0, :]), ALU.is_equal))
                    dve.scalar_tensor_tensor(out=a3(sk), in0=a3(oh[0]), scalar=-3e38, in1=a3(sk), op0=ALU.mult,
                                             op1=ALU.add).then_inc(side, 1)
                    dve.wait_ge(side, 3)
                else:
                    dve.tensor_tensor(a3(oh[1]), be(eid[:, :]), bt(ei[:, 1, :]), ALU.is_equal).then_inc(side, 1)
                    dve.wait_ge(side, 4)
                    step(dve.tensor_tensor(a3(A), a3(oh[0]), a3(oh[1]), ALU.add))
            for k in range(2):
                dve.tensor_tensor(a3(tmp if k else up), a3(oh[k]), a3(sc), ALU.mult).then_inc(side, 1)
                dve.wait_ge(side, 5 + 2 * k)
                dve.tensor_reduce(w[:, k, :], a3(tmp if k else up), X, ALU.add).then_inc(side, 1)
            dve.wait_ge(side, 8)
            step(dve.tensor_tensor(den[:, :], w[:, 0, :], w[:, 1, :], ALU.add))
            step(dve.reciprocal(den[:, :], den[:, :]))
            dve.wait_ge(count_psum, 1)
            step(dve.tensor_copy(a3(pos), ps[0][0:TT, 0:NT * E].rearrange("p (t e) -> p t e", e=E)))
            for k in range(2):
                dve.tensor_tensor(a3(tmp if k else up), a3(oh[k]), a3(pos), ALU.mult).then_inc(side, 1)
                dve.wait_ge(side, 9 + 2 * k)
                dve.tensor_reduce(ps_[:, k, :], a3(tmp if k else up), X, ALU.add).then_inc(side, 1)
            dve.wait_ge(side, 12)
            step(dve.tensor_scalar(a3(valid), a3(ps_), float(CAP), None, ALU.is_lt))
            step(dve.tensor_scalar(a3(base), a3(ei), NOE, float(CAP), ALU.add, ALU.mult))
            step(dve.tensor_tensor(a3(gidx), a3(ps_), a3(valid), ALU.mult))
            step(dve.tensor_tensor(a3(sidx), a3(base), a3(ps_), ALU.add))
            dve.tensor_tensor(a3(gidx), a3(gidx), a3(base), ALU.add).then_inc(side, 1)
            dve.tensor_tensor(a3(sidx), a3(sidx), a3(trash), ALU.subtract).then_inc(side, 1)
            dve.wait_ge(side, 14)
            step(dve.tensor_tensor(a3(sidx), a3(sidx), a3(valid), ALU.mult))
            step(dve.tensor_tensor(a3(sidx), a3(sidx), a3(trash), ALU.add))
            dve.tensor_copy(gu[:, :], gidx[:, :, :].rearrange("p k t -> p (k t)")).then_inc(side, 1)
            step(dve.tensor_copy(su[:, :], sidx[:, :, :].rearrange("p k t -> p (k t)")))
            dve.tensor_tensor(a3(w), a3(w), a3(valid), ALU.mult).then_inc(side, 1)
            dve.wait_ge(side, 16)
            dve.tensor_tensor(a3(w), a3(w), den[:, :].unsqueeze(1).broadcast_to([TT, 2, NT]), ALU.mult).then_inc(side, 1)

            for part in range(2):
                m = FB if part else P
                for half in range(2):
                    t_ = ts[0:m, half * HALF:(half + 1) * HALF]
                    h_ = hs[0:m, part, half * HALF:(half + 1) * HALF]
                    dve.wait_ge(sh_tanh, 2 * part + half + 1)
                    dve.scalar_tensor_tensor(out=h_, in0=t_, scalar=1.0, in1=ps[1 + half][0:m, 0:HALF],
                                             op0=ALU.add, op1=ALU.mult).then_inc(sh_steps, 1)
                    dve.wait_ge(sh_steps, 4 * part + 2 * half + 1)
                    dve.tensor_tensor(h_, h_, ps[3 + half][0:m, 0:HALF], ALU.mult).then_inc(sh_steps, 1)
            for t in range(NT):
                dve.wait_ge(sh_out, t + 1)
                dve.scalar_tensor_tensor(out=g.x[:, t, :], in0=ps[5 + t % 2][0:TT, 0:D], scalar=0.5, in1=g.x[:, t, :],
                                         op0=ALU.mult, op1=ALU.add).then_inc(sh_added, 1)

            def step(n, pair, i):
                if at_stage(n, 0):
                    dve.wait_ge(xT_psum, n + 1)
                    if from_(n, 2):
                        dve.wait_ge(gu_psum, n - 1)
                    dve.tensor_copy(xeT[i][:, :], bT[i][:, 0:2 * P]).then_inc(xT_ready, 1)
                if at_stage(n, 1):
                    e = n - 1
                    dve.wait_ge(e_tanh, e + 1)
                    if from_(n, 3):
                        dve.wait_ge(hT_psum, e - 1)
                    dve.scalar_tensor_tensor(out=he[1 - i][:, :], in0=th[1 - i][:, :], scalar=1.0,
                                             in1=bGU[1 - i][:, 0:FF], op0=ALU.add, op1=ALU.mult).then_inc(gated, 1)
                    dve.wait_ge(gated, e + 1)
                    dve.tensor_tensor(he[1 - i][:, :], he[1 - i][:, :], bGU[1 - i][:, FF:2 * FF], ALU.mult)\
                       .then_inc(h_ready, 1)
            s = stages(step)
            next(s)
            with dve.Fori(0, E // 2 - 2) as u:
                for i in range(2):
                    step(2 * u + 4 + i, u + 2, i)
            for _ in s:
                pass
            for t in range(NT):
                for k in range(2):
                    n = k * NT + t
                    dve.wait_ge(gathered[t // 4], 16 * NT)
                    if t or k:
                        dve.wait_ge(summed, 2 * t + k)
                    dve.scalar_tensor_tensor(out=g.x[:, t, :], in0=yg[:, n, :], scalar=w[:, k, t:t + 1],
                                             in1=g.x[:, t, :], op0=ALU.mult, op1=ALU.add).then_inc(summed, 1)


def ternary_weights(nc, g, ctx):
    sb = lambda n, s, d=F32: ctx.enter_context(nc.sbuf_tensor(f"b_{n}", s, d))
    g.wf = [sb("wg", [P, 2, FI]), sb("wu", [P, 2, FI]), sb("wd", [P, FT, D])]
    g.wq = [sb("wgq", [P, 2, FI], BF16), sb("wuq", [P, 2, FI], BF16), sb("wdq", [P, FT, D], BF16)]
    g.wabs, g.wm, g.wsc = sb("wabs", [P, 3]), sb("wm", [P, 3]), sb("wsc", [P, 3])
    g.wb_in, g.wd_zero, g.wabs_sums = g.sem("b_w_in"), g.sem("b_wd_zero"), g.sem("b_wabs_sums")
    g.wsum_psum, g.w_steps = g.sem("b_wsum_psum"), g.sem("b_w_steps")


def load_ternary(sp, g):
    sp.dma_start(g.wf[0][:, :, :], g.a["WgT"]).then_inc(g.wb_in, 16)
    sp.dma_start(g.wf[1][:, :, :], g.a["WuT"]).then_inc(g.wb_in, 16)
    sp.wait_ge(g.wd_zero, 1)
    sp.dma_start(g.wf[2][:, 0:FT - 1, :], g.a["WdT"][0:(FT - 1) * P, :].rearrange("(f p) d -> p f d", p=P))\
      .then_inc(g.wb_in, 16)
    sp.dma_start(g.wf[2][0:LASTF, FT - 1, :], g.a["WdT"][(FT - 1) * P:FI, :]).then_inc(g.wb_in, 16)


def sum_ternary(dve, g):
    dve.wait_ge(g.wb_in, 64)
    for m in range(3):
        dve.tensor_reduce(g.wabs[:, m:m + 1], g.wf[m][:, :, :], mybir.AxisListType.XY, ALU.add,
                          apply_absolute_value=True).then_inc(g.wabs_sums, 1)


def round_ternary(dve, g, total):
    dve.wait_ge(g.wsum_psum, 1)
    dve.tensor_scalar(g.wm[:, :], total, 1.0 / (FI * D), 1e-5, ALU.mult, ALU.max).then_inc(g.w_steps, 1)
    dve.wait_ge(g.w_steps, 1)
    dve.reciprocal(g.wsc[:, :], g.wm[:, :]).then_inc(g.w_steps, 1)
    dve.wait_ge(g.w_steps, 2)
    for m in range(3):
        w = g.wf[m][:, :, :]
        dve.tensor_scalar(w, w, g.wsc[:, m:m + 1], 1.0, ALU.mult, ALU.min).then_inc(g.w_steps, 1)
        dve.wait_ge(g.w_steps, 3 * m + 3)
        dve.tensor_scalar(w, w, -1.0, MAGIC, ALU.max, ALU.add).then_inc(g.w_steps, 1)
        dve.wait_ge(g.w_steps, 3 * m + 4)
        dve.tensor_scalar(g.wq[m][:, :, :], w, MAGIC, None, ALU.subtract).then_inc(g.w_steps, 1)


def phase_bitlinear(nc, g):
    with ExitStack() as ctx:
        sb = lambda n, s, d=F32: ctx.enter_context(nc.sbuf_tensor(f"b_{n}", s, d))
        N = lambda n: g.sem(f"b_{n}")
        wq, wm, w_steps = g.wq, g.wm, g.w_steps
        ma, sx, sg, cc = sb("ma", [TT, NT]), sb("sx", [TT, NT]), sb("sg", [TT, NT]), sb("cc", [TT, NT])
        xq = sb("xq", [TT, NT, D])
        xqT = sb("xqT", [P, 2, T], BF16)
        th = sb("th", [TT, FI])
        hh, hm = [sb(f"hh{i}", [TT, FI]) for i in range(2)], [sb(f"hm{i}", [TT, 4]) for i in range(2)]
        hT = sb("hT", [P, FT, TT], BF16)
        pgu = [ctx.enter_context(nc.psum_tensor(f"b_pgu{i}", [P, 1024], F32)) for i in range(2)]
        pt = ctx.enter_context(nc.psum_tensor("b_pt", [P, 1024], F32))
        pd = ctx.enter_context(nc.psum_tensor("b_pd", [P, 512], F32))
        pw = ctx.enter_context(nc.psum_tensor("b_pw", [P, 512], F32))
        rounded = N("rounded")
        x_steps, xT_psum, xT_ready = N("x_steps"), N("xT_psum"), N("xT_ready")
        gu_psum, tanh_ready, h_steps, hT_psum, hT_ready, d_psum, added, stored = [
            N(n) for n in ("gu_psum", "tanh_ready", "h_steps", "hT_psum", "hT_ready", "d_psum", "added", "stored")]
        block = ctx.enter_context(nc.Block())
        h_sc = N("h_scaled")
        HS = 7
        FC = [(0, 512), (512, FI)]

        @block.sync
        def _(sp):
            o = g.out.rearrange("b q d -> (b q) d").rearrange("(t p) d -> p t d", p=TT)
            for half in range(2):
                sp.wait_ge(added, 4 * half + 4)
                sp.dma_start(o[:, 4 * half:4 * half + 4, :], g.x[:, 4 * half:4 * half + 4, :]).then_inc(stored, 16)
            sp.wait_ge(stored, 32)

        @block.tensor
        def _(pe):
            pe.wait_ge(x_steps, 13)
            for n in range(4):
                k, half = n // 2, n % 2
                bank = [pt[:, 0:512], pt[:, 512:1024], pd[:, :], pw[:, :]][n]
                for t in range(4):
                    mm = pe.transpose(bank[:, t * TT:(t + 1) * TT], xq[:, 4 * half + t, k * P:(k + 1) * P],
                                      g.ident[0:TT, 0:TT])
                mm.then_inc(xT_psum, 1)

            def gate_up(t):
                for m in range(2):
                    for lo, hi in FC:
                        for k in range(2):
                            mm = pe.matmul(pgu[m][0:TT, lo:hi], xqT[:, k, bass.ds(t * TT, TT)], wq[m][:, k, lo:hi],
                                           start=(k == 0), stop=(k == 1))
                mm.then_inc(gu_psum, 1)

            def tile(t, i, last):
                if not last:
                    pe.wait_ge(h_steps, HS * t + 2)
                    gate_up(t + 1)
                pe.wait_ge(h_steps, HS * t + HS)
                pe.wait_ge(hT_ready, 3 * t)
                for f in range(FT):
                    n = P if f < FT - 1 else LASTF
                    lo = f * TT if f < 4 else 512 + (f - 4) * TT
                    mm = pe.transpose(pt[0:n, lo:lo + TT], hh[i][:, f * P:f * P + n], g.ident[0:TT, 0:TT])
                mm.then_inc(hT_psum, 1)
                pe.wait_ge(hT_ready, 3 * t + 3)
                pe.wait_ge(added, t)
                for f in range(FT):
                    n = P if f < FT - 1 else LASTF
                    mm = pe.matmul(pd[0:TT, 0:D], hT[0:n, f, :], wq[2][0:n, f, :], start=(f == 0), stop=(f == FT - 1))
                mm.then_inc(d_psum, 1)
            pe.wait_ge(w_steps, 12)
            pe.wait_ge(xT_ready, 4)
            gate_up(0)
            with pe.Fori(0, NT // 2 - 1) as u:
                for i in range(2):
                    tile(2 * u + i, i, False)
            tile(NT - 2, 0, False)
            tile(NT - 1, 1, True)

        @block.scalar
        def _(act):
            def tanh(t, first):
                act.wait_ge(gu_psum, t + 1)
                if first:
                    act.wait_ge(x_steps, 15)
                else:
                    act.wait_ge(h_steps, HS * (t - 1) + 1)
                act.activation(th[:, :], pgu[0][0:TT, 0:FI], ACT.Tanh, scale=sg[:, bass.ds(t, 1)]).then_inc(tanh_ready, 1)

            def transposed(t):
                act.wait_ge(d_psum, t)
                act.wait_ge(hT_psum, t + 1)
                act.activation(hT[:, 0:4, :].rearrange("p f n -> p (f n)"), pt[:, 0:4 * TT], ACT.Copy).then_inc(hT_ready, 1)
                act.activation(hT[:, 4:6, :].rearrange("p f n -> p (f n)"), pt[:, 512:512 + 2 * TT], ACT.Copy)\
                   .then_inc(hT_ready, 1)
                act.activation(hT[0:LASTF, 6, :], pt[0:LASTF, 512 + 2 * TT:512 + 3 * TT], ACT.Copy).then_inc(hT_ready, 1)
            tanh(0, True)
            with act.Fori(0, NT - 1) as t:
                tanh(t + 1, False)
                transposed(t)
            transposed(NT - 1)

        @block.vector
        def _(dve):
            dve.tensor_reduce(ma[:, :], g.xn[:, :, :], X, ALU.max, apply_absolute_value=True).then_inc(x_steps, 1)
            dve.wait_ge(x_steps, 1)
            dve.tensor_scalar(ma[:, :], ma[:, :], 1e-5, None, ALU.max).then_inc(x_steps, 1)
            dve.wait_ge(x_steps, 2)
            dve.reciprocal(sx[:, :], ma[:, :]).then_inc(x_steps, 1)
            dve.wait_ge(x_steps, 3)
            dve.tensor_scalar(sx[:, :], sx[:, :], 127.0, None, ALU.mult).then_inc(x_steps, 1)
            dve.wait_ge(x_steps, 4)
            for t in range(NT):
                ins = dve.tensor_scalar(xq[:, t, :], g.xn[:, t, :], sx[:, t:t + 1], 127.0, ALU.mult, ALU.min)
                ins.then_inc(x_steps, 1)
            dve.wait_ge(x_steps, 12)
            dve.tensor_scalar(xq[:, :, :], xq[:, :, :], -128.0, MAGIC, ALU.max, ALU.add).then_inc(rounded, 1)
            dve.wait_ge(rounded, 1)
            dve.tensor_scalar(xq[:, :, :], xq[:, :, :], MAGIC, None, ALU.subtract).then_inc(x_steps, 1)

            for n in range(4):
                k, half = n // 2, n % 2
                bank = [pt[:, 0:512], pt[:, 512:1024], pd[:, :], pw[:, :]][n]
                dve.wait_ge(xT_psum, n + 1)
                dve.tensor_copy(xqT[:, k, half * HALF:(half + 1) * HALF], bank[:, 0:HALF]).then_inc(xT_ready, 1)
            dve.wait_ge(x_steps, 13)
            dve.tensor_scalar(sg[:, :], ma[:, :], wm[0:TT, 0:1], 0.5 / 127.0, ALU.mult, ALU.mult).then_inc(x_steps, 1)
            dve.wait_ge(w_steps, 11)
            dve.wait_ge(x_steps, 14)
            dve.tensor_tensor(cc[:, :], sg[:, :], ma[:, :], ALU.mult).then_inc(x_steps, 1)
            dve.wait_ge(x_steps, 15)
            dve.tensor_scalar(cc[:, :], cc[:, :], wm[0:TT, 1:2], 1.0 / 127.0, ALU.mult, ALU.mult).then_inc(w_steps, 1)
            dve.wait_ge(w_steps, 12)

            def quantised(t, i):
                h, m = hh[i], hm[i]
                c = cc[:, bass.ds(t, 1)]
                dve.wait_ge(tanh_ready, t + 1)
                if not isinstance(t, int) or t >= 2:
                    dve.wait_ge(hT_psum, t - 1)
                dve.scalar_tensor_tensor(out=h[:, :], in0=th[:, :], scalar=1.0, in1=pgu[0][0:TT, 0:FI],
                                         op0=ALU.add, op1=ALU.mult).then_inc(h_steps, 1)
                dve.wait_ge(h_steps, HS * t + 1)
                dve.tensor_tensor(h[:, :], h[:, :], pgu[1][0:TT, 0:FI], ALU.mult).then_inc(h_steps, 1)
                dve.wait_ge(h_steps, HS * t + 2)
                dve.tensor_reduce(m[:, 0:1], h[:, :], X, ALU.max, apply_absolute_value=True).then_inc(h_steps, 1)
                dve.wait_ge(h_steps, HS * t + 3)
                dve.tensor_scalar(m[:, 1:2], m[:, 0:1], c, 1e-5, ALU.mult, ALU.max).then_inc(h_steps, 1)
                dve.wait_ge(h_steps, HS * t + 4)
                dve.reciprocal(m[:, 2:3], m[:, 1:2]).then_inc(h_steps, 1)
                dve.wait_ge(h_steps, HS * t + 5)
                dve.tensor_scalar(m[:, 3:4], m[:, 2:3], c, 127.0, ALU.mult, ALU.mult).then_inc(h_sc, 1)
                dve.wait_ge(h_sc, 3 * t + 1)
                dve.tensor_scalar(h[:, :], h[:, :], m[:, 3:4], 127.0, ALU.mult, ALU.min).then_inc(h_sc, 1)
                dve.wait_ge(h_sc, 3 * t + 2)
                dve.tensor_scalar(h[:, :], h[:, :], -128.0, MAGIC, ALU.max, ALU.add).then_inc(h_sc, 1)
                dve.wait_ge(h_sc, 3 * t + 3)
                dve.tensor_scalar(h[:, :], h[:, :], MAGIC, None, ALU.subtract).then_inc(h_steps, 1)
                dve.tensor_scalar(m[:, 2:3], m[:, 1:2], wm[0:TT, 2:3], 1.0 / 127.0, ALU.mult, ALU.mult)\
                   .then_inc(h_steps, 1)

            def add(t, i):
                dve.wait_ge(d_psum, t + 1)
                dve.wait_ge(h_steps, HS * t + HS)
                xs = g.x[:, t, :] if isinstance(t, int) else g.x[:, bass.ds(t, 1), :][:, 0]
                dve.scalar_tensor_tensor(out=xs, in0=pd[0:TT, 0:D], scalar=hm[i][:, 2:3], in1=xs,
                                         op0=ALU.mult, op1=ALU.add).then_inc(added, 1)
            quantised(0, 0)
            with dve.Fori(0, NT // 2 - 1) as u:
                for i in range(2):
                    quantised(2 * u + 1 + i, 1 - i)
                    add(2 * u + i, i)
            quantised(NT - 1, 1)
            add(NT - 2, 0)
            add(NT - 1, 1)


def phase_setup(nc, g):
    loaded = g.sem("loaded")
    with nc.Block() as block:
        @block.sync
        def _(sp):
            items = [(g.x, g.a["x"]), (g.ident, g.a["ident"]), (g.ones, g.a["ones"]),
                     (g.cen, g.a["cen"]), (g.blk, g.a["blk"]), (g.hmask, g.a["hmask"]), (g.bk0row, g.a["bk0"]), (g.bkdrow, g.a["bkd"])]
            for dst, src in items:
                sp.dma_start(dst[tuple(slice(None) for _ in dst.shape)], src).then_inc(loaded, 16)
            sp.wait_ge(loaded, 16 * len(items))


def build(nc, a, out):
    with ExitStack() as ctx:
        sb = lambda n, s, d=F32: ctx.enter_context(nc.sbuf_tensor(n, s, d))
        g = Shared()
        g.a, g.out = a, out
        g.sem = nc.alloc_semaphore
        g.x = sb("x", [TT, NT, D])
        g.rk_all = sb("rk", [P, B + 1, NK, 2 * H])
        g.rk = g.rk_all[:, 1:, :, :]
        g.ident, g.ones = sb("ident", [P, P]), sb("ones", [P, P])
        g.cen, g.blk, g.hmask = sb("cen", [P, P]), sb("blk", [P, P]), sb("hmask", [P, 8])
        g.bk0row, g.bkdrow = sb("bk0row", [1, D]), sb("bkdrow", [1, D])
        g.qdram = [nc.dram_tensor(f"qdram{l}", [B, P, HQ], F32).ap() for l in range(2)]
        g.odram = [nc.dram_tensor(f"odram{l}", [B, P, HQ], F32).ap() for l in range(2)]
        g.bdram = nc.dram_tensor("bdram", [B, 3, HQ], BF16).ap()
        g.xbuf = nc.dram_tensor("xbuf", [E * CAP + 2 * T, D], F32).ap()
        g.ybuf = nc.dram_tensor("ybuf", [E * CAP, D], F32).ap()
        g.ddram = nc.dram_tensor("ddram", [P, 2, T], F32).ap()

        def with_normed(name, *phases):
            with nc.sbuf_tensor(f"{name}_xn", [TT, NT, D], F32) as g.xn, \
                    nc.sbuf_tensor(f"{name}_xnT", [P, 2, T], F32) as g.xnT:
                phase_layernorm(nc, g, name)
                for phase in phases:
                    phase()
        with nc.cleanup_on_exit(), ExitStack() as context:
            phase_setup(nc, g)
            phase_norms(nc, g)
            first_context(nc, g, context, 0)
            with nc.sbuf_tensor("qs0", [P, T], F32) as qs0, nc.sbuf_tensor("qs1", [P, T], F32) as qs1, \
                    nc.sbuf_tensor("cols", [P, 2, 5], F32) as g.cols:
                g.qs = [qs0, qs1]
                with_normed("l0", lambda: phase_queries0(nc, g))
                phase_dca(nc, g)
            phase_attention(nc, g, 0)
            context.close()
            phase_project0(nc, g)
            with_normed("l1", lambda: phase_moe(nc, g))
        with nc.cleanup_on_exit():
            with ExitStack() as context:
                first_context(nc, g, context, 1)
                with_normed("l2", lambda: phase_queries1(nc, g))
                phase_attention(nc, g, 1)
            with ExitStack() as weights:
                ternary_weights(nc, g, weights)
                phase_project1(nc, g)
                with_normed("l3", lambda: phase_bitlinear(nc, g))


def laid_out(i):
    rows = lambda w: w.reshape(2, P, -1).transpose(1, 0, 2)
    wkv = np.concatenate([i["L0_xattn_Wk"], i["L0_xattn_Wv"]], 1).reshape(C, H, 2, HD0)
    bkv = np.concatenate([i["L0_xattn_bk"], i["L0_xattn_bv"]]).reshape(H, 2, HD0)
    wk0, wv0 = wkv[:, :, 0].reshape(C, D), wkv[:, :, 1].reshape(C, D)
    bk0, bv0 = bkv[:, 0].reshape(D), bkv[:, 1].reshape(D)
    wkd, wvd = i["L0_xattn_Wkv_dca"][:, :D], i["L0_xattn_Wkv_dca"][:, D:]
    bkd, bvd = i["L0_xattn_bkv_dca"][:D], i["L0_xattn_bkv_dca"][D:]
    k0T = np.concatenate([wk0, bk0[None]], 0).T.reshape(2, P, C + 1)
    rep = lambda w: np.tile(w, 8)
    bq = i["L0_xattn_bq"].reshape(2, P)
    cols = np.stack([np.stack([bq[s], rep(i["L0_xattn_qn_w"]), rep(i["L0_xattn_qn_b"]),
                               rep(i["L0_xattn_kn_w"]), rep(i["L0_xattn_kn_dca_w"])], 1) for s in range(2)])
    head = np.arange(P) // HD0
    same = (head[:, None] == head[None, :]).astype(np.float32)
    a = {
        "x": i["x"].reshape(NT, TT, D).transpose(1, 0, 2),
        "ctx": i["ctx_1024"], "ctxT": i["ctx_1024"].transpose(0, 2, 1),
        "ident": np.eye(P, dtype=np.float32), "ones": np.ones((P, P), np.float32),
        "cen": np.eye(P, dtype=np.float32) - same / np.float32(HD0), "blk": same,
        "hmask": (head[:, None] == np.arange(8)[None, :]).astype(np.float32),
        "low": np.triu(np.ones((TT, TT), np.float32), 1),
        "L0_Wk": wk0, "L0_Wkd": wkd, "L0_Wvd": wvd, "ydT": i["ctx_1024"][:, SEQ - DCA:].transpose(2, 0, 1).reshape(C, B * DCA), "bk0": bk0[None], "bkd": bkd[None],
        "k0T": k0T.transpose(1, 0, 2), "cols0": cols.transpose(1, 0, 2),
        "L0_Wq": rows(i["L0_xattn_Wq"]),
        "L0_Wv": wv0,
        "bv0": np.stack([bv0.reshape(2, P).T, bvd.reshape(2, P).T], 1), "L0_Wo": rows(i["L0_xattn_Wo"]),
        "bo0": np.broadcast_to(i["L0_xattn_bo"], (TT, D)),
        "L1_Wk": i["L1_xattn_Wk"],
        "L1_Wq": i["L1_xattn_Wq"].reshape(2, P, H, P).transpose(2, 1, 0, 3),
        "L1_WkT": i["L1_xattn_Wk"].T.reshape(H, P, C),
        "gq": i["L1_xattn_gq"][:, None], "gk": i["L1_xattn_gk"][:, None],
        "L1_WvT": i["L1_xattn_Wv"].T.reshape(H, P, C), "L1_Wo": i["L1_xattn_Wo"].reshape(H, P, D),
    }
    kxn = lambda w: w.transpose(0, 2, 1).reshape(E + 1, 2, P, FF).transpose(2, 0, 1, 3)
    a["W13"] = np.stack([kxn(np.concatenate([i[f"L0_ffn_W{n}"], i[f"L0_ffn_Ws{n}"][None]])) for n in (1, 3)], 3)
    w2 = np.concatenate([i["L0_ffn_W2"], i["L0_ffn_Ws2"][None]]).transpose(2, 0, 1)
    a["W2a"], a["W2b"] = w2[:P], w2[P:]
    a["gw"] = rows(i["L0_ffn_gate_w"].T)
    a["gb"] = np.broadcast_to(i["L0_ffn_gate_b"], (TT, E))
    a["eid"] = np.broadcast_to(np.arange(E, dtype=np.float32) - 99, (TT, E))
    token = np.arange(NT)[None, None, :] * TT + np.arange(TT)[:, None, None]
    a["WgT"], a["WuT"] = rows(i["L1_ffn_w_gate"].T), rows(i["L1_ffn_w_up"].T)
    a["WdT"] = i["L1_ffn_w_down"].T
    a["trash"] = (E * CAP + 2 * token + np.arange(2)[None, :, None]).astype(np.float32)
    return a


_OUTS = [((B, NQ, D), "float32")]


def kernel(**inputs):
    import numpy as _np
    import concourse.bacc as _bacc
    from concourse import mybir as _mybir
    from concourse.bass_utils import run_bass_kernel_spmd as _run

    nc = _bacc.Bacc("TRN2", target_bir_lowering=False, num_devices=1)
    arrays, aps = {}, {}
    for name, arr in laid_out({k: _np.asarray(v) for k, v in inputs.items()}).items():
        arr = _np.ascontiguousarray(arr)
        arrays[f"in_{name}"] = arr
        aps[name] = nc.dram_tensor(f"in_{name}", arr.shape, _mybir.dt.from_np(arr.dtype), kind="ExternalInput").ap()
    out = nc.dram_tensor("out_0", _OUTS[0][0], F32, kind="ExternalOutput").ap()
    build(nc, aps, out)
    return _run(nc, [arrays], core_ids=[0]).results[0]["out_0"]
```
